# Optimizing a Trainium2 kernel written in Bass

```python
import numpy as np
import jax
import jax.numpy as jnp

def _softmax(x, axis=-1):
    return jax.nn.softmax(x, axis=axis)

def _gelu(x):
    return jax.nn.gelu(x, approximate=True)

def _silu(x):
    return jax.nn.silu(x)

def _sigmoid(x):
    return jax.nn.sigmoid(x)

def _layernorm(x, axis=-1, eps=1e-05):
    m = jnp.mean(x, axis=axis, keepdims=True)
    v = jnp.var(x, axis=axis, keepdims=True)
    return (x - m) / jnp.sqrt(v + eps)

def _scatter_add(tgt, idx, src, axis=0):
    return tgt.at[idx].add(src)

def _segment_sum(src, seg, n):
    return jax.ops.segment_sum(src, seg, n)
kernel_name = 'mk_early_fusion_d2_tok_img768_r4_2fbfd4'

def setup_inputs(seed: int=0):
    np.random.seed(seed)
    _w = jnp.asarray

    def _rec_inputs():
        import jax
        import jax.numpy as jnp
        _rk = jax.random.key(seed)
        x = -0.000222058 + 0.999998 * jax.random.normal(jax.random.fold_in(_rk, 1), (16, 3, 96, 96), jnp.float32)
        txt = 0.000626447 + 0.554253 * jax.random.normal(jax.random.fold_in(_rk, 2), (16, 77, 192), jnp.float32)
        return (x, txt)
    x, txt = _rec_inputs()

    def _L0_tok_setup():
        import jax, jax.numpy as jnp
        import numpy as np
        from jax import lax
        HIDDEN = 192
        C_IN = 3
        PATCH = 16
        SIDE = 32
        NUM_PATCHES = SIDE * SIDE

        def _position_ids(nb_h, nb_w):
            boundaries = np.arange(1.0 / SIDE, 1.0, 1.0 / SIDE, dtype=np.float32)
            frac_h = np.arange(0.0, 1.0 - 1e-06, 1.0 / nb_h, dtype=np.float32)
            frac_w = np.arange(0.0, 1.0 - 1e-06, 1.0 / nb_w, dtype=np.float32)
            bh = np.searchsorted(boundaries, frac_h, side='right')
            bw = np.searchsorted(boundaries, frac_w, side='right')
            return jnp.asarray((bh[:, None] * SIDE + bw).reshape(-1), dtype=jnp.int32)
        key = jax.random.key(seed)
        k1, k2, k3 = jax.random.split(key, 3)
        pixel_values = jax.random.normal(k1, (32, C_IN, 128, 128), dtype=jnp.float32)
        conv_w = jax.random.normal(k2, (HIDDEN, C_IN, PATCH, PATCH), dtype=jnp.float32) * 0.02
        conv_b = jnp.zeros((HIDDEN,), dtype=jnp.float32)
        pos_table = jax.random.normal(k3, (NUM_PATCHES, HIDDEN), dtype=jnp.float32) * 0.02
        return {'pixel_values': pixel_values, 'conv_w': conv_w, 'conv_b': conv_b, 'pos_table': pos_table}
    _L0_tok_all = _L0_tok_setup()
    _L0_tok_in = {k: v for k, v in _L0_tok_all.items() if k in ('conv_w', 'conv_b', 'pos_table')}
    del _L0_tok_all

    def _L0_attn_setup():
        import jax, jax.numpy as jnp
        import numpy as np
        B, N, M, D = (128, 64, 8, 192)
        key = jax.random.key(seed)
        ks = jax.random.split(key, 6)
        w_scale = D ** (-0.5)
        return {'x': jax.random.normal(ks[0], (B, N, D), dtype=jnp.float32), 'memory': jax.random.normal(ks[1], (M, D), dtype=jnp.float32) * 0.02, 'Wq': jax.random.normal(ks[2], (D, D), dtype=jnp.float32) * w_scale, 'bq': jnp.zeros((D,), dtype=jnp.float32), 'Wk': jax.random.normal(ks[3], (D, D), dtype=jnp.float32) * w_scale, 'bk': jnp.zeros((D,), dtype=jnp.float32), 'Wv': jax.random.normal(ks[4], (D, D), dtype=jnp.float32) * w_scale, 'bv': jnp.zeros((D,), dtype=jnp.float32), 'Wo': jax.random.normal(ks[5], (D, D), dtype=jnp.float32) * w_scale, 'bo': jnp.zeros((D,), dtype=jnp.float32)}
    _L0_attn_all = _L0_attn_setup()
    _L0_attn_in = {k: v for k, v in _L0_attn_all.items() if k in ('memory', 'Wq', 'bq', 'Wk', 'bk', 'Wv', 'bv', 'Wo', 'bo')}
    del _L0_attn_all

    def _L0_ffn_setup():
        import jax, jax.numpy as jnp
        import numpy as np
        B, S, H = (2, 256, 192)
        E, K, I = (16, 4, 192)
        ALPHA, LIMIT, EPS = (1.702, 7.0, 1e-05)

        def _swiglu(h):
            x_glu, x_lin = jnp.split(h, 2, axis=-1)
            x_glu = jnp.minimum(x_glu, LIMIT)
            x_lin = jnp.clip(x_lin, -LIMIT, LIMIT)
            return x_glu * jax.nn.sigmoid(ALPHA * x_glu) * (x_lin + 1.0)
        key = jax.random.key(seed)
        ks = jax.random.split(key, 7)
        x = jax.random.normal(ks[0], (B, S, H), dtype=jnp.float32)
        scale = jnp.ones((H,), jnp.float32)
        gate_w = jax.random.normal(ks[1], (E, H), jnp.float32) * 0.02
        gate_b = jnp.zeros((E,), jnp.float32)
        w1 = jax.random.normal(ks[2], (E, H, 2 * I), jnp.float32) * 0.02
        b1 = jax.random.normal(ks[3], (E, 2 * I), jnp.float32) * 0.02
        w2 = jax.random.normal(ks[4], (E, I, H), jnp.float32) * 0.02
        b2 = jax.random.normal(ks[5], (E, H), jnp.float32) * 0.02
        return {'x': x, 'scale': scale, 'gate_w': gate_w, 'gate_b': gate_b, 'w1': w1, 'b1': b1, 'w2': w2, 'b2': b2}
    _L0_ffn_all = _L0_ffn_setup()
    _L0_ffn_in = {k: v for k, v in _L0_ffn_all.items() if k in ('scale', 'gate_w', 'gate_b', 'w1', 'b1', 'w2', 'b2')}
    del _L0_ffn_all

    def _L1_attn_setup():
        import jax, jax.numpy as jnp
        import numpy as np
        DIM = 192
        NUM_HEADS = 8
        GROUPS = 2
        key = jax.random.key(seed)
        ks = jax.random.split(key, 6)
        B, N, C = (8, 256, DIM)
        x = jax.random.normal(ks[0], (B, N, C), dtype=jnp.float32)
        w_qkv = jax.random.normal(ks[1], (3 * C, C), dtype=jnp.float32) * 0.02
        g_dim = C // GROUPS
        w_g0 = jax.random.normal(ks[2], (3 * g_dim, g_dim), dtype=jnp.float32) * 0.02
        w_g1 = jax.random.normal(ks[3], (3 * g_dim, g_dim), dtype=jnp.float32) * 0.02
        w_proj = jax.random.normal(ks[4], (C, C), dtype=jnp.float32) * 0.02
        b_proj = jax.random.normal(ks[5], (C,), dtype=jnp.float32) * 0.02
        return {'x': x, 'w_qkv': w_qkv, 'w_g0': w_g0, 'w_g1': w_g1, 'w_proj': w_proj, 'b_proj': b_proj}
    _L1_attn_all = _L1_attn_setup()
    _L1_attn_in = {k: v for k, v in _L1_attn_all.items() if k in ('w_qkv', 'w_g0', 'w_g1', 'w_proj', 'b_proj')}
    del _L1_attn_all

    def _L1_ffn_setup():
        import jax, jax.numpy as jnp
        import numpy as np
        DIM = 192
        HEADS = 12
        HD = DIM // HEADS
        MLP = 768
        RHD = 128
        RANK = 64
        BS = 2
        RESERVE = 1
        EPS = 1e-05

        def _ln(x, g, b):
            m = jnp.mean(x, axis=-1, keepdims=True)
            v = jnp.var(x, axis=-1, keepdims=True)
            return (x - m) / jnp.sqrt(v + EPS) * g + b

        def _gelu(t):
            return jax.nn.gelu(t, approximate=False)

        def _forward(x, wq, bq, wk, bk, wv, bv, wo, bo, ln1_g, ln1_b, ln2_g, ln2_b, fc1_w, fc1_b, fc2_w, fc2_b, r_ln_g, r_ln_b, r_in_w, r_in_b, r_o1_w, r_o1_b, r_o2_w, r_o2_b, r_o3_w, r_o3_b, lra_down, lra_up):
            B, N, _ = x.shape
            e = _gelu(_ln(x, r_ln_g, r_ln_b) @ r_in_w.T + r_in_b)
            g = jnp.mean(e[:, RESERVE:, :], axis=1, keepdims=True)
            f = jnp.concatenate([e, jnp.broadcast_to(g, e.shape)], axis=-1)
            h1 = _gelu(f @ r_o1_w.T + r_o1_b)
            h2 = _gelu(h1 @ r_o2_w.T + r_o2_b)
            logits = (h2 @ r_o3_w.T + r_o3_b).reshape(B, N, BS, 2)
            hard = jax.nn.one_hot(jnp.argmax(logits, axis=-1), 2, dtype=x.dtype)
            keep = jnp.broadcast_to(jnp.array([0.0, 1.0], dtype=x.dtype), hard[:, :RESERVE].shape)
            hard = hard.at[:, :RESERVE].set(keep)
            hard = jax.lax.stop_gradient(hard)
            bits = hard[..., 1]
            indices = (bits * jnp.array([2.0, 1.0], dtype=x.dtype)).sum(-1).astype(jnp.int32)
            indices = jax.lax.stop_gradient(indices)
            xa = _ln(x, ln1_g, ln1_b)
            q = (xa @ wq.T + bq).reshape(B, N, HEADS, HD).transpose(0, 2, 1, 3)
            k = (xa @ wk.T + bk).reshape(B, N, HEADS, HD).transpose(0, 2, 1, 3)
            v = (xa @ wv.T + bv).reshape(B, N, HEADS, HD).transpose(0, 2, 1, 3)
            s = jax.nn.softmax(jnp.einsum('bhqd,bhkd->bhqk', q, k) / np.float32(np.sqrt(HD)), axis=-1)
            o = jnp.einsum('bhqk,bhkd->bhqd', s, v).transpose(0, 2, 1, 3).reshape(B, N, DIM)
            o = o @ wo.T + bo
            h = x + bits[:, :, 0:1] * o
            xf = _ln(h, ln2_g, ln2_b)
            ff = _gelu(xf @ fc1_w.T + fc1_b) @ fc2_w.T + fc2_b
            out = h + bits[:, :, 1:2] * ff
            down = jnp.einsum('bnd,krd->bknr', out, lra_down)
            up = jnp.einsum('bknr,kdr->bknd', down, lra_up)
            sel = jax.nn.one_hot(indices, 3, dtype=x.dtype)
            out = out + jnp.einsum('bknd,bnk->bnd', up, sel)
            return out
        key = jax.random.key(seed)
        ks = iter(jax.random.split(key, 40))

        def w(shape, std=0.02):
            return (jax.random.normal(next(ks), shape) * std).astype(jnp.float32)
        B, N = (128, 197)
        inp = {'x': jax.random.normal(next(ks), (B, N, DIM), dtype=jnp.float32)}
        inp.update(wq=w((DIM, DIM)), bq=jnp.zeros((DIM,), jnp.float32), wk=w((DIM, DIM)), bk=jnp.zeros((DIM,), jnp.float32), wv=w((DIM, DIM)), bv=jnp.zeros((DIM,), jnp.float32), wo=w((DIM, DIM)), bo=jnp.zeros((DIM,), jnp.float32), ln1_g=jnp.ones((DIM,), jnp.float32), ln1_b=jnp.zeros((DIM,), jnp.float32), ln2_g=jnp.ones((DIM,), jnp.float32), ln2_b=jnp.zeros((DIM,), jnp.float32), fc1_w=w((MLP, DIM)), fc1_b=jnp.zeros((MLP,), jnp.float32), fc2_w=w((DIM, MLP)), fc2_b=jnp.zeros((DIM,), jnp.float32), r_ln_g=jnp.ones((DIM,), jnp.float32), r_ln_b=jnp.zeros((DIM,), jnp.float32), r_in_w=w((RHD, DIM)), r_in_b=jnp.zeros((RHD,), jnp.float32), r_o1_w=w((RHD, 2 * RHD)), r_o1_b=jnp.zeros((RHD,), jnp.float32), r_o2_w=w((RHD // 2, RHD)), r_o2_b=jnp.zeros((RHD // 2,), jnp.float32), r_o3_w=w((2 * BS, RHD // 2), 0.01), r_o3_b=jnp.array([0.0, 5.0, 0.0, 5.0], dtype=jnp.float32), lra_down=w((3, RANK, DIM), 0.01), lra_up=w((3, DIM, RANK), 0.01))
        return inp
    _L1_ffn_all = _L1_ffn_setup()
    _L1_ffn_in = {k: v for k, v in _L1_ffn_all.items() if k in ('wq', 'bq', 'wk', 'bk', 'wv', 'bv', 'wo', 'bo', 'ln1_g', 'ln1_b', 'ln2_g', 'ln2_b', 'fc1_w', 'fc1_b', 'fc2_w', 'fc2_b', 'r_ln_g', 'r_ln_b', 'r_in_w', 'r_in_b', 'r_o1_w', 'r_o1_b', 'r_o2_w', 'r_o2_b', 'r_o3_w', 'r_o3_b', 'lra_down', 'lra_up')}
    del _L1_ffn_all
    return {'x': x, 'txt': txt, 'L0_tok_conv_w': _L0_tok_in['conv_w'], 'L0_tok_conv_b': _L0_tok_in['conv_b'], 'L0_tok_pos_table': _L0_tok_in['pos_table'], 'L0_attn_memory': _L0_attn_in['memory'], 'L0_attn_Wq': _L0_attn_in['Wq'], 'L0_attn_bq': _L0_attn_in['bq'], 'L0_attn_Wk': _L0_attn_in['Wk'], 'L0_attn_bk': _L0_attn_in['bk'], 'L0_attn_Wv': _L0_attn_in['Wv'], 'L0_attn_bv': _L0_attn_in['bv'], 'L0_attn_Wo': _L0_attn_in['Wo'], 'L0_attn_bo': _L0_attn_in['bo'], 'L0_ffn_scale': _L0_ffn_in['scale'], 'L0_ffn_gate_w': _L0_ffn_in['gate_w'], 'L0_ffn_gate_b': _L0_ffn_in['gate_b'], 'L0_ffn_w1': _L0_ffn_in['w1'], 'L0_ffn_b1': _L0_ffn_in['b1'], 'L0_ffn_w2': _L0_ffn_in['w2'], 'L0_ffn_b2': _L0_ffn_in['b2'], 'L1_attn_w_qkv': _L1_attn_in['w_qkv'], 'L1_attn_w_g0': _L1_attn_in['w_g0'], 'L1_attn_w_g1': _L1_attn_in['w_g1'], 'L1_attn_w_proj': _L1_attn_in['w_proj'], 'L1_attn_b_proj': _L1_attn_in['b_proj'], 'L1_ffn_wq': _L1_ffn_in['wq'], 'L1_ffn_bq': _L1_ffn_in['bq'], 'L1_ffn_wk': _L1_ffn_in['wk'], 'L1_ffn_bk': _L1_ffn_in['bk'], 'L1_ffn_wv': _L1_ffn_in['wv'], 'L1_ffn_bv': _L1_ffn_in['bv'], 'L1_ffn_wo': _L1_ffn_in['wo'], 'L1_ffn_bo': _L1_ffn_in['bo'], 'L1_ffn_ln1_g': _L1_ffn_in['ln1_g'], 'L1_ffn_ln1_b': _L1_ffn_in['ln1_b'], 'L1_ffn_ln2_g': _L1_ffn_in['ln2_g'], 'L1_ffn_ln2_b': _L1_ffn_in['ln2_b'], 'L1_ffn_fc1_w': _L1_ffn_in['fc1_w'], 'L1_ffn_fc1_b': _L1_ffn_in['fc1_b'], 'L1_ffn_fc2_w': _L1_ffn_in['fc2_w'], 'L1_ffn_fc2_b': _L1_ffn_in['fc2_b'], 'L1_ffn_r_ln_g': _L1_ffn_in['r_ln_g'], 'L1_ffn_r_ln_b': _L1_ffn_in['r_ln_b'], 'L1_ffn_r_in_w': _L1_ffn_in['r_in_w'], 'L1_ffn_r_in_b': _L1_ffn_in['r_in_b'], 'L1_ffn_r_o1_w': _L1_ffn_in['r_o1_w'], 'L1_ffn_r_o1_b': _L1_ffn_in['r_o1_b'], 'L1_ffn_r_o2_w': _L1_ffn_in['r_o2_w'], 'L1_ffn_r_o2_b': _L1_ffn_in['r_o2_b'], 'L1_ffn_r_o3_w': _L1_ffn_in['r_o3_w'], 'L1_ffn_r_o3_b': _L1_ffn_in['r_o3_b'], 'L1_ffn_lra_down': _L1_ffn_in['lra_down'], 'L1_ffn_lra_up': _L1_ffn_in['lra_up']}

def reference(x, txt, L0_tok_conv_w, L0_tok_conv_b, L0_tok_pos_table, L0_attn_memory, L0_attn_Wq, L0_attn_bq, L0_attn_Wk, L0_attn_bk, L0_attn_Wv, L0_attn_bv, L0_attn_Wo, L0_attn_bo, L0_ffn_scale, L0_ffn_gate_w, L0_ffn_gate_b, L0_ffn_w1, L0_ffn_b1, L0_ffn_w2, L0_ffn_b2, L1_attn_w_qkv, L1_attn_w_g0, L1_attn_w_g1, L1_attn_w_proj, L1_attn_b_proj, L1_ffn_wq, L1_ffn_bq, L1_ffn_wk, L1_ffn_bk, L1_ffn_wv, L1_ffn_bv, L1_ffn_wo, L1_ffn_bo, L1_ffn_ln1_g, L1_ffn_ln1_b, L1_ffn_ln2_g, L1_ffn_ln2_b, L1_ffn_fc1_w, L1_ffn_fc1_b, L1_ffn_fc2_w, L1_ffn_fc2_b, L1_ffn_r_ln_g, L1_ffn_r_ln_b, L1_ffn_r_in_w, L1_ffn_r_in_b, L1_ffn_r_o1_w, L1_ffn_r_o1_b, L1_ffn_r_o2_w, L1_ffn_r_o2_b, L1_ffn_r_o3_w, L1_ffn_r_o3_b, L1_ffn_lra_down, L1_ffn_lra_up):
    import jax
    import jax.numpy as jnp

    def _L0_tok_ref(pixel_values, conv_w, conv_b, pos_table):
        import jax, jax.numpy as jnp
        import numpy as np
        from jax import lax
        HIDDEN = 192
        C_IN = 3
        PATCH = 16
        SIDE = 32
        NUM_PATCHES = SIDE * SIDE

        def _position_ids(nb_h, nb_w):
            boundaries = np.arange(1.0 / SIDE, 1.0, 1.0 / SIDE, dtype=np.float32)
            frac_h = np.arange(0.0, 1.0 - 1e-06, 1.0 / nb_h, dtype=np.float32)
            frac_w = np.arange(0.0, 1.0 - 1e-06, 1.0 / nb_w, dtype=np.float32)
            bh = np.searchsorted(boundaries, frac_h, side='right')
            bw = np.searchsorted(boundaries, frac_w, side='right')
            return jnp.asarray((bh[:, None] * SIDE + bw).reshape(-1), dtype=jnp.int32)
        B, _, H, W = pixel_values.shape
        nb_h, nb_w = (H // PATCH, W // PATCH)
        patches = lax.conv_general_dilated(pixel_values, conv_w, window_strides=(PATCH, PATCH), padding='VALID', dimension_numbers=('NCHW', 'OIHW', 'NCHW'))
        patches = patches + conv_b[None, :, None, None]
        embeddings = patches.reshape(B, HIDDEN, nb_h * nb_w).transpose(0, 2, 1)
        pos_ids = _position_ids(nb_h, nb_w)
        pos_emb = pos_table[pos_ids]
        return embeddings + pos_emb[None, :, :]

    def _L0_attn_ref(x, memory, Wq, bq, Wk, bk, Wv, bv, Wo, bo):
        import jax, jax.numpy as jnp
        import numpy as np
        B, N, M, D = (128, 64, 8, 192)
        b, n, d = x.shape
        m = memory.shape[0]
        t = n + m
        scaling = d ** (-0.5)
        cat = jnp.concatenate([x, jnp.broadcast_to(memory[None], (b, m, d))], axis=1)
        q = cat @ Wq + bq
        k = cat @ Wk + bk
        v = cat @ Wv + bv
        att = jax.nn.softmax(jnp.einsum('bqd,bkd->bqk', q, k) * scaling, axis=-1)
        row_mask = (jnp.arange(t) < n).astype(att.dtype)[None, :, None]
        att = att * row_mask
        head_out = jnp.einsum('bqk,bkd->bqd', att, v)
        attended = head_out @ Wo + bo
        return attended[:, :n, :]

    def _L0_ffn_ref(x, scale, gate_w, gate_b, w1, b1, w2, b2):
        import jax, jax.numpy as jnp
        import numpy as np
        B, S, H = (2, 256, 192)
        E, K, I = (16, 4, 192)
        ALPHA, LIMIT, EPS = (1.702, 7.0, 1e-05)

        def _swiglu(h):
            x_glu, x_lin = jnp.split(h, 2, axis=-1)
            x_glu = jnp.minimum(x_glu, LIMIT)
            x_lin = jnp.clip(x_lin, -LIMIT, LIMIT)
            return x_glu * jax.nn.sigmoid(ALPHA * x_glu) * (x_lin + 1.0)
        Bx, Sx, Hx = x.shape
        xf = x.astype(jnp.float32)
        t = xf * jax.lax.rsqrt(jnp.mean(xf * xf, axis=-1, keepdims=True) + EPS) * scale
        t = t.reshape(-1, Hx)
        T = t.shape[0]
        g = t @ gate_w.T + gate_b
        vals, idx = jax.lax.top_k(g, K)
        w = jax.nn.softmax(vals, axis=-1) / K
        full_w = jnp.zeros((T, E), jnp.float32).at[jnp.arange(T)[:, None], idx].set(w)
        h = jnp.einsum('th,ehf->tef', t, w1) + b1
        h = _swiglu(h)
        y = jnp.einsum('tei,eih->teh', h, w2) + b2
        out = jnp.einsum('teh,te->th', y, full_w) * K
        return x + out.astype(x.dtype).reshape(Bx, Sx, Hx)

    def _L1_attn_ref(x, w_qkv, w_g0, w_g1, w_proj, b_proj):
        import jax, jax.numpy as jnp
        import numpy as np
        DIM = 192
        NUM_HEADS = 8
        GROUPS = 2
        B, N, C = x.shape
        H = NUM_HEADS
        hd = C // H
        scale = hd ** (-0.5)
        g = GROUPS
        g_dim = C // g
        qkv = (x @ w_qkv.T).reshape(B, N, 3, H, hd)
        qkv = jnp.transpose(qkv, (2, 0, 3, 1, 4))
        q, k, v = (qkv[0], qkv[1], qkv[2])
        attn = jax.nn.softmax(jnp.einsum('bhnd,bhmd->bhnm', q, k) * scale, axis=-1)
        origin = jnp.einsum('bhnm,bhmd->bhnd', attn, v)
        origin = origin.swapaxes(1, 2).reshape(B, N, g, g_dim)
        xg = x.reshape(B, N, g, g_dim)
        head_x = jnp.zeros((B, N, g_dim), dtype=x.dtype)
        outputs = []
        for i, w in enumerate([w_g0, w_g1]):
            cur = xg[:, :, i] + head_x
            qkv2 = (cur @ w.T).reshape(B, N, 3, g_dim)
            q2, k2, v2 = (qkv2[:, :, 0], qkv2[:, :, 1], qkv2[:, :, 2])
            a2 = jax.nn.softmax(jnp.einsum('bnd,bmd->bnm', q2, k2) * scale, axis=-1)
            head_x = jnp.einsum('bnm,bmd->bnd', a2, v2)
            outputs.append(head_x + origin[:, :, i])
        out = jnp.concatenate(outputs, axis=-1)
        return out @ w_proj.T + b_proj

    def _L1_ffn_ref(x, wq, bq, wk, bk, wv, bv, wo, bo, ln1_g, ln1_b, ln2_g, ln2_b, fc1_w, fc1_b, fc2_w, fc2_b, r_ln_g, r_ln_b, r_in_w, r_in_b, r_o1_w, r_o1_b, r_o2_w, r_o2_b, r_o3_w, r_o3_b, lra_down, lra_up):
        import jax, jax.numpy as jnp
        import numpy as np
        DIM = 192
        HEADS = 12
        HD = DIM // HEADS
        MLP = 768
        RHD = 128
        RANK = 64
        BS = 2
        RESERVE = 1
        EPS = 1e-05

        def _ln(x, g, b):
            m = jnp.mean(x, axis=-1, keepdims=True)
            v = jnp.var(x, axis=-1, keepdims=True)
            return (x - m) / jnp.sqrt(v + EPS) * g + b

        def _gelu(t):
            return jax.nn.gelu(t, approximate=False)

        def _forward(x, wq, bq, wk, bk, wv, bv, wo, bo, ln1_g, ln1_b, ln2_g, ln2_b, fc1_w, fc1_b, fc2_w, fc2_b, r_ln_g, r_ln_b, r_in_w, r_in_b, r_o1_w, r_o1_b, r_o2_w, r_o2_b, r_o3_w, r_o3_b, lra_down, lra_up):
            B, N, _ = x.shape
            e = _gelu(_ln(x, r_ln_g, r_ln_b) @ r_in_w.T + r_in_b)
            g = jnp.mean(e[:, RESERVE:, :], axis=1, keepdims=True)
            f = jnp.concatenate([e, jnp.broadcast_to(g, e.shape)], axis=-1)
            h1 = _gelu(f @ r_o1_w.T + r_o1_b)
            h2 = _gelu(h1 @ r_o2_w.T + r_o2_b)
            logits = (h2 @ r_o3_w.T + r_o3_b).reshape(B, N, BS, 2)
            hard = jax.nn.one_hot(jnp.argmax(logits, axis=-1), 2, dtype=x.dtype)
            keep = jnp.broadcast_to(jnp.array([0.0, 1.0], dtype=x.dtype), hard[:, :RESERVE].shape)
            hard = hard.at[:, :RESERVE].set(keep)
            hard = jax.lax.stop_gradient(hard)
            bits = hard[..., 1]
            indices = (bits * jnp.array([2.0, 1.0], dtype=x.dtype)).sum(-1).astype(jnp.int32)
            indices = jax.lax.stop_gradient(indices)
            xa = _ln(x, ln1_g, ln1_b)
            q = (xa @ wq.T + bq).reshape(B, N, HEADS, HD).transpose(0, 2, 1, 3)
            k = (xa @ wk.T + bk).reshape(B, N, HEADS, HD).transpose(0, 2, 1, 3)
            v = (xa @ wv.T + bv).reshape(B, N, HEADS, HD).transpose(0, 2, 1, 3)
            s = jax.nn.softmax(jnp.einsum('bhqd,bhkd->bhqk', q, k) / np.float32(np.sqrt(HD)), axis=-1)
            o = jnp.einsum('bhqk,bhkd->bhqd', s, v).transpose(0, 2, 1, 3).reshape(B, N, DIM)
            o = o @ wo.T + bo
            h = x + bits[:, :, 0:1] * o
            xf = _ln(h, ln2_g, ln2_b)
            ff = _gelu(xf @ fc1_w.T + fc1_b) @ fc2_w.T + fc2_b
            out = h + bits[:, :, 1:2] * ff
            down = jnp.einsum('bnd,krd->bknr', out, lra_down)
            up = jnp.einsum('bknr,kdr->bknd', down, lra_up)
            sel = jax.nn.one_hot(indices, 3, dtype=x.dtype)
            out = out + jnp.einsum('bknd,bnk->bnd', up, sel)
            return out
        return _forward(x, wq, bq, wk, bk, wv, bv, wo, bo, ln1_g, ln1_b, ln2_g, ln2_b, fc1_w, fc1_b, fc2_w, fc2_b, r_ln_g, r_ln_b, r_in_w, r_in_b, r_o1_w, r_o1_b, r_o2_w, r_o2_b, r_o3_w, r_o3_b, lra_down, lra_up)
    h = _L0_tok_ref(x, L0_tok_conv_w, L0_tok_conv_b, L0_tok_pos_table)
    h = jnp.concatenate([h, txt], axis=1)
    h = h + _L0_attn_ref(_layernorm(h, axis=-1), L0_attn_memory, L0_attn_Wq, L0_attn_bq, L0_attn_Wk, L0_attn_bk, L0_attn_Wv, L0_attn_bv, L0_attn_Wo, L0_attn_bo)
    h = h + _L0_ffn_ref(_layernorm(h, axis=-1), L0_ffn_scale, L0_ffn_gate_w, L0_ffn_gate_b, L0_ffn_w1, L0_ffn_b1, L0_ffn_w2, L0_ffn_b2)
    h = h + _L1_attn_ref(_layernorm(h, axis=-1), L1_attn_w_qkv, L1_attn_w_g0, L1_attn_w_g1, L1_attn_w_proj, L1_attn_b_proj)
    h = h + _L1_ffn_ref(_layernorm(h, axis=-1), L1_ffn_wq, L1_ffn_bq, L1_ffn_wk, L1_ffn_bk, L1_ffn_wv, L1_ffn_bv, L1_ffn_wo, L1_ffn_bo, L1_ffn_ln1_g, L1_ffn_ln1_b, L1_ffn_ln2_g, L1_ffn_ln2_b, L1_ffn_fc1_w, L1_ffn_fc1_b, L1_ffn_fc2_w, L1_ffn_fc2_b, L1_ffn_r_ln_g, L1_ffn_r_ln_b, L1_ffn_r_in_w, L1_ffn_r_in_b, L1_ffn_r_o1_w, L1_ffn_r_o1_b, L1_ffn_r_o2_w, L1_ffn_r_o2_b, L1_ffn_r_o3_w, L1_ffn_r_o3_b, L1_ffn_lra_down, L1_ffn_lra_up)
    return h

_drawn_inputs = setup_inputs


def setup_inputs(seed=0):
    import zlib

    import numpy as np

    out = dict(_drawn_inputs(seed))
    spreads = {'L0_tok_conv_b': (0.0, 0.1),
     'L0_attn_bq': (0.0, 0.336),
     'L0_attn_bk': (0.0, 2.0),
     'L0_attn_bv': (0.0, 0.1),
     'L0_attn_bo': (0.0, 0.1),
     'L0_ffn_scale': (1.0, 0.6),
     'L0_ffn_gate_b': (0.0, 0.8),
     'L1_ffn_bq': (0.0, 0.8),
     'L1_ffn_bk': (0.0, 2.0),
     'L1_ffn_bv': (0.0, 0.8),
     'L1_ffn_bo': (0.0, 0.388),
     'L1_ffn_ln1_g': (1.0, 0.6),
     'L1_ffn_ln1_b': (0.0, 0.8),
     'L1_ffn_ln2_g': (1.0, 0.6),
     'L1_ffn_ln2_b': (0.0, 2.0),
     'L1_ffn_fc1_b': (0.0, 0.715),
     'L1_ffn_fc2_b': (0.0, 0.336),
     'L1_ffn_r_ln_g': (1.0, 0.2),
     'L1_ffn_r_ln_b': (0.0, 0.1),
     'L1_ffn_r_in_b': (0.0, 0.1),
     'L1_ffn_r_o1_b': (0.0, 0.1),
     'L1_ffn_r_o2_b': (0.0, 0.1)}
    factors = {'L0_tok_pos_table': 2.737,
     'L0_attn_memory': 8.0,
     'L0_ffn_gate_w': 4.361,
     'L0_ffn_w1': 4.131,
     'L0_ffn_b1': 8.0,
     'L0_ffn_w2': 4.041,
     'L0_ffn_b2': 8.0,
     'L1_attn_w_qkv': 4.067,
     'L1_attn_w_g0': 7.652,
     'L1_attn_w_g1': 7.158,
     'L1_attn_w_proj': 2.993,
     'L1_attn_b_proj': 4.249,
     'L1_ffn_wq': 8.0,
     'L1_ffn_wk': 8.0,
     'L1_ffn_wv': 5.839,
     'L1_ffn_wo': 4.053}
    for name, (base, spread) in spreads.items():
        noise = np.random.default_rng([zlib.crc32(name.encode()), seed]).standard_normal(out[name].shape)
        drawn = base * np.exp(spread * noise) if base else spread * noise
        out[name] = jnp.asarray(drawn.astype(out[name].dtype))
    for name, factor in factors.items():
        out[name] = (out[name] * factor).astype(out[name].dtype)
    return out
```

```python
from contextlib import ExitStack

import numpy as np

import concourse.bass as bass
from concourse import mybir

ALU = mybir.AluOpType
ACT = mybir.ActivationFunctionType
AX = mybir.AxisListType
F32 = mybir.dt.float32
F32R = mybir.dt.float32r
U32 = mybir.dt.uint32

B = 16
SIDE, PATCH, CHANNELS = 96, 16, 3
GRID = SIDE // PATCH
NP = GRID * GRID
NT = 77
N = NP + NT
D = 192
LO, HI = 128, D - 128
M = 8
NK = N + M
G = 4
STEPS = B // G
GN = G * N
E, TOPK, I = 16, 4, 192
EPS = 1e-5


class Names:
    pass


class Counted:
    def __init__(self, sem, per):
        self.sem, self.per = sem, per


class W0:
    q, k, v, o, g = 0, D, 2 * D, 3 * D, 4 * D
    cq, ck, cs = 0, 1, 2


class W1:
    q, k, v, o = 0, 256, 512, 512 + D


class W4:
    r, q, k, v, o, f, dn, up = 0, 128, 512, 896, 896 + D, 896 + 2 * D, 1664 + 2 * D, 1664 + 3 * D
    width = 1664 + 4 * D


class C4:
    rg, rb, g1, b1, g2, b2, r, h1, h2, q, k, f = 0, 1, 2, 3, 4, 5, 6, 7, 8, 9, 12, 15


def counted(nc, ctx, name, per):
    return Counted(ctx.enter_context(nc.semaphore(name)), per)


def done(s, it, n):
    return s.sem, s.per * (it + 1) + n + 1


def before(n, ring, per):
    return n - ring if n >= ring else max(m for m in range(per) if m % ring == n % ring) - per


def credit(eng, *sems):
    for s in sems:
        eng.sem_inc(s.sem, s.per)


def settle(eng, S):
    eng.sem_inc(S.settled, 1)


def bc(ap, shape):
    return ap.to_broadcast(shape)


def tok_phase(nc, dram, S):
    KT = CHANNELS * PATCH * PATCH // 128
    PER = 3
    CH = [(b, min(PER, B - b)) for b in range(0, B, PER)]
    with ExitStack() as ctx:
        patches = ctx.enter_context(nc.sbuf_tensor("patches", [128, KT, B * NP], F32))
        conv = ctx.enter_context(nc.sbuf_tensor("conv", [128, KT, D], F32))
        pos = ctx.enter_context(nc.sbuf_tensor("pos", [PER * NP, D], F32))
        convb = ctx.enter_context(nc.sbuf_tensor("convb", [PER * NP, D], F32))
        emb = ctx.enter_context(nc.sbuf_tensor("emb", [PER * NP, len(CH), D], F32))
        ps = [ctx.enter_context(nc.psum_tensor(f"tok_ps{i}", [128, 512], F32)) for i in range(len(CH))]
        sem = lambda n: ctx.enter_context(nc.semaphore(n))
        k_in = [sem(f"tok_in{k}") for k in range(KT)]
        rows_in, posb, emb_ps, emb_ok, h_in = sem("tok_rows"), sem("tok_posb"), sem("tok_ps"), sem("tok_emb"), sem("tok_h")
        ident0 = sem("ident0")
        block = ctx.enter_context(nc.Block())

        @block.sync
        def _(sp):
            for k in range(KT):
                sp.dma_start(patches[:, k, :], dram.patches[:, k, :]).then_inc(k_in[k], 16)
                sp.dma_start(conv[:, k, :], dram.conv[:, k, :]).then_inc(k_in[k], 16)
            sp.dma_start(S.H[NP:N, :, :], dram.txt.rearrange("b t d -> t b d")).then_inc(h_in, 16)
            for c, (b, nb) in enumerate(CH):
                for j in range(nb):
                    sp.wait_ge(emb_ok, c + 1)
                    sp.dma_start(S.H[0:NP, b + j, :], emb[j * NP:(j + 1) * NP, c, :]).then_inc(h_in, 16)
            sp.wait_ge(h_in, 16 * (B + 1))

        @block.scalar
        def _(act):
            act.dma_start(pos[:], dram.pos).then_inc(rows_in, 16)
            act.dma_start(convb[:], bc(dram.conv_b, [PER * NP, D])).then_inc(rows_in, 16)
            for t, src in S.loads:
                act.dma_start(t, src).then_inc(S.weights_in, 16)
            act.wait_ge(S.weights_in, 16 * len(S.loads))

        @block.gpsimd
        def _(pool):
            nc.gpsimd.memset(S.ident[:], 0.0).then_inc(ident0, 1)
            pool.wait_ge(ident0, 1)
            nc.gpsimd.affine_select(out=S.ident[:], in_=S.ident[:], compare_op=ALU.not_equal, fill=1.0, base=0,
                                    pattern=[[-1, 128]], channel_multiplier=1).then_inc(S.consts_ok, 1)
            nc.gpsimd.iota(S.iota[:], pattern=[[1, E]], base=0, channel_multiplier=0,
                           allow_small_or_imprecise_dtypes=True).then_inc(S.consts_ok, 1)
            nc.gpsimd.memset(S.mhalf[:], -0.5).then_inc(S.consts_ok, 1)
            for n, t in enumerate(S.ones_rows):
                pool.wait_ge(S.consts_ok, 3 + n)
                nc.gpsimd.memset(t, 1.0).then_inc(S.consts_ok, 1)

        @block.tensor
        def _(pe):
            for k in range(KT):
                pe.wait_ge(k_in[k], 32)
                for c, (b, nb) in enumerate(CH):
                    mm = nc.tensor.matmul(ps[c][0:nb * NP, 0:D], patches[:, k, b * NP:(b + nb) * NP], conv[:, k, :],
                                          start=(k == 0), stop=(k == KT - 1))
                    if k == KT - 1:
                        mm.then_inc(emb_ps, 1)

        @block.vector
        def _(dve):
            dve.wait_ge(rows_in, 32)
            nc.vector.tensor_tensor(pos[:], pos[:], convb[:], ALU.add).then_inc(posb, 1)
            dve.wait_ge(posb, 1)
            for c, (b, nb) in enumerate(CH):
                dve.wait_ge(emb_ps, c + 1)
                nc.vector.tensor_tensor(emb[0:nb * NP, c, :], ps[c][0:nb * NP, 0:D], pos[0:nb * NP, :],
                                        ALU.add).then_inc(emb_ok, 1)


def attn0_phase(nc, dram, S):
    with ExitStack() as ctx:
        def sb(name, shape, dt=F32):
            return ctx.enter_context(nc.sbuf_tensor("a0_" + name, shape, dt))

        def sem(name, per):
            return counted(nc, ctx, "a0_" + name, per)

        w = W0
        xn = sb("xn", [N, G, D])
        stats, mv, veps, rstd = sb("stats", [N, G, 6]), sb("mv", [N, G, 2]), sb("veps", [N, G]), sb("rstd", [N, G])
        cat1, cat2 = S.cat1, S.cat2
        q1, q2 = sb("q1", [LO, G, N]), sb("q2", [HI, G, N])
        k1, k2 = sb("k1", [LO, G, NK]), sb("k2", [HI, G, NK])
        v = sb("v", [NK, G, D])
        mx, rs, ri = sb("mx", [N, G]), sb("rs", [N, G]), sb("ri", [N, G])
        p, pT = sb("p", [N, G, NK]), sb("pT", [NK, G, N])
        o1, o2 = sb("o1", [LO, G, N]), S.a0_o2
        stats2, mv2, veps2, rstd2 = sb("stats2", [N, G, 6]), sb("mv2", [N, G, 2]), sb("veps2", [N, G]), sb("rstd2", [N, G])
        x, sq, ssq, veps3, rrms = sb("x", [N, G, D]), sb("sq", [N, D]), sb("ssq", [N, G]), sb("veps3", [N, G]), sb("rrms", [N, G])
        t, tS1, tS2 = sb("t", [N, G, D]), sb("tS1", [LO, G, N]), S.a0_tS2
        g, top, idx, idxf = sb("g", [N, G, E]), sb("top", [N, G, 8]), sb("idx", [N, G, 8], U32), sb("idxf", [N, G, TOPK])
        e4, s4, r4, w4 = sb("e4", [N, G, TOPK]), sb("s4", [N, G]), sb("r4", [N, G]), sb("w4", [N, G, TOPK])
        oh, fw, fwT = sb("oh", [N, G, E, TOPK]), sb("fw", [N, G, E]), sb("fwT", [E, GN])
        bank = [ctx.enter_context(nc.psum_tensor(f"a0_ps{i}", [128, 512], F32)) for i in range(8)]
        A, V, SC, PT = bank[0:2], bank[2:5], bank[5], bank[6]

        stat_ok, mean_ok, veps_ok, rstd_ok = sem("stat_ok", 8), sem("mean_ok", 8), sem("veps_ok", 3), sem("rstd_ok", 3)
        xn_ok, x_ok, ssq_ok, t_ok, hx_ok = sem("xn_ok", 4), sem("x_ok", 4), sem("ssq_ok", 4), sem("t_ok", 4), sem("hx_ok", 1)
        a_ps, a_out = sem("a_ps", 6), sem("a_out", 6)
        v_ps, v_out = sem("v_ps", 10), sem("v_out", 10)
        sc_ps, mx_ok, sub_ok, exp_ok, sum_ok, rec_ok, p_ok = (sem(n, 1) for n in (
            "sc_ps", "mx_ok", "sub_ok", "exp_ok", "sum_ok", "rec_ok", "p_ok"))
        pt_ps, pt_out = sem("pt_ps", 1), sem("pt_out", 1)
        top_ok, idx_ok = sem("top_ok", 4), sem("idx_ok", 4)
        idxf_ok, e4_ok, e4x_ok, s4_ok, r4_ok, w4_ok, oh_ok, ohw_ok, fw_ok = (sem(n, 1) for n in (
            "idxf_ok", "e4_ok", "e4x_ok", "s4_ok", "r4_ok", "w4_ok", "oh_ok", "ohw_ok", "fw_ok"))
        t_stored, fw_stored = sem("t_stored", 32), sem("fw_stored", 32)
        block = ctx.enter_context(nc.Block())
        A_X, A_Q, A_K, A_O, A_T, A_W = range(6)
        V_X, V_Q, V_K, V_V, _, V_O, V_H, _, V_T, V_G = range(10)

        def rows(it):
            return S.H[0:N, :, :].rearrange("p b d -> p (b d)")[:, bass.ds(it * (G * D), G * D)].rearrange(
                "p (b d) -> p b d", b=G)

        def ring(tiles, n):
            return tiles[n % len(tiles)]

        @block.tensor
        def _(pe):
            credit(pe, a_ps, v_ps, sc_ps, pt_ps)
            pe.wait_ge(S.consts_ok, S.n_consts)
            mm = nc.tensor.matmul
            with pe.Fori(0, STEPS) as it:
                def fill(n):
                    pe.wait_ge(*done(a_out, it, before(n, len(A), a_out.per)))
                    return ring(A, n)

                def fill_v(n):
                    pe.wait_ge(*done(v_out, it, before(n, len(V), v_out.per)))
                    return ring(V, n)

                a, b = fill(A_X), fill_v(V_X)
                for j in range(G):
                    pe.wait_ge(*done(xn_ok, it, j))
                    m = nc.tensor.transpose(a[0:LO, j * N:(j + 1) * N], xn[:, j, 0:LO], S.ident[0:N, 0:N])
                m.then_inc(a_ps.sem, 1)
                for j in range(G):
                    m = nc.tensor.transpose(b[0:HI, j * N:(j + 1) * N], xn[:, j, LO:D], S.ident[0:N, 0:N])
                m.then_inc(v_ps.sem, 1)
                pe.wait_ge(*done(a_out, it, A_X))
                pe.wait_ge(*done(v_out, it, V_X))
                for col, wd, n1, n2 in ((w.q, N, A_Q, V_Q), (w.k, NK, V_K, A_K)):
                    for half, (c0, c1) in enumerate(((0, LO), (LO, D))):
                        n = (n1, n2)[half]
                        to_act = (n in (A_Q, A_K)) and ((col is w.q) == (half == 0))
                        o = fill(n) if to_act else fill_v(n)
                        o = o[0:c1 - c0, 0:G * wd].rearrange("p (g n) -> p g n", g=G)
                        mm(o, S.w0a[:, col + c0:col + c1], cat1[:, :, 0:wd], start=True, stop=False)
                        mm(o, S.w0b[0:HI, col + c0:col + c1], cat2[0:HI, :, 0:wd], start=False, stop=True
                           ).then_inc((a_ps if to_act else v_ps).sem, 1)
                for h in range(2):
                    o = fill_v(V_V + h)
                    for j in (2 * h, 2 * h + 1):
                        c = (j % 2) * D
                        mm(o[0:NK, c:c + D], cat1[:, j, :], S.w0a[:, w.v:w.v + D], start=True, stop=False)
                        m = mm(o[0:NK, c:c + D], cat2[:, j, :], S.w0b[:, w.v:w.v + D], start=False, stop=True)
                    m.then_inc(v_ps.sem, 1)
                pe.wait_ge(*done(a_out, it, A_K))
                pe.wait_ge(*done(v_out, it, V_K))
                pe.wait_ge(*done(sub_ok, it, -1))
                for j in range(G):
                    o = SC[0:N, j * NK:(j + 1) * NK]
                    mm(o, q1[:, j, :], k1[:, j, :], start=True, stop=False)
                    m = mm(o, q2[:, j, :], k2[:, j, :], start=False, stop=True)
                m.then_inc(sc_ps.sem, 1)
                pe.wait_ge(*done(p_ok, it, 0))
                pe.wait_ge(*done(pt_out, it, -1))
                for j in range(G):
                    m = nc.tensor.transpose(PT[0:NK, j * N:(j + 1) * N], p[:, j, :], S.ident[0:N, 0:N])
                m.then_inc(pt_ps.sem, 1)
                pe.wait_ge(*done(pt_out, it, 0))
                pe.wait_ge(*done(v_out, it, V_V + 1))
                a, b = fill(A_O), fill_v(V_O)
                for j in range(G):
                    m = mm(a[0:LO, j * N:(j + 1) * N], v[:, j, 0:LO], pT[:, j, :], start=True, stop=True)
                m.then_inc(a_ps.sem, 1)
                for j in range(G):
                    m = mm(b[0:HI, j * N:(j + 1) * N], v[:, j, LO:D], pT[:, j, :], start=True, stop=True)
                m.then_inc(v_ps.sem, 1)
                pe.wait_ge(*done(a_out, it, A_O))
                pe.wait_ge(*done(v_out, it, V_O))
                for h in range(2):
                    o = fill_v(V_H + h)
                    for j in (2 * h, 2 * h + 1):
                        c = (j % 2) * D
                        mm(o[0:N, c:c + D], o1[:, j, :], S.w0a[:, w.o:w.o + D], start=True, stop=False)
                        m = mm(o[0:N, c:c + D], o2[:, j, :], S.w0b[:, w.o:w.o + D], start=False, stop=True)
                    m.then_inc(v_ps.sem, 1)
                a, b = fill(A_T), fill_v(V_T)
                for j in range(G):
                    pe.wait_ge(*done(t_ok, it, j))
                    m = nc.tensor.transpose(a[0:LO, j * N:(j + 1) * N], t[:, j, 0:LO], S.ident[0:N, 0:N])
                m.then_inc(a_ps.sem, 1)
                for j in range(G):
                    m = nc.tensor.transpose(b[0:HI, j * N:(j + 1) * N], t[:, j, LO:D], S.ident[0:N, 0:N])
                m.then_inc(v_ps.sem, 1)
                pe.wait_ge(*done(a_out, it, A_T))
                pe.wait_ge(*done(v_out, it, V_T))
                o = fill_v(V_G)
                for j in range(G):
                    mm(o[0:N, j * E:(j + 1) * E], tS1[:, j, :], S.w0a[:, w.g:w.g + E], start=True, stop=False)
                    m = mm(o[0:N, j * E:(j + 1) * E], tS2[:, j, :], S.w0b[:, w.g:w.g + E], start=False, stop=True)
                m.then_inc(v_ps.sem, 1)
                pe.wait_ge(*done(fw_ok, it, 0))
                a = fill(A_W)
                for j in range(G):
                    m = nc.tensor.transpose(a[0:E, j * N:(j + 1) * N], fw[:, j, :], S.ident[0:N, 0:N])
                m.then_inc(a_ps.sem, 1)

        @block.scalar
        def _(act):
            credit(act, a_out, exp_ok, pt_out, ssq_ok, e4x_ok)
            cp = nc.scalar.activation
            with act.Fori(0, STEPS) as it:
                act.wait_ge(*done(a_ps, it, A_X))
                act.wait_ge(*done(v_ps, it, V_V + 1 - v_ps.per))
                cp(cat1[:, :, 0:N], ring(A, A_X)[0:LO, 0:GN].rearrange("p (g n) -> p g n", g=G), ACT.Copy
                   ).then_inc(a_out.sem, 1)
                act.wait_ge(*done(a_ps, it, A_Q))
                act.wait_ge(*done(sc_ps, it, -1))
                cp(q1[:], ring(A, A_Q)[0:LO, 0:GN], ACT.Identity, bias=S.c0a[:, w.cq:w.cq + 1]).then_inc(a_out.sem, 1)
                act.wait_ge(*done(a_ps, it, A_K))
                cp(k2[:], ring(A, A_K)[0:HI, 0:G * NK], ACT.Identity, bias=S.c0b[:, w.ck:w.ck + 1]).then_inc(a_out.sem, 1)
                act.wait_ge(*done(sub_ok, it, 0))
                cp(p[:], p[:], ACT.Exp, scale=float(D) ** -0.5).then_inc(exp_ok.sem, 1)
                act.wait_ge(*done(pt_ps, it, 0))
                act.wait_ge(*done(v_ps, it, V_O - v_ps.per))
                cp(pT[:], PT[0:NK, 0:GN], ACT.Copy).then_inc(pt_out.sem, 1)
                act.wait_ge(*done(a_ps, it, A_O))
                act.wait_ge(*done(v_ps, it, V_H + 1 - v_ps.per))
                cp(o1[:], ring(A, A_O)[0:LO, 0:GN], ACT.Copy).then_inc(a_out.sem, 1)
                for j in range(G):
                    act.wait_ge(*done(x_ok, it, j))
                    if j == 0:
                        act.wait_ge(*done(veps_ok, it, -1))
                    cp(sq[:], x[:, j, :], ACT.Square, accum_out=ssq[:, j:j + 1]).then_inc(ssq_ok.sem, 1)
                    act.wait_ge(*done(ssq_ok, it, j))
                act.wait_ge(*done(a_ps, it, A_T))
                act.wait_ge(*done(v_ps, it, V_G - v_ps.per))
                act.wait_ge(*done(t_stored, it, -1))
                cp(tS1[:], ring(A, A_T)[0:LO, 0:GN], ACT.Identity, scale=S.c0a[:, w.cs:w.cs + 1]).then_inc(a_out.sem, 1)
                act.wait_ge(*done(e4_ok, it, 0))
                cp(e4[:], e4[:], ACT.Exp).then_inc(e4x_ok.sem, 1)
                act.wait_ge(*done(a_ps, it, A_W))
                act.wait_ge(*done(fw_stored, it, -1))
                cp(fwT[:], ring(A, A_W)[0:E, 0:GN], ACT.Copy).then_inc(a_out.sem, 1)

        @block.gpsimd
        def _(pool):
            credit(pool, veps_ok, rstd_ok, hx_ok)
            ts, tt = nc.gpsimd.tensor_scalar, nc.gpsimd.tensor_tensor
            with pool.Fori(0, STEPS) as it:
                for n, (ok, k, src, sc, ve, out) in enumerate((
                        (mean_ok, 3, mv[:, :, 1], 1.0, veps, rstd), (mean_ok, 7, mv2[:, :, 1], 1.0, veps2, rstd2),
                        (ssq_ok, 3, ssq[:], 1.0 / D, veps3, rrms))):
                    pool.wait_ge(*done(ok, it, k))
                    settle(pool, S)
                    ts(ve[:], src, sc, EPS, ALU.mult, ALU.add).then_inc(veps_ok.sem, 1)
                    pool.wait_ge(*done(veps_ok, it, n))
                    pool.wait_ge(*done((xn_ok, x_ok, t_ok)[n], it, -1))
                    tt(out[:], ve[:], S.mhalf[0:N, 0:G], ALU.pow).then_inc(rstd_ok.sem, 1)
                hg = rows(it)
                tt(hg, hg, x[:], ALU.add).then_inc(hx_ok.sem, 1)

        @block.vector
        def _(dve):
            credit(dve, stat_ok, mean_ok, xn_ok, x_ok, t_ok, v_out, mx_ok, sub_ok, sum_ok, rec_ok, p_ok,
                   top_ok, idx_ok, idxf_ok, e4_ok, s4_ok, r4_ok, w4_ok, oh_ok, ohw_ok, fw_ok)
            nv = nc.vector
            with dve.Fori(0, STEPS) as it:
                hg = rows(it)

                def norm(src, st, m, r, out, base, k, ok):
                    settle(dve, S)
                    for j in range(G):
                        nv.bn_stats(st[:, j, :], src[:, j, :]).then_inc(stat_ok.sem, 1)
                    dve.wait_ge(*done(stat_ok, it, base + 3))
                    settle(dve, S)
                    for j in range(G):
                        nv.bn_aggr(m[:, j, :], st[:, j, :]).then_inc(mean_ok.sem, 1)
                    dve.wait_ge(*done(mean_ok, it, base + 3))
                    dve.wait_ge(*done(rstd_ok, it, k))
                    for j in range(G):
                        nv.tensor_scalar(out[:, j, :], src[:, j, :], m[:, j, 0:1], r[:, j:j + 1],
                                         ALU.subtract, ALU.mult).then_inc(ok.sem, 1)

                dve.wait_ge(*done(v_ps, it, V_X - v_ps.per))
                norm(hg, stats, mv, rstd, xn, 0, 0, xn_ok)
                dve.wait_ge(*done(v_ps, it, V_X))
                nv.tensor_copy(cat2[0:HI, :, 0:N], ring(V, V_X)[0:HI, 0:GN].rearrange("p (g n) -> p g n", g=G)
                               ).then_inc(v_out.sem, 1)
                dve.wait_ge(*done(v_ps, it, V_Q))
                nv.tensor_scalar(q2[:], ring(V, V_Q)[0:HI, 0:GN].rearrange("p (g n) -> p g n", g=G),
                                 S.c0b[:, w.cq:w.cq + 1], None, ALU.add).then_inc(v_out.sem, 1)
                dve.wait_ge(*done(v_ps, it, V_K))
                nv.tensor_scalar(k1[:], ring(V, V_K)[0:LO, 0:G * NK].rearrange("p (g n) -> p g n", g=G),
                                 S.c0a[:, w.ck:w.ck + 1], None, ALU.add).then_inc(v_out.sem, 1)
                for h in range(2):
                    dve.wait_ge(*done(v_ps, it, V_V + h))
                    nv.tensor_copy(v[:, 2 * h:2 * h + 2, :],
                                   ring(V, V_V + h)[0:NK, 0:2 * D].rearrange("p (g n) -> p g n", g=2)
                                   ).then_inc(v_out.sem, 1)
                sc = SC[0:N, 0:G * NK].rearrange("p (g n) -> p g n", g=G)
                dve.wait_ge(*done(sc_ps, it, 0))
                nv.tensor_reduce(mx[:], sc, AX.X, ALU.max).then_inc(mx_ok.sem, 1)
                dve.wait_ge(*done(mx_ok, it, 0))
                dve.wait_ge(*done(pt_ps, it, -1))
                nv.tensor_tensor(p[:], sc, bc(mx[:].unsqueeze(2), [N, G, NK]), ALU.subtract).then_inc(sub_ok.sem, 1)
                dve.wait_ge(*done(exp_ok, it, 0))
                nv.tensor_reduce(rs[:], p[:], AX.X, ALU.add).then_inc(sum_ok.sem, 1)
                dve.wait_ge(*done(sum_ok, it, 0))
                nv.reciprocal(ri[:], rs[:]).then_inc(rec_ok.sem, 1)
                dve.wait_ge(*done(rec_ok, it, 0))
                nv.tensor_tensor(p[:], p[:], bc(ri[:].unsqueeze(2), [N, G, NK]), ALU.mult).then_inc(p_ok.sem, 1)
                dve.wait_ge(*done(v_ps, it, V_O))
                nv.tensor_copy(o2[0:HI, :, :], ring(V, V_O)[0:HI, 0:GN].rearrange("p (g n) -> p g n", g=G)
                               ).then_inc(v_out.sem, 1)
                for h in range(2):
                    dve.wait_ge(*done(v_ps, it, V_H + h))
                    nv.tensor_tensor(hg[:, 2 * h:2 * h + 2, :],
                                     ring(V, V_H + h)[0:N, 0:2 * D].rearrange("p (g n) -> p g n", g=2),
                                     hg[:, 2 * h:2 * h + 2, :], ALU.add).then_inc(v_out.sem, 1)
                dve.wait_ge(*done(v_out, it, V_H + 1))
                dve.wait_ge(*done(hx_ok, it, -1))
                norm(hg, stats2, mv2, rstd2, x, 4, 1, x_ok)
                dve.wait_ge(*done(x_ok, it, 3))
                dve.wait_ge(*done(rstd_ok, it, 2))
                dve.wait_ge(*done(v_ps, it, V_T - v_ps.per))
                for j in range(G):
                    nv.tensor_scalar(t[:, j, :], x[:, j, :], rrms[:, j:j + 1], None, ALU.mult).then_inc(t_ok.sem, 1)
                dve.wait_ge(*done(v_ps, it, V_T))
                dve.wait_ge(*done(t_stored, it, -1))
                nv.tensor_scalar(tS2[0:HI, :, :], ring(V, V_T)[0:HI, 0:GN].rearrange("p (g n) -> p g n", g=G),
                                 S.c0b[:, w.cs:w.cs + 1], None, ALU.mult).then_inc(v_out.sem, 1)
                dve.wait_ge(*done(v_ps, it, V_G))
                nv.tensor_copy(g[:], ring(V, V_G)[0:N, 0:G * E].rearrange("p (g n) -> p g n", g=G)
                               ).then_inc(v_out.sem, 1)
                dve.wait_ge(*done(v_out, it, V_G))
                settle(dve, S)
                for j in range(G):
                    nv.max(top[:, j, :], g[:, j, :]).then_inc(top_ok.sem, 1)
                dve.wait_ge(*done(top_ok, it, 3))
                settle(dve, S)
                for j in range(G):
                    nv.max_index(idx[:, j, :], top[:, j, :], g[:, j, :]).then_inc(idx_ok.sem, 1)
                nv.tensor_tensor(e4[:], top[:, :, 0:TOPK], bc(top[:, :, 0:1], [N, G, TOPK]), ALU.subtract
                                 ).then_inc(e4_ok.sem, 1)
                dve.wait_ge(*done(idx_ok, it, 3))
                nv.tensor_copy(idxf[:], idx[:, :, 0:TOPK]).then_inc(idxf_ok.sem, 1)
                dve.wait_ge(*done(e4x_ok, it, 0))
                nv.tensor_reduce(s4[:], e4[:], AX.X, ALU.add).then_inc(s4_ok.sem, 1)
                dve.wait_ge(*done(s4_ok, it, 0))
                nv.reciprocal(r4[:], s4[:]).then_inc(r4_ok.sem, 1)
                dve.wait_ge(*done(idxf_ok, it, 0))
                nv.tensor_tensor(oh[:], bc(S.iota[0:N, :].unsqueeze(1).unsqueeze(3), [N, G, E, TOPK]),
                                 bc(idxf[:].unsqueeze(2), [N, G, E, TOPK]), ALU.is_equal).then_inc(oh_ok.sem, 1)
                dve.wait_ge(*done(r4_ok, it, 0))
                nv.tensor_tensor(w4[:], e4[:], bc(r4[:].unsqueeze(2), [N, G, TOPK]), ALU.mult).then_inc(w4_ok.sem, 1)
                dve.wait_ge(*done(oh_ok, it, 0))
                dve.wait_ge(*done(w4_ok, it, 0))
                nv.tensor_tensor(oh[:], oh[:], bc(w4[:].unsqueeze(2), [N, G, E, TOPK]), ALU.mult).then_inc(ohw_ok.sem, 1)
                dve.wait_ge(*done(ohw_ok, it, 0))
                dve.wait_ge(*done(a_ps, it, A_W - a_ps.per))
                nv.tensor_reduce(fw[:], oh[:], AX.X, ALU.add).then_inc(fw_ok.sem, 1)

        @block.sync
        def _(sp):
            credit(sp, t_stored, fw_stored)
            with sp.Fori(0, STEPS) as it:
                sp.wait_ge(*done(a_out, it, A_T))
                settle(sp, S)
                sp.dma_start(S.t1[:, bass.ds(it * GN, GN)], tS1[:].rearrange("p g n -> p (g n)")).then_inc(t_stored.sem, 16)
                sp.wait_ge(*done(v_out, it, V_T))
                settle(sp, S)
                sp.dma_start(S.t2[:, bass.ds(it * GN, GN)], tS2[:].rearrange("p g n -> p (g n)")).then_inc(t_stored.sem, 16)
                sp.wait_ge(*done(a_out, it, A_W))
                settle(sp, S)
                sp.dma_start(S.fwT[:, bass.ds(it * GN, GN)], fwT[:]).then_inc(fw_stored.sem, 16)
                sp.dma_start(dram.fw[:, bass.ds(it * GN, GN)], fwT[:]).then_inc(fw_stored.sem, 16)
            sp.wait_ge(*done(t_stored, STEPS - 1, 31))
            sp.wait_ge(*done(fw_stored, STEPS - 1, 31))


def experts_phase(nc, dram, S, half):
    PAIRS, SLOTS, TILES, CHUNKS = E // 2, 2, 3, 2
    UNITS = SLOTS * CHUNKS * TILES
    LOOPS = PAIRS // SLOTS
    HB = B // 2
    HN = HB * N
    ALPHA, LIMIT = 1.702, 7.0
    SIG_LIMIT = float(1.0 / (1.0 + np.exp(-ALPHA * LIMIT)))
    W1 = 2 * TILES * 128
    with ExitStack() as ctx:
        def sb(name, shape, dt=F32):
            return ctx.enter_context(nc.sbuf_tensor(f"ex{half}_" + name, shape, dt))

        def sem(name, per):
            return counted(nc, ctx, f"ex{half}_" + name, per)

        raw1, raw2, raw3 = sb("raw1", [LO, SLOTS, W1]), sb("raw2", [HI + 1, SLOTS, W1]), sb("raw3", [128, SLOTS, TILES * D])
        h1, l1 = sb("h1", [LO, SLOTS, W1], F32R), sb("l1", [LO, SLOTS, W1], F32R)
        h2, l2 = sb("h2", [HI + 1, SLOTS, W1], F32R), sb("l2", [HI + 1, SLOTS, W1], F32R)
        h3, l3 = sb("h3", [128, SLOTS, TILES * D], F32R), sb("l3", [128, SLOTS, TILES * D], F32R)
        wbc = sb("wbc", [128, SLOTS, TILES, HN])
        th1, tl1 = sb("th1", [LO, HN], F32R), sb("tl1", [LO, HN], F32R)
        th2, tl2 = sb("th2", [HI + 1, HN], F32R), sb("tl2", [HI + 1, HN], F32R)
        sg, sw, aa, bb = (sb(n, [128, 2, GN]) for n in ("sg", "sw", "aa", "bb"))
        act_f, act_h, act_l = sb("act_f", [128, 2, GN]), sb("act_h", [128, 3, GN], F32R), sb("act_l", [128, 3, GN], F32R)
        gp = [ctx.enter_context(nc.psum_tensor(f"ex{half}_gps{i}", [128, 512], F32)) for i in range(2)]
        lp = [ctx.enter_context(nc.psum_tensor(f"ex{half}_lps{i}", [128, 512], F32)) for i in range(2)]
        acc = [ctx.enter_context(nc.psum_tensor(f"ex{half}_acc{i}", [128, 512], F32)) for i in range(HB // 2)]

        raw_in = [sem(f"raw_in{s}", 48) for s in range(SLOTS)]
        wbc_in = [sem(f"wbc_in{s}", 64) for s in range(SLOTS)]
        bias_ok = sem("bias_ok", SLOTS)
        hi_ok, lo_ok = sem("hi_ok", 3 * SLOTS), sem("lo_ok", 3 * SLOTS)
        g_ps, l_ps, y_ps = sem("g_ps", UNITS), sem("l_ps", UNITS), sem("y_ps", UNITS)
        sig_ok, sw_ok, a_ok, b_ok = sem("sig_ok", UNITS), sem("sw_ok", UNITS), sem("a_ok", UNITS), sem("b_ok", UNITS)
        f_ok, h_ok, l_ok = sem("f_ok", UNITS), sem("h_ok", UNITS), sem("l_ok", UNITS)
        th_ok, tl_ok, h_done = (ctx.enter_context(nc.semaphore(f"ex{half}_{n}")) for n in ("th_ok", "tl_ok", "h_done"))
        block = ctx.enter_context(nc.Block())

        def unit(k):
            k %= UNITS
            return k // (CHUNKS * TILES), k // TILES % CHUNKS, k % TILES

        def steps(eng, body):
            with eng.Fori(0, LOOPS - 1) as it:
                body(it, False)
            body(LOOPS - 1, True)

        @block.sync
        def _(sp):
            credit(sp, *raw_in, *wbc_in)

            def raw(it, s):
                p = bass.ds(it * SLOTS + s, 1)
                for t, src in ((raw1, dram.w1a), (raw2, dram.w1b), (raw3, dram.w2)):
                    sp.dma_start(t[:, s, :], src[p, :, :].rearrange("e p n -> (e p) n")).then_inc(raw_in[s].sem, 16)

            def routing(it, s):
                for e, p0, p1, m in ((0, 0, 128, 0), (1, 0, 128, 1), (0, 0, 64, 2), (1, 64, 128, 2)):
                    row = dram.fw[bass.ds((it * SLOTS + s) * 2 + e, 1), half * HN:(half + 1) * HN]
                    sp.dma_start(wbc[p0:p1, s, m, :], bc(row, [p1 - p0, HN])).then_inc(wbc_in[s].sem, 16)

            for s in range(SLOTS):
                raw(0, s)
                routing(0, s)

            def body(it, last):
                if last:
                    return
                for s in range(SLOTS):
                    sp.wait_ge(*done(lo_ok, it, 3 * s + 2))
                    settle(sp, S)
                    raw(it + 1, s)
                    sp.wait_ge(*done(sw_ok, it, (s + 1) * CHUNKS * TILES - 1))
                    settle(sp, S)
                    routing(it + 1, s)

            steps(sp, body)

        @block.tensor
        def _(pe):
            credit(pe, g_ps, l_ps, y_ps)
            mm = nc.tensor.matmul
            for j in range(HB):
                b = half * HB + j
                mm(acc[j // 2][0:N, (j % 2) * D:(j % 2 + 1) * D], S.fwT[:, b * N:(b + 1) * N], S.b2[:],
                   start=(j % 2 == 0), stop=False, skip_group_check=True)
            pe.wait_ge(tl_ok, 2)

            def up(it, k):
                s, c, m = unit(k)
                pe.wait_ge(*done(lo_ok, it, 3 * SLOTS * (k // UNITS) + 3 * s + 2))
                cols = slice(c * GN, (c + 1) * GN)
                for o, ok, free, base in ((gp, g_ps, a_ok, 0), (lp, l_ps, b_ok, TILES * 128)):
                    pe.wait_ge(*done(free, it, k - 2))
                    wc = slice(base + m * 128, base + (m + 1) * 128)
                    parts = [(h1, th1), (h1, tl1), (l1, th1), (h2, th2), (h2, tl2), (l2, th2)]
                    for n, (wt, x) in enumerate(parts):
                        i = mm(o[k % 2][:, 0:GN], wt[:, s, wc], x[:, cols], start=(n == 0), stop=(n == len(parts) - 1))
                    i.then_inc(ok.sem, 1)

            def down(it, k):
                s, c, m = unit(k)
                pe.wait_ge(*done(h_ok, it, k))
                pe.wait_ge(*done(l_ok, it, k))
                wc = slice(m * D, (m + 1) * D)
                for j in range(G):
                    img = c * G + j
                    o = acc[img // 2][0:N, (img % 2) * D:(img % 2 + 1) * D]
                    x = slice(j * N, (j + 1) * N)
                    for a, wt in ((act_h, h3), (act_h, l3), (act_l, h3)):
                        i = mm(o, a[:, k % 3, x], wt[:, s, wc], start=False, stop=True, skip_group_check=True)
                i.then_inc(y_ps.sem, 1)

            up(0, 0)
            up(0, 1)

            def body(it, last):
                for k in range(UNITS):
                    if k + 2 < UNITS or not last:
                        up(it, k + 2)
                    down(it, k)

            steps(pe, body)

        @block.scalar
        def _(act):
            credit(act, sig_ok, h_ok, hi_ok)
            cp = nc.scalar.activation
            cp(th1[:], S.t1[:, half * HN:(half + 1) * HN], ACT.Copy).then_inc(th_ok, 1)
            cp(th2[:], S.t2[:, half * HN:(half + 1) * HN], ACT.Copy).then_inc(th_ok, 1)

            def split(it, s, before):
                act.wait_ge(*done(raw_in[s], it, 47))
                act.wait_ge(*done(bias_ok, it, s))
                if before is not None:
                    act.wait_ge(*done(y_ps, *before))
                for h, r in ((h1, raw1), (h2, raw2), (h3, raw3)):
                    cp(h[:, s, :], r[:, s, :], ACT.Copy).then_inc(hi_ok.sem, 1)

            def sigmoid(it, k):
                act.wait_ge(*done(g_ps, it, k))
                act.wait_ge(*done(sw_ok, it, k - 2))
                cp(sg[:, k % 2, :], gp[k % 2][:, 0:GN], ACT.Sigmoid, scale=ALPHA).then_inc(sig_ok.sem, 1)

            split(0, 0, None)
            sigmoid(0, 0)

            def body(it, last):
                for k in range(UNITS):
                    if k + 1 < UNITS or not last:
                        sigmoid(it, k + 1)
                    act.wait_ge(*done(f_ok, it, k))
                    act.wait_ge(*done(y_ps, it, k - 3))
                    act.wait_ge(*done(l_ok, it, k - 3))
                    cp(act_h[:, k % 3, :], act_f[:, k % 2, :], ACT.Copy).then_inc(h_ok.sem, 1)
                    if k == 3:
                        split(it, 1, (it, -1))
                    if k == 9 and not last:
                        split(it + 1, 0, (it, 5))

            steps(act, body)

        @block.vector
        def _(dve):
            credit(dve, bias_ok, sw_ok, a_ok, b_ok, lo_ok)
            nv = nc.vector
            for n, (l, t, h) in enumerate(((tl1, S.t1, th1), (tl2, S.t2, th2))):
                dve.wait_ge(th_ok, n + 1)
                nv.tensor_tensor(l[:], t[:, half * HN:(half + 1) * HN], h[:].bitcast(F32), ALU.subtract).then_inc(tl_ok, 1)

            def split(it, s):
                for n, (l, r, h) in enumerate(((l1, raw1, h1), (l2, raw2, h2), (l3, raw3, h3))):
                    dve.wait_ge(*done(hi_ok, it, 3 * s + n))
                    nv.tensor_tensor(l[:, s, :], r[:, s, :], h[:, s, :].bitcast(F32), ALU.subtract).then_inc(lo_ok.sem, 1)

            def bias(it, s):
                dve.wait_ge(*done(raw_in[s], it, 47))
                row = raw2[HI:HI + 1, s, TILES * 128:W1]
                nv.tensor_scalar(row, row, 1.0, None, ALU.add).then_inc(bias_ok.sem, 1)

            bias(0, 0)
            split(0, 0)

            def body(it, last):
                for k in range(UNITS):
                    s, c, m = unit(k)
                    if m == 0 and c == 0:
                        dve.wait_ge(*done(wbc_in[s], it, 63))
                    dve.wait_ge(*done(sig_ok, it, k))
                    nv.scalar_tensor_tensor(out=sw[:, k % 2, :], in0=sg[:, k % 2, :], scalar=SIG_LIMIT,
                                            in1=wbc[:, s, m, c * GN:(c + 1) * GN], op0=ALU.min, op1=ALU.mult
                                            ).then_inc(sw_ok.sem, 1)
                    dve.wait_ge(*done(l_ps, it, k))
                    dve.wait_ge(*done(f_ok, it, k - 2))
                    nv.tensor_scalar(bb[:, k % 2, :], lp[k % 2][:, 0:GN], LIMIT + 1.0, 1.0 - LIMIT, ALU.min, ALU.max
                                     ).then_inc(b_ok.sem, 1)
                    dve.wait_ge(*done(sw_ok, it, k))
                    nv.scalar_tensor_tensor(out=aa[:, k % 2, :], in0=gp[k % 2][:, 0:GN], scalar=LIMIT,
                                            in1=sw[:, k % 2, :], op0=ALU.min, op1=ALU.mult).then_inc(a_ok.sem, 1)
                    if k == 1:
                        bias(it, 1)
                    if k == 7 and not last:
                        bias(it + 1, 0)
                    if k == 3:
                        split(it, 1)
                    if k == 9 and not last:
                        split(it + 1, 0)

            steps(dve, body)
            dve.wait_ge(*done(y_ps, LOOPS - 1, UNITS - 1))
            for q in range(HB // 2):
                h = S.H[0:N, half * HB + 2 * q:half * HB + 2 * q + 2, :]
                nv.tensor_tensor(h, acc[q][0:N, 0:2 * D].rearrange("p (g n) -> p g n", g=2), h, ALU.add).then_inc(h_done, 1)

        @block.gpsimd
        def _(pool):
            credit(pool, f_ok, l_ok)

            def product(it, k):
                pool.wait_ge(*done(a_ok, it, k))
                pool.wait_ge(*done(h_ok, it, k - 2))
                pool.wait_ge(*done(l_ok, it, k - 2))
                nc.gpsimd.tensor_tensor(act_f[:, k % 2, :], aa[:, k % 2, :], bb[:, k % 2, :], ALU.mult).then_inc(f_ok.sem, 1)

            product(0, 0)

            def body(it, last):
                for k in range(UNITS):
                    if k + 1 < UNITS or not last:
                        product(it, k + 1)
                    pool.wait_ge(*done(h_ok, it, k))
                    nc.gpsimd.tensor_tensor(act_l[:, k % 3, :], act_f[:, k % 2, :], act_h[:, k % 3, :].bitcast(F32),
                                            ALU.subtract).then_inc(l_ok.sem, 1)

            steps(pool, body)


def attn1_phase(nc, dram, S):
    HEADS, HD, GROUPS = 8, D // 8, 2
    GD = D // GROUPS
    SCALE = float(HD) ** -0.5
    UNITS = [0, "g0", 1, 2, 3, 4, "g1", 5, 6, 7]
    NU = len(UNITS)
    GROUP_LINEAR, NEXT_NORM = 4, 5
    with ExitStack() as ctx:
        def sb(name, shape, dt=F32):
            return ctx.enter_context(nc.sbuf_tensor("a1_" + name, shape, dt))

        def sem(name, per):
            return counted(nc, ctx, "a1_" + name, per)

        w = W1
        xn = sb("xn", [N, G, D])
        stats, mv, veps, rstd = sb("stats", [N, G, 6]), sb("mv", [N, G, 2]), sb("veps", [N, G]), sb("rstd", [N, G])
        xa, xb, cur = sb("xa", [GD, G, N]), sb("xb", [GD, G, N]), sb("cur", [GD, G, N])
        q, k = sb("q", [128, 2, GN]), sb("k", [128, 2, GN])
        v = S.a1_v
        gq, gk, gv = sb("gq", [GD, GN]), sb("gk", [GD, GN]), sb("gv", [N, G, GD])
        p, pT, mx = sb("p", [N, 2, G, N]), sb("pT", [N, 2, G, N]), sb("mx", [N, 2, G])
        rs, ri = sb("rs", [N, G]), sb("ri", [N, G])
        hx = sb("hx", [GD, GROUPS, GN])
        den, o = sb("den", [N, G, HEADS]), sb("o", [N, G, D])
        out0, out1 = sb("out0", [GD, GN]), S.a1_out1
        bank = [ctx.enter_context(nc.psum_tensor(f"a1_ps{i}", [128, 512], F32)) for i in range(8)]
        A, V, SC, PT, O = bank[0:1], bank[1:3], bank[3:5], bank[5], bank[6:8]

        stat_ok, mean_ok, veps_ok, rstd_ok, xn_ok = sem("stat_ok", 4), sem("mean_ok", 4), sem("veps_ok", 1), sem("rstd_ok", 1), sem("xn_ok", 4)
        a_ps, a_out = sem("a_ps", 5), sem("a_out", 5)
        v_ps, v_out = sem("v_ps", 11), sem("v_out", 11)
        z_ps, z_out = sem("z_ps", 4), sem("z_out", 4)
        sc_ps, mx_ok, sub_ok, exp_ok = sem("sc_ps", NU), sem("mx_ok", NU), sem("sub_ok", NU), sem("exp_ok", NU)
        sum_ok, rec_ok, nrm_ok = sem("sum_ok", 2), sem("rec_ok", 2), sem("nrm_ok", 2)
        pt_ps, pt_out, pv_ps = sem("pt_ps", NU), sem("pt_out", NU), sem("pv_ps", HEADS)
        den_ok, o_ok = sem("den_ok", 2), sem("o_ok", 2)
        block = ctx.enter_context(nc.Block())
        A_X, A_Q, A_K, A_GQ0, A_GQ1 = range(5)
        V_X, V_Q, V_K, V_GK0, V_V, _, V_GV0, V_HX0, V_GK1, V_GV1, V_HX1 = range(11)
        Z_O, _, Z_H, _ = range(4)

        def rows(it):
            return S.H[0:N, :, :].rearrange("p b d -> p (b d)")[:, bass.ds(it * (G * D), G * D)].rearrange(
                "p (b d) -> p b d", b=G)

        def steps(eng, first, body):
            first()
            with eng.Fori(0, STEPS - 1) as it:
                body(it, False)
            body(STEPS - 1, True)

        def images(ap):
            return ap.rearrange("p (g n) -> p g n", g=G)

        @block.sync
        def _(sp):
            for t, src in S.late_loads:
                sp.dma_start(t, src).then_inc(S.late_in, 16)
            sp.wait_ge(S.late_in, 16 * len(S.late_loads))

        @block.tensor
        def _(pe):
            credit(pe, a_ps, v_ps, z_ps, sc_ps, pt_ps, pv_ps)
            mm = nc.tensor.matmul

            def fill(tiles, out, it, n):
                pe.wait_ge(*done(out, it, before(n, len(tiles), out.per)))
                return tiles[n % len(tiles)]

            def linear(o, wcol, cols, xs):
                for i, x in enumerate(xs):
                    m = mm(o, S.w1w[0:GD, i, wcol:wcol + cols], x, start=(i == 0), stop=(i == len(xs) - 1))
                return m

            def group_linear(it, i, x, nq, nk, nv):
                for tiles, ps, out, n, c in ((A, a_ps, a_out, nq, 0), (V, v_ps, v_out, nk, GD)):
                    o = fill(tiles, out, it, n)
                    mm(o[0:GD, 0:GN], S.w1g[0:GD, i, c:c + GD], x[:], start=True, stop=True).then_inc(ps.sem, 1)
                o = fill(V, v_out, it, nv)
                for j in range(G):
                    m = mm(o[0:N, j * GD:(j + 1) * GD], x[:, j, :], S.w1g[0:GD, i, 2 * GD:3 * GD], start=True, stop=True)
                m.then_inc(v_ps.sem, 1)

            def pre(it):
                for tiles, ps, out, n, c in ((A, a_ps, a_out, A_X, 0), (V, v_ps, v_out, V_X, GD)):
                    o = fill(tiles, out, it, n)
                    for j in range(G):
                        if c == 0:
                            pe.wait_ge(*done(xn_ok, it, j))
                        m = nc.tensor.transpose(o[0:GD, j * N:(j + 1) * N], xn[:, j, c:c + GD], S.ident[0:N, 0:N])
                    m.then_inc(ps.sem, 1)
                pe.wait_ge(*done(a_out, it, A_X))
                pe.wait_ge(*done(v_out, it, V_X))
                x = (xa[:], xb[:])
                for n, col in ((0, w.q), (1, w.k)):
                    for t, (tiles, ps, out, nn) in enumerate(((A, a_ps, a_out, A_Q + n), (V, v_ps, v_out, V_Q + n))):
                        linear(fill(tiles, out, it, nn)[:, 0:GN], col + 128 * t, 128, x).then_inc(ps.sem, 1)
                o = fill(A, a_out, it, A_GQ0)
                mm(o[0:GD, 0:GN], S.w1g[0:GD, 0, 0:GD], xa[:], start=True, stop=True).then_inc(a_ps.sem, 1)
                o = fill(V, v_out, it, V_GK0)
                mm(o[0:GD, 0:GN], S.w1g[0:GD, 0, GD:2 * GD], xa[:], start=True, stop=True).then_inc(v_ps.sem, 1)
                for h in range(2):
                    o = fill(V, v_out, it, V_V + h)
                    for j in (2 * h, 2 * h + 1):
                        c = (j % 2) * D
                        mm(o[0:N, c:c + D], xa[:, j, :], S.w1w[0:GD, 0, w.v:w.v + D], start=True, stop=False)
                        m = mm(o[0:N, c:c + D], xb[:, j, :], S.w1w[0:GD, 1, w.v:w.v + D], start=False, stop=True)
                    m.then_inc(v_ps.sem, 1)
                o = fill(V, v_out, it, V_GV0)
                for j in range(G):
                    m = mm(o[0:N, j * GD:(j + 1) * GD], xa[:, j, :], S.w1g[0:GD, 0, 2 * GD:3 * GD], start=True, stop=True)
                m.then_inc(v_ps.sem, 1)

            def scores(it, n):
                u = UNITS[n]
                pe.wait_ge(*done(sub_ok, it, n - 2))
                if n < 2:
                    pe.wait_ge(*done(z_out, it, n - 2))
                o = SC[n % 2]
                if u in ("g0", "g1"):
                    g0 = u == "g0"
                    pe.wait_ge(*done(a_out, it, A_GQ0 if g0 else A_GQ1))
                    pe.wait_ge(*done(v_out, it, V_GK0 if g0 else V_GK1))
                    for j in range(G):
                        c = slice(j * N, (j + 1) * N)
                        m = mm(o[0:N, c], gq[:, c], gk[:, c], start=True, stop=True)
                else:
                    t, r = u // 4, 32 * (u % 4)
                    if t == 0:
                        pe.wait_ge(*done(a_out, it, A_K))
                    else:
                        pe.wait_ge(*done(v_out, it, V_K))
                    for j in range(G):
                        c = slice(j * N, (j + 1) * N)
                        m = mm(o[0:N, c], q[r:r + HD, t, c], k[r:r + HD, t, c], start=True, stop=True,
                               tile_position=(r, 0))
                m.then_inc(sc_ps.sem, 1)

            def turn(it, n):
                u = UNITS[n]
                if u in ("g0", "g1"):
                    pe.wait_ge(*done(nrm_ok, it, int(u == "g1")))
                else:
                    pe.wait_ge(*done(exp_ok, it, n))
                pe.wait_ge(*done(pt_out, it, n - 1))
                for j in range(G):
                    m = nc.tensor.transpose(PT[0:N, j * N:(j + 1) * N], p[:, n % 2, j, :], S.ident[0:N, 0:N])
                m.then_inc(pt_ps.sem, 1)

            def values(it, n):
                u = UNITS[n]
                pe.wait_ge(*done(pt_out, it, n))
                if u in ("g0", "g1"):
                    nn = V_HX0 if u == "g0" else V_HX1
                    pe.wait_ge(*done(v_out, it, V_GV0 if u == "g0" else V_GV1))
                    o = fill(V, v_out, it, nn)
                    for j in range(G):
                        m = mm(o[0:GD, j * N:(j + 1) * N], gv[:, j, :], pT[:, n % 2, j, :], start=True, stop=True)
                    m.then_inc(v_ps.sem, 1)
                    return
                if u == 0:
                    pe.wait_ge(*done(o_ok, it, -1))
                    pe.wait_ge(*done(v_out, it, V_V + 1))
                for j in range(G):
                    c = (j % 2) * HEADS * (HD + 1) + u * (HD + 1)
                    m = mm(O[j // 2][0:N, c:c + HD + 1], pT[:, n % 2, j, :], v[:, j, u, :], start=True, stop=True)
                m.then_inc(pv_ps.sem, 1)

            def tail(it):
                pe.wait_ge(*done(o_ok, it, 1))
                for i in range(GROUPS):
                    pe.wait_ge(*done(sub_ok, it, NU - 1))
                    for j in range(G):
                        m = nc.tensor.transpose(SC[i][0:GD, j * N:(j + 1) * N], o[:, j, i * GD:(i + 1) * GD], S.ident[0:N, 0:N])
                    m.then_inc(z_ps.sem, 1)
                pe.wait_ge(*done(z_out, it, Z_O + 1))
                for h in range(2):
                    for j in (2 * h, 2 * h + 1):
                        c, t = (j % 2) * D, slice(j * N, (j + 1) * N)
                        mm(SC[h][0:N, c:c + D], out0[:, t], S.w1w[0:GD, 0, w.o:w.o + D], start=True, stop=False)
                        m = mm(SC[h][0:N, c:c + D], out1[:, t], S.w1w[:, 1, w.o:w.o + D], start=False, stop=True)
                    m.then_inc(z_ps.sem, 1)

            def body(it, last):
                for n in range(NU + 2):
                    if n < NU:
                        scores(it, n)
                    if 0 <= n - 1 < NU:
                        turn(it, n - 1)
                    if n - 2 >= 0:
                        values(it, n - 2)
                    if n == GROUP_LINEAR:
                        pe.wait_ge(*done(v_out, it, V_HX0))
                        group_linear(it, 1, cur, A_GQ1, V_GK1, V_GV1)
                if not last:
                    pre(it + 1)
                tail(it)

            steps(pe, lambda: pre(0), body)

        @block.scalar
        def _(act):
            credit(act, a_out, exp_ok, pt_out)
            cp = nc.scalar.activation

            def evac(it, n, out, rows_):
                act.wait_ge(*done(a_ps, it, n))
                cp(out, A[n % len(A)][0:rows_, 0:GN], ACT.Copy).then_inc(a_out.sem, 1)

            def pre(it):
                evac(it, A_X, xa[:], GD)
                evac(it, A_Q, q[:, 0, :], 128)
                evac(it, A_K, k[:, 0, :], 128)
                evac(it, A_GQ0, gq[:], GD)

            def body(it, last):
                for n in range(NU + 1):
                    if n < NU:
                        act.wait_ge(*done(sub_ok, it, n))
                        cp(p[:, n % 2, :, :], p[:, n % 2, :, :], ACT.Exp, scale=SCALE).then_inc(exp_ok.sem, 1)
                    if n - 1 >= 0:
                        act.wait_ge(*done(pt_ps, it, n - 1))
                        cp(pT[:, (n - 1) % 2, :, :], PT[0:N, 0:GN], ACT.Copy).then_inc(pt_out.sem, 1)
                    if n == GROUP_LINEAR + 1:
                        evac(it, A_GQ1, gq[:], GD)
                if not last:
                    pre(it + 1)

            steps(act, lambda: pre(0), body)

        @block.gpsimd
        def _(pool):
            credit(pool, veps_ok, rstd_ok)

            def pre(it):
                pool.wait_ge(*done(mean_ok, it, 3))
                settle(pool, S)
                nc.gpsimd.tensor_scalar(veps[:], mv[:, :, 1], 1.0, EPS, ALU.mult, ALU.add).then_inc(veps_ok.sem, 1)
                pool.wait_ge(*done(veps_ok, it, 0))
                nc.gpsimd.tensor_tensor(rstd[:], veps[:], S.mhalf[0:N, 0:G], ALU.pow).then_inc(rstd_ok.sem, 1)

            def body(it, last):
                if not last:
                    pre(it + 1)

            for n, t in enumerate(S.late_ones):
                if n:
                    pool.wait_ge(S.late_ones_ok, n)
                nc.gpsimd.memset(t, 1.0).then_inc(S.late_ones_ok, 1)
            steps(pool, lambda: pre(0), body)

        @block.vector
        def _(dve):
            credit(dve, stat_ok, mean_ok, xn_ok, v_out, z_out, mx_ok, sub_ok, sum_ok, rec_ok, nrm_ok, den_ok, o_ok)
            nv = nc.vector

            def stat(it):
                hg = rows(it)
                settle(dve, S)
                for j in range(G):
                    nv.bn_stats(stats[:, j, :], hg[:, j, :]).then_inc(stat_ok.sem, 1)
                dve.wait_ge(*done(stat_ok, it, 3))
                settle(dve, S)
                for j in range(G):
                    nv.bn_aggr(mv[:, j, :], stats[:, j, :]).then_inc(mean_ok.sem, 1)

            def norm(it):
                hg = rows(it)
                dve.wait_ge(*done(mean_ok, it, 3))
                dve.wait_ge(*done(rstd_ok, it, 0))
                dve.wait_ge(*done(v_ps, it, V_X - v_ps.per))
                for j in range(G):
                    nv.tensor_scalar(xn[:, j, :], hg[:, j, :], mv[:, j, 0:1], rstd[:, j:j + 1],
                                     ALU.subtract, ALU.mult).then_inc(xn_ok.sem, 1)

            def evac(it, n, out, rows_, wd, shape=None):
                dve.wait_ge(*done(v_ps, it, n))
                i = V[n % len(V)][0:rows_, 0:wd]
                nv.tensor_copy(out, i.rearrange(*shape[0:1], **shape[1]) if shape else i).then_inc(v_out.sem, 1)

            per_image = ("p (g n) -> p g n", {"g": G})

            def pre(it):
                evac(it, V_X, xb[:], GD, GN, per_image)
                evac(it, V_Q, q[:, 1, :], 128, GN)
                evac(it, V_K, k[:, 1, :], 128, GN)
                evac(it, V_GK0, gk[:], GD, GN)
                for h in range(2):
                    evac(it, V_V + h, v[:, 2 * h:2 * h + 2, :, 0:HD], N, 2 * D, ("p (g h d) -> p g h d", {"g": 2, "h": HEADS}))
                evac(it, V_GV0, gv[:], N, G * GD, per_image)

            def softmax_in(it, n):
                sc = images(SC[n % 2][0:N, 0:GN])
                dve.wait_ge(*done(sc_ps, it, n))
                nv.tensor_reduce(mx[:, n % 2, :], sc, AX.X, ALU.max).then_inc(mx_ok.sem, 1)
                dve.wait_ge(*done(mx_ok, it, n))
                dve.wait_ge(*done(pt_ps, it, n - 2))
                nv.tensor_tensor(p[:, n % 2, :, :], sc, bc(mx[:, n % 2, :].unsqueeze(2), [N, G, N]), ALU.subtract
                                 ).then_inc(sub_ok.sem, 1)

            def normalise(it, n, i):
                pp = p[:, n % 2, :, :]
                dve.wait_ge(*done(exp_ok, it, n))
                nv.tensor_reduce(rs[:], pp, AX.X, ALU.add).then_inc(sum_ok.sem, 1)
                dve.wait_ge(*done(sum_ok, it, i))
                nv.reciprocal(ri[:], rs[:]).then_inc(rec_ok.sem, 1)
                dve.wait_ge(*done(rec_ok, it, i))
                nv.tensor_tensor(pp, pp, bc(ri[:].unsqueeze(2), [N, G, N]), ALU.mult).then_inc(nrm_ok.sem, 1)

            def first():
                stat(0)
                norm(0)
                pre(0)

            def body(it, last):
                hg = rows(it)
                for n in range(NU + 2):
                    if n < NU:
                        softmax_in(it, n)
                        if UNITS[n] in ("g0", "g1"):
                            normalise(it, n, int(UNITS[n] == "g1"))
                    if n == 3:
                        dve.wait_ge(*done(v_ps, it, V_HX0))
                        hx0 = V[V_HX0 % len(V)][0:GD, 0:GN]
                        nv.tensor_tensor(cur[:], images(hx0), xb[:], ALU.add)
                        nv.tensor_copy(hx[:, 0, :], hx0).then_inc(v_out.sem, 1)
                    if n == GROUP_LINEAR + 1:
                        evac(it, V_GK1, gk[:], GD, GN)
                        evac(it, V_GV1, gv[:], N, G * GD, per_image)
                    if n == NEXT_NORM and not last:
                        stat(it + 1)
                    if n == NEXT_NORM + 2 and not last:
                        norm(it + 1)
                    if n == 8:
                        evac(it, V_HX1, hx[:, 1, :], GD, GN)
                dve.wait_ge(*done(pv_ps, it, HEADS - 1))
                for h in range(2):
                    oo = O[h][0:N, 0:2 * HEADS * (HD + 1)].rearrange("p (g h d) -> p g h d", g=2, h=HEADS)
                    nv.reciprocal(den[:, 2 * h:2 * h + 2, :], oo[:, :, :, HD]).then_inc(den_ok.sem, 1)
                for h in range(2):
                    oo = O[h][0:N, 0:2 * HEADS * (HD + 1)].rearrange("p (g h d) -> p g h d", g=2, h=HEADS)
                    dve.wait_ge(*done(den_ok, it, h))
                    if h == 0:
                        dve.wait_ge(*done(z_ps, it, Z_O + 1 - z_ps.per))
                    nv.tensor_tensor(o[:, 2 * h:2 * h + 2, :].rearrange("p g (h d) -> p g h d", h=HEADS), oo[:, :, :, 0:HD],
                                     bc(den[:, 2 * h:2 * h + 2, :].unsqueeze(3), [N, 2, HEADS, HD]), ALU.mult
                                     ).then_inc(o_ok.sem, 1)
                if not last:
                    pre(it + 1)
                for i, out in enumerate((out0[:], out1[0:GD, :])):
                    dve.wait_ge(*done(z_ps, it, Z_O + i))
                    nv.tensor_tensor(out, SC[i][0:GD, 0:GN], hx[:, i, :], ALU.add).then_inc(z_out.sem, 1)
                for h in range(2):
                    dve.wait_ge(*done(z_ps, it, Z_H + h))
                    hh = hg[:, 2 * h:2 * h + 2, :]
                    nv.tensor_tensor(hh, SC[h][0:N, 0:2 * D].rearrange("p (g n) -> p g n", g=2), hh, ALU.add
                                     ).then_inc(z_out.sem, 1)

            steps(dve, first, body)


def ffn1_phase(nc, dram, S):
    HEADS, HD, MLP, RHD = 12, D // 12, 768, 128
    NU, KF = HEADS, MLP // 128
    NEXT_NORM = 2
    with ExitStack() as ctx:
        def sb(name, shape, dt=F32):
            return ctx.enter_context(nc.sbuf_tensor("f_" + name, shape, dt))

        def sem(name, per):
            return counted(nc, ctx, "f_" + name, per)

        w, c = W4, C4
        stats, mv, veps, rstd = sb("stats", [N, 3, G, 6]), sb("mv", [N, 3, G, 2]), sb("veps", [N, 3, G]), sb("rstd", [N, 3, G])
        xnext, x, z, hh, y = (sb(n, [N, G, D]) for n in ("xnext", "x", "z", "hh", "y"))
        xa1, xa2, r1, r2 = sb("xa1", [LO, G, N]), S.f_xa2, sb("r1", [LO, GN]), sb("r2", [HI, GN])
        e, gm, gs = sb("e", [RHD, G, N]), sb("gm", [RHD, G]), sb("gs", [RHD, G])
        h1, h2 = sb("h1", [RHD, GN]), S.f_h2
        logit, bits, nbits, sel = sb("logit", [N, G, 4]), sb("bits", [N, G, 2]), sb("nbits", [N, G, 2]), sb("sel", [N, G, 3])
        q, k, v = sb("q", [128, 3, GN]), sb("k", [128, 3, GN]), S.f_v
        p, pT, mx = sb("p", [N, 2, G, N]), sb("pT", [N, 2, G, N]), sb("mx", [N, 2, G])
        den, o = sb("den", [N, G, HEADS]), sb("o", [N, G, D])
        o1, o2 = sb("o1", [LO, GN]), S.f_o2
        xf1, xf2, ff = sb("xf1", [LO, GN]), sb("xf2", [HI, GN]), sb("ff", [128, KF, GN])
        u1, u2, dn, d1, d2 = sb("u1", [LO, GN]), sb("u2", [HI, GN]), sb("dn", [N, G, 3, D // 3]), sb("d1", [LO, GN]), sb("d2", [HI, GN])
        bank = [ctx.enter_context(nc.psum_tensor(f"f_ps{i}", [128, 512], F32)) for i in range(8)]
        A, V, SC, PT, O = bank[0:1], bank[1:3], bank[3:5], bank[5], bank[6:8]
        ZA, ZV = (SC[0], PT, O[0]), (SC[1], O[1])

        stat_ok, mean_ok = [sem(f"stat_ok{i}", 4) for i in range(3)], [sem(f"mean_ok{i}", 4) for i in range(3)]
        veps_ok, rstd_ok = [sem(f"veps_ok{i}", 1) for i in range(3)], [sem(f"rstd_ok{i}", 1) for i in range(3)]
        x_ok, z_ok, y_ok, xcopy_ok, hx_ok = sem("x_ok", 4), sem("z_ok", 4), sem("y_ok", 4), sem("xcopy_ok", 1), sem("hx_ok", 1)
        a_ps, a_out, v_ps, v_out = sem("a_ps", 7), sem("a_out", 7), sem("v_ps", 7), sem("v_out", 7)
        za_ps, za_out, zv_ps, zv_out = sem("za_ps", 10), sem("za_out", 10), sem("zv_ps", 12), sem("zv_out", 12)
        gm_ok, gs_ok, bit_ok, nb_ok, sel_ok = sem("gm_ok", 1), sem("gs_ok", 1), sem("bit_ok", 2), sem("nb_ok", 1), sem("sel_ok", 3)
        sc_ps, mx_ok, sub_ok, exp_ok = sem("sc_ps", NU), sem("mx_ok", NU), sem("sub_ok", NU), sem("exp_ok", NU)
        pt_ps, pt_out, pv_ps = sem("pt_ps", NU), sem("pt_out", NU), sem("pv_ps", NU)
        den_ok, o_ok = sem("den_ok", 2), sem("o_ok", 2)
        hh_ok, out_ok = sem("hh_ok", 4), sem("out_ok", 4)
        stored = sem("stored", 16)
        block = ctx.enter_context(nc.Block())
        A_Z, A_Q0, A_Q2, A_K1, A_R, A_H1, A_H2 = range(7)
        V_Z, V_Q1, V_K0, V_K2, V_V, _, V_L = range(7)
        ZA_O, ZA_Y, ZA_F, ZA_U, ZA_D = 0, 1, 2, 8, 9
        ZV_O, ZV_WO, ZV_Y, ZV_F, ZV_U, ZV_DN, ZV_D, ZV_UP = 0, 1, 3, 4, 6, 7, 9, 10

        def rows(it):
            return S.H[0:N, :, :].rearrange("p b d -> p (b d)")[:, bass.ds(it * (G * D), G * D)].rearrange(
                "p (b d) -> p b d", b=G)

        def steps(eng, first, body):
            first()
            with eng.Fori(0, STEPS - 1) as it:
                body(it, False)
            body(STEPS - 1, True)

        def images(ap, g=G):
            return ap.rearrange("p (g n) -> p g n", g=g)

        @block.sync
        def _(sp):
            credit(sp, stored)

            def body(it, last):
                sp.wait_ge(*done(zv_out, it, ZV_UP + 1))
                settle(sp, S)
                sp.dma_start(dram.out[bass.ds(it * G, G), :, :].rearrange("b t d -> t b d"), rows(it)).then_inc(stored.sem, 16)

            steps(sp, lambda: None, body)
            sp.wait_ge(*done(stored, STEPS - 1, 15))

        @block.tensor
        def _(pe):
            credit(pe, a_ps, v_ps, za_ps, zv_ps, sc_ps, pt_ps, pv_ps)
            mm = nc.tensor.matmul

            def fill(tiles, out, it, n, ready=-100):
                pe.wait_ge(*done(out, it, max(before(n, len(tiles), out.per), ready)))
                return tiles[n % len(tiles)]

            def linear(o, lo, hi, xs):
                mm(o, lo, xs[0], start=True, stop=False)
                return mm(o, hi, xs[1], start=False, stop=True)

            def cols(col, n):
                return S.w4a[:, col:col + n], S.w4b[0:HI, col:col + n]

            def transposed(o, src, c0, c1, ok, it):
                if ok is None:
                    settle(pe, S)
                for j in range(G):
                    if ok is not None:
                        pe.wait_ge(*done(ok, it, j))
                    m = nc.tensor.transpose(o[0:c1 - c0, j * N:(j + 1) * N], src[:, j, c0:c1], S.ident[0:N, 0:N])
                return m

            def by_image(o, h, lo, hi, col, hi_rows):
                for j in (2 * h, 2 * h + 1):
                    t = slice(j * N, (j + 1) * N)
                    m = linear(o[0:N, (j % 2) * D:(j % 2 + 1) * D], lo[:, t], hi[:, t],
                               (S.w4a[:, col:col + D], S.w4b[0:hi_rows, col:col + D]))
                return m

            def pre1(it):
                transposed(fill(A, a_out, it, A_Z), z, 0, LO, z_ok, it).then_inc(a_ps.sem, 1)
                transposed(fill(V, v_out, it, V_Z), z, LO, D, None, it).then_inc(v_ps.sem, 1)
                pe.wait_ge(*done(a_out, it, A_Z))
                pe.wait_ge(*done(v_out, it, V_Z))
                xs = (xa1[:], xa2[0:HI, :])
                for n, a, col in ((A_Q0, True, w.q), (V_Q1, False, w.q + 128), (A_Q2, True, w.q + 256),
                                  (V_K0, False, w.k), (A_K1, True, w.k + 128), (V_K2, False, w.k + 256)):
                    o_ = fill(A, a_out, it, n) if a else fill(V, v_out, it, n)
                    linear(o_[:, 0:GN], *cols(col, 128), xs).then_inc((a_ps if a else v_ps).sem, 1)

            def pre2(it):
                linear(fill(A, a_out, it, A_R)[:, 0:GN], *cols(w.r, RHD), (r1[:], r2[:])).then_inc(a_ps.sem, 1)
                xaf = (xa1[:].rearrange("p g n -> p (g n)"), xa2[:])
                for h in range(2):
                    by_image(fill(V, v_out, it, V_V + h), h, *xaf, w.v, HI + 1).then_inc(v_ps.sem, 1)

            def pre3(it):
                pe.wait_ge(*done(a_out, it, A_R))
                pe.wait_ge(*done(gs_ok, it, 0))
                o_ = fill(A, a_out, it, A_H1)[:, 0:GN]
                mm(o_, S.ro1[:, 0, :], e[:], start=True, stop=False)
                mm(images(o_), S.ro1[:, 1, :], bc(gs[:].unsqueeze(2), [RHD, G, N]), start=False, stop=True).then_inc(a_ps.sem, 1)

            def pre4(it):
                pe.wait_ge(*done(a_out, it, A_H1))
                o_ = fill(A, a_out, it, A_H2)[0:RHD // 2, 0:GN]
                mm(o_, S.ro2[:], h1[:], start=True, stop=True).then_inc(a_ps.sem, 1)

            def logits(it):
                pe.wait_ge(*done(a_out, it, A_H2))
                o_ = fill(V, v_out, it, V_L)
                for j in range(G):
                    m = mm(o_[0:N, 4 * j:4 * j + 4], h2[:, j * N:(j + 1) * N], S.ro3[:], start=True, stop=True)
                m.then_inc(v_ps.sem, 1)

            def scores(it, n):
                pe.wait_ge(*done(sub_ok, it, n - 2))
                if n == 0:
                    pe.wait_ge(*done(za_out, it, -1))
                    pe.wait_ge(*done(zv_out, it, -1))
                    pe.wait_ge(*done(a_out, it, A_K1))
                    pe.wait_ge(*done(v_out, it, V_K2))
                t, r = n // 4, 32 * (n % 4)
                for j in range(G):
                    s = slice(j * N, (j + 1) * N)
                    m = mm(SC[n % 2][0:N, s], q[r:r + HD, t, s], k[r:r + HD, t, s], start=True, stop=True, tile_position=(r, 0))
                m.then_inc(sc_ps.sem, 1)

            def turn(it, n):
                pe.wait_ge(*done(exp_ok, it, n))
                pe.wait_ge(*done(pt_out, it, n - 1))
                for j in range(G):
                    m = nc.tensor.transpose(PT[0:N, j * N:(j + 1) * N], p[:, n % 2, j, :], S.ident[0:N, 0:N])
                m.then_inc(pt_ps.sem, 1)

            def values(it, n):
                pe.wait_ge(*done(pt_out, it, n))
                if n == 0:
                    pe.wait_ge(*done(v_out, it, V_V + 1))
                for j in range(G):
                    cc = (j % 2) * HEADS * (HD + 1) + n * (HD + 1)
                    m = mm(O[j // 2][0:N, cc:cc + HD + 1], pT[:, n % 2, j, :], v[:, j, n, :], start=True, stop=True)
                m.then_inc(pv_ps.sem, 1)

            def tail_heads(it):
                pe.wait_ge(*done(sub_ok, it, NU - 1))
                pe.wait_ge(*done(o_ok, it, 1))
                transposed(fill(ZA, za_out, it, ZA_O), o, 0, LO, None, it).then_inc(za_ps.sem, 1)
                transposed(fill(ZV, zv_out, it, ZV_O), o, LO, D, None, it).then_inc(zv_ps.sem, 1)

            def tail_wo(it):
                pe.wait_ge(*done(za_out, it, ZA_O))
                for h in range(2):
                    by_image(fill(ZV, zv_out, it, ZV_WO + h, ZV_O), h, o1[:], o2[:], w.o, HI + 1).then_inc(zv_ps.sem, 1)

            def tail_mlp(it):
                transposed(fill(ZA, za_out, it, ZA_Y), y, 0, LO, y_ok, it).then_inc(za_ps.sem, 1)
                transposed(fill(ZV, zv_out, it, ZV_Y), y, LO, D, None, it).then_inc(zv_ps.sem, 1)
                pe.wait_ge(*done(zv_out, it, ZV_Y))
                for f in range(KF):
                    linear(fill(ZA, za_out, it, ZA_F + f, ZA_Y)[:, 0:GN], *cols(w.f + 128 * f, 128), (xf1[:], xf2[:])).then_inc(za_ps.sem, 1)
                for h in range(2):
                    o_ = fill(ZV, zv_out, it, ZV_F + h)
                    for j in (2 * h, 2 * h + 1):
                        oo = o_[0:N, (j % 2) * D:(j % 2 + 1) * D]
                        mm(oo, S.ones1[:], S.fc2b[:], start=True, stop=False)
                        for f in range(KF):
                            if h == 0 and j == 0:
                                pe.wait_ge(*done(za_out, it, ZA_F + f))
                            m = mm(oo, ff[:, f, j * N:(j + 1) * N], S.fc2[:, f, :], start=False, stop=(f == KF - 1))
                    m.then_inc(zv_ps.sem, 1)

            def tail_lra(it):
                transposed(fill(ZA, za_out, it, ZA_U), hh, 0, LO, out_ok, it).then_inc(za_ps.sem, 1)
                transposed(fill(ZV, zv_out, it, ZV_U), hh, LO, D, None, it).then_inc(zv_ps.sem, 1)
                pe.wait_ge(*done(za_out, it, ZA_U))
                for h in range(2):
                    by_image(fill(ZV, zv_out, it, ZV_DN + h, ZV_U), h, u1[:], u2[:], w.dn, HI).then_inc(zv_ps.sem, 1)
                pe.wait_ge(*done(zv_out, it, ZV_DN + 1))
                dd = dn[:].rearrange("p g k r -> p g (k r)")
                transposed(fill(ZA, za_out, it, ZA_D), dd, 0, LO, None, it).then_inc(za_ps.sem, 1)
                transposed(fill(ZV, zv_out, it, ZV_D), dd, LO, D, None, it).then_inc(zv_ps.sem, 1)
                pe.wait_ge(*done(za_out, it, ZA_D))
                for h in range(2):
                    by_image(fill(ZV, zv_out, it, ZV_UP + h, ZV_D), h, d1[:], d2[:], w.up, HI).then_inc(zv_ps.sem, 1)

            def first():
                pre1(0)
                pre2(0)
                pre3(0)
                pre4(0)

            def body(it, last):
                for n in range(NU + 2):
                    if n < NU:
                        scores(it, n)
                    if n == 1:
                        logits(it)
                    if 0 <= n - 1 < NU:
                        turn(it, n - 1)
                    if n - 2 >= 0:
                        values(it, n - 2)
                if not last:
                    pre1(it + 1)
                tail_heads(it)
                if not last:
                    pre2(it + 1)
                tail_wo(it)
                if not last:
                    pre3(it + 1)
                    pre4(it + 1)
                tail_mlp(it)
                tail_lra(it)

            steps(pe, first, body)

        @block.scalar
        def _(act):
            credit(act, a_out, za_out, exp_ok, pt_out)
            cp = nc.scalar.activation

            def one(it, n, out, rows_, func, **kw):
                act.wait_ge(*done(a_ps, it, n))
                cp(out, A[n % len(A)][0:rows_, 0:GN], func, **kw).then_inc(a_out.sem, 1)

            def za(it, n, out, rows_, func=ACT.Copy, **kw):
                act.wait_ge(*done(za_ps, it, n))
                cp(out, ZA[n % len(ZA)][0:rows_, 0:GN], func, **kw).then_inc(za_out.sem, 1)

            def col(i):
                return S.c4a[:, i:i + 1]

            def pre1(it):
                act.wait_ge(*done(a_ps, it, A_Z))
                cp(r1[:], A[0][0:LO, 0:GN], ACT.Identity, scale=col(c.rg), bias=col(c.rb))
                cp(xa1[:], images(A[0][0:LO, 0:GN]), ACT.Identity, scale=col(c.g1), bias=col(c.b1)).then_inc(a_out.sem, 1)
                one(it, A_Q0, q[:, 0, :], 128, ACT.Identity, bias=col(c.q))
                one(it, A_Q2, q[:, 2, :], 128, ACT.Identity, bias=col(c.q + 2))
                one(it, A_K1, k[:, 1, :], 128, ACT.Identity, bias=col(c.k + 1))

            def pre2(it):
                act.wait_ge(*done(a_ps, it, A_R))
                act.wait_ge(*done(gm_ok, it, -1))
                cp(e[:], images(A[0][0:RHD, 0:GN]), ACT.Gelu, bias=col(c.r)).then_inc(a_out.sem, 1)

            def pre3(it):
                one(it, A_H1, h1[:], RHD, ACT.Gelu, bias=col(c.h1))

            def pre4(it):
                act.wait_ge(*done(a_ps, it, A_H2))
                cp(h2[0:RHD // 2, :], A[0][0:RHD // 2, 0:GN], ACT.Gelu, bias=S.c4a[0:RHD // 2, c.h2:c.h2 + 1]).then_inc(a_out.sem, 1)

            def first():
                pre1(0)
                pre2(0)
                pre3(0)
                pre4(0)

            def body(it, last):
                for n in range(NU + 1):
                    if n < NU:
                        act.wait_ge(*done(sub_ok, it, n))
                        cp(p[:, n % 2, :, :], p[:, n % 2, :, :], ACT.Exp, scale=float(HD) ** -0.5).then_inc(exp_ok.sem, 1)
                    if n - 1 >= 0:
                        act.wait_ge(*done(pt_ps, it, n - 1))
                        cp(pT[:, (n - 1) % 2, :, :], PT[0:N, 0:GN], ACT.Copy).then_inc(pt_out.sem, 1)
                if not last:
                    pre1(it + 1)
                za(it, ZA_O, o1[:], LO)
                if not last:
                    pre2(it + 1)
                    pre3(it + 1)
                    pre4(it + 1)
                za(it, ZA_Y, xf1[:], LO, ACT.Identity, scale=col(c.g2), bias=col(c.b2))
                for f in range(KF):
                    za(it, ZA_F + f, ff[:, f, :], 128, ACT.Gelu, bias=col(c.f + f))
                za(it, ZA_U, u1[:], LO)
                za(it, ZA_D, d1[:], LO)

            steps(act, first, body)

        @block.gpsimd
        def _(pool):
            credit(pool, *veps_ok, *rstd_ok, xcopy_ok, hx_ok)

            def power(it, i):
                pool.wait_ge(*done(mean_ok[i], it, 3))
                settle(pool, S)
                nc.gpsimd.tensor_scalar(veps[:, i, :], mv[:, i, :, 1], 1.0, EPS, ALU.mult, ALU.add).then_inc(veps_ok[i].sem, 1)
                pool.wait_ge(*done(veps_ok[i], it, 0))
                nc.gpsimd.tensor_tensor(rstd[:, i, :], veps[:, i, :], S.mhalf[0:N, 0:G], ALU.pow).then_inc(rstd_ok[i].sem, 1)

            def first():
                power(0, 0)
                power(0, 1)
                pool.wait_ge(*done(x_ok, 0, 3))
                nc.gpsimd.tensor_copy(x[:], xnext[:]).then_inc(xcopy_ok.sem, 1)

            def body(it, last):
                if not last:
                    power(it + 1, 0)
                    power(it + 1, 1)
                    pool.wait_ge(*done(hh_ok, it, 3))
                    settle(pool, S)
                    nc.gpsimd.tensor_copy(x[:], xnext[:]).then_inc(xcopy_ok.sem, 1)
                power(it, 2)
                pool.wait_ge(*done(out_ok, it, 3))
                hg = rows(it)
                nc.gpsimd.tensor_tensor(hg, hg, hh[:], ALU.add).then_inc(hx_ok.sem, 1)

            steps(pool, first, body)

        @block.vector
        def _(dve):
            credit(dve, *stat_ok, *mean_ok, x_ok, z_ok, y_ok, v_out, zv_out, gm_ok, gs_ok, bit_ok, nb_ok, sel_ok, mx_ok, sub_ok,
                   den_ok, o_ok, hh_ok, out_ok)
            nv = nc.vector

            def stat(it, i, src):
                settle(dve, S)
                for j in range(G):
                    nv.bn_stats(stats[:, i, j, :], src[:, j, :]).then_inc(stat_ok[i].sem, 1)
                dve.wait_ge(*done(stat_ok[i], it, 3))
                settle(dve, S)
                for j in range(G):
                    nv.bn_aggr(mv[:, i, j, :], stats[:, i, j, :]).then_inc(mean_ok[i].sem, 1)

            def norm(it, i, src, out, ok):
                dve.wait_ge(*done(mean_ok[i], it, 3))
                dve.wait_ge(*done(rstd_ok[i], it, 0))
                for j in range(G):
                    nv.tensor_scalar(out[:, j, :], src[:, j, :], mv[:, i, j, 0:1], rstd[:, i, j:j + 1],
                                     ALU.subtract, ALU.mult).then_inc(ok.sem, 1)

            def one(it, n, out, rows_, b=None):
                dve.wait_ge(*done(v_ps, it, n))
                i = V[n % len(V)][0:rows_, 0:GN]
                nv.tensor_scalar(out, i, b, None, ALU.add).then_inc(v_out.sem, 1)

            def col(i):
                return S.c4a[:, i:i + 1]

            def colb(i):
                return S.c4b[:, i:i + 1]

            def pre1(it):
                dve.wait_ge(*done(v_ps, it, V_Z))
                zz = V[V_Z % len(V)][0:HI, 0:GN]
                nv.tensor_scalar(r2[:], zz, colb(c.rg), colb(c.rb), ALU.mult, ALU.add)
                nv.tensor_scalar(xa2[0:HI, :], zz, colb(c.g1), colb(c.b1), ALU.mult, ALU.add).then_inc(v_out.sem, 1)
                one(it, V_Q1, q[:, 1, :], 128, col(c.q + 1))
                one(it, V_K0, k[:, 0, :], 128, col(c.k))
                one(it, V_K2, k[:, 2, :], 128, col(c.k + 2))

            def pre2(it):
                for h in range(2):
                    dve.wait_ge(*done(v_ps, it, V_V + h))
                    nv.tensor_copy(v[:, 2 * h:2 * h + 2, :, 0:HD], V[(V_V + h) % len(V)][0:N, 0:2 * D].rearrange(
                        "p (g h d) -> p g h d", g=2, h=HEADS)).then_inc(v_out.sem, 1)

            def pre3(it):
                dve.wait_ge(*done(a_out, it, A_R))
                nv.tensor_reduce(gm[:], e[:, :, 1:N], AX.X, ALU.add).then_inc(gm_ok.sem, 1)
                dve.wait_ge(*done(gm_ok, it, 0))
                nv.tensor_scalar(gs[:], gm[:], 1.0 / (N - 1), None, ALU.mult).then_inc(gs_ok.sem, 1)

            def router(it):
                dve.wait_ge(*done(v_ps, it, V_L))
                nv.tensor_copy(logit[:], V[V_L % len(V)][0:N, 0:4 * G].rearrange("p (g n) -> p g n", g=G)).then_inc(v_out.sem, 1)
                dve.wait_ge(*done(v_out, it, V_L))
                pair = logit[:].rearrange("p g (b t) -> p g b t", t=2)
                nv.tensor_tensor(bits[:], pair[:, :, :, 1], pair[:, :, :, 0], ALU.is_gt).then_inc(bit_ok.sem, 1)
                dve.wait_ge(*done(bit_ok, it, 0))
                nv.memset(bits[0:1, :, :], 1.0).then_inc(bit_ok.sem, 1)
                dve.wait_ge(*done(bit_ok, it, 1))
                nv.tensor_scalar(nbits[:], bits[:], -1.0, 1.0, ALU.mult, ALU.add).then_inc(nb_ok.sem, 1)
                dve.wait_ge(*done(nb_ok, it, 0))
                for i, (a_, b_) in enumerate(((nbits, nbits), (nbits, bits), (bits, nbits))):
                    nv.tensor_tensor(sel[:, :, i], a_[:, :, 0], b_[:, :, 1], ALU.mult).then_inc(sel_ok.sem, 1)

            def softmax_in(it, n):
                sc = images(SC[n % 2][0:N, 0:GN])
                dve.wait_ge(*done(sc_ps, it, n))
                nv.tensor_reduce(mx[:, n % 2, :], sc, AX.X, ALU.max).then_inc(mx_ok.sem, 1)
                dve.wait_ge(*done(mx_ok, it, n))
                dve.wait_ge(*done(pt_ps, it, n - 2))
                nv.tensor_tensor(p[:, n % 2, :, :], sc, bc(mx[:, n % 2, :].unsqueeze(2), [N, G, N]), ALU.subtract
                                 ).then_inc(sub_ok.sem, 1)

            def zv(it, n, wd, g):
                dve.wait_ge(*done(zv_ps, it, n))
                t = ZV[n % len(ZV)]
                return t[0:N, 0:wd].rearrange("p (g n) -> p g n", g=g) if g else t[0:HI, 0:wd]

            def first():
                hg = rows(0)
                stat(0, 0, hg)
                norm(0, 0, hg, xnext, x_ok)
                dve.wait_ge(*done(x_ok, 0, 3))
                stat(0, 1, xnext)
                norm(0, 1, xnext, z, z_ok)
                pre1(0)
                pre2(0)
                pre3(0)

            def body(it, last):
                hg = rows(it)
                for n in range(NU):
                    softmax_in(it, n)
                    if n == 1:
                        router(it)
                    if not last:
                        if n == NEXT_NORM:
                            stat(it + 1, 0, rows(it + 1))
                        if n == NEXT_NORM + 2:
                            dve.wait_ge(*done(xcopy_ok, it, 0))
                            norm(it + 1, 0, rows(it + 1), xnext, x_ok)
                            dve.wait_ge(*done(x_ok, it + 1, 3))
                            stat(it + 1, 1, xnext)
                        if n == NEXT_NORM + 4:
                            norm(it + 1, 1, xnext, z, z_ok)
                dve.wait_ge(*done(pv_ps, it, NU - 1))
                for h in range(2):
                    oo = O[h][0:N, 0:2 * HEADS * (HD + 1)].rearrange("p (g h d) -> p g h d", g=2, h=HEADS)
                    nv.reciprocal(den[:, 2 * h:2 * h + 2, :], oo[:, :, :, HD]).then_inc(den_ok.sem, 1)
                for h in range(2):
                    oo = O[h][0:N, 0:2 * HEADS * (HD + 1)].rearrange("p (g h d) -> p g h d", g=2, h=HEADS)
                    dve.wait_ge(*done(den_ok, it, h))
                    nv.tensor_tensor(o[:, 2 * h:2 * h + 2, :].rearrange("p g (h d) -> p g h d", h=HEADS), oo[:, :, :, 0:HD],
                                     bc(den[:, 2 * h:2 * h + 2, :].unsqueeze(3), [N, 2, HEADS, HD]), ALU.mult
                                     ).then_inc(o_ok.sem, 1)
                if not last:
                    pre1(it + 1)
                t = zv(it, ZV_O, GN, 0)
                nv.tensor_copy(o2[0:HI, :], t).then_inc(zv_out.sem, 1)
                if not last:
                    pre2(it + 1)
                dve.wait_ge(*done(xcopy_ok, it, 0))
                for h in range(2):
                    t = zv(it, ZV_WO + h, 2 * D, 2)
                    for j in (2 * h, 2 * h + 1):
                        nv.scalar_tensor_tensor(out=hh[:, j, :], in0=t[:, j % 2, :], scalar=bits[:, j, 0:1], in1=x[:, j, :],
                                                op0=ALU.mult, op1=ALU.add).then_inc(hh_ok.sem, 1)
                    dve.wait_ge(*done(hh_ok, it, 2 * h + 1))
                    dve.sem_inc(zv_out.sem, 1)
                stat(it, 2, hh)
                if not last:
                    pre3(it + 1)
                norm(it, 2, hh, y, y_ok)
                t = zv(it, ZV_Y, GN, 0)
                nv.tensor_scalar(xf2[:], t, colb(c.g2), colb(c.b2), ALU.mult, ALU.add).then_inc(zv_out.sem, 1)
                for h in range(2):
                    t = zv(it, ZV_F + h, 2 * D, 2)
                    for j in (2 * h, 2 * h + 1):
                        nv.scalar_tensor_tensor(out=hh[:, j, :], in0=t[:, j % 2, :], scalar=bits[:, j, 1:2], in1=hh[:, j, :],
                                                op0=ALU.mult, op1=ALU.add).then_inc(out_ok.sem, 1)
                    dve.wait_ge(*done(out_ok, it, 2 * h + 1))
                    dve.sem_inc(zv_out.sem, 1)
                t = zv(it, ZV_U, GN, 0)
                nv.tensor_copy(u2[:], t).then_inc(zv_out.sem, 1)
                for h in range(2):
                    t = zv(it, ZV_DN + h, 2 * D, 2).rearrange("p g (k r) -> p g k r", k=3)
                    nv.tensor_tensor(dn[:, 2 * h:2 * h + 2, :, :], t, bc(sel[:, 2 * h:2 * h + 2, :].unsqueeze(3),
                                     [N, 2, 3, D // 3]), ALU.mult).then_inc(zv_out.sem, 1)
                t = zv(it, ZV_D, GN, 0)
                nv.tensor_copy(d2[:], t).then_inc(zv_out.sem, 1)
                dve.wait_ge(*done(hx_ok, it, 0))
                for h in range(2):
                    t = zv(it, ZV_UP + h, 2 * D, 2)
                    hj = hg[:, 2 * h:2 * h + 2, :]
                    nv.tensor_tensor(hj, t, hj, ALU.add).then_inc(zv_out.sem, 1)

            steps(dve, first, body)


def program(nc, dram):
    with ExitStack() as ctx:
        def sb(name, shape, dt=F32):
            return ctx.enter_context(nc.sbuf_tensor(name, shape, dt))

        S = Names()
        S.H = sb("H", [128, B, D])
        S.ident, S.iota, S.mhalf = sb("ident", [128, 128]), sb("iota", [128, E]), sb("mhalf", [128, 8])
        S.consts_ok = ctx.enter_context(nc.semaphore("consts_ok"))
        S.settled = ctx.enter_context(nc.semaphore("settled"))
        S.weights_in = ctx.enter_context(nc.semaphore("weights_in"))
        o0 = dram.w0a.shape[1]
        S.w0a, S.w0b = sb("w0a", [LO, o0]), sb("w0b", [HI + 1, o0])
        S.c0a, S.c0b = sb("c0a", [LO, 3]), sb("c0b", [HI, 3])
        S.cat1, S.cat2 = sb("cat1", [LO, G, NK]), sb("cat2", [HI + 1, G, NK])
        S.a0_o2, S.a0_tS2 = sb("a0_o2", [HI + 1, G, N]), sb("a0_tS2", [HI + 1, G, N])
        S.t1, S.t2, S.fwT = sb("t1", [LO, B * N]), sb("t2", [HI + 1, B * N]), sb("fwT", [E, B * N])
        S.w1w, S.w1g = sb("w1w", [D // 2 + 1, 2, 512 + 2 * D]), sb("w1g", [D // 2, 2, 3 * D // 2])
        S.a1_v, S.a1_out1 = sb("a1_v", [N, G, 8, D // 8 + 1]), sb("a1_out1", [D // 2 + 1, GN])
        S.ones_rows = [S.a1_v[:, :, :, D // 8:D // 8 + 1], S.a1_out1[D // 2:D // 2 + 1, :],
                       S.cat2[HI:HI + 1, :, :], S.a0_o2[HI:HI + 1, :, :], S.a0_tS2[HI:HI + 1, :, :]]
        S.b2 = sb("b2", [E, D])
        S.n_consts = 3 + len(S.ones_rows)
        S.loads = [(S.w0a[:], dram.w0a), (S.w0b[:], dram.w0b), (S.c0a[:], dram.c0a), (S.c0b[:], dram.c0b)]
        S.loads += [(S.cat1[:, j, N:NK], dram.mem[0:LO, :]) for j in range(G)]
        S.loads += [(S.cat2[0:HI, j, N:NK], dram.mem[LO:D, :]) for j in range(G)]
        S.loads += [(S.b2[:], dram.b2), (S.w1w[:], dram.w1w), (S.w1g[:], dram.w1g)]
        tok_phase(nc, dram, S)
        attn0_phase(nc, dram, S)
        experts_phase(nc, dram, S, 0)
        experts_phase(nc, dram, S, 1)
        S.w4a, S.w4b = sb("w4a", [LO, W4.width]), sb("w4b", [HI + 1, W4.width])
        S.c4a, S.c4b = sb("c4a", [LO, 21]), sb("c4b", [HI, 6])
        S.ro1, S.ro2, S.ro3 = sb("ro1", [128, 2, 128]), sb("ro2", [128, 64]), sb("ro3", [65, 4])
        S.fc2, S.fc2b, S.ones1 = sb("fc2", [128, 6, D]), sb("fc2b", [1, D]), sb("ones1", [1, N])
        S.f_xa2, S.f_o2, S.f_h2 = sb("f_xa2", [HI + 1, GN]), sb("f_o2", [HI + 1, GN]), sb("f_h2", [65, GN])
        S.f_v = sb("f_v", [N, G, 12, D // 12 + 1])
        S.late_ones = [S.f_xa2[HI:HI + 1, :], S.f_o2[HI:HI + 1, :], S.f_h2[64:65, :], S.f_v[:, :, :, D // 12:D // 12 + 1],
                       S.ones1[:]]
        S.late_loads = [(t[:], d) for t, d in ((S.w4a, dram.w4a), (S.w4b, dram.w4b), (S.c4a, dram.c4a), (S.c4b, dram.c4b),
                                               (S.ro1, dram.ro1), (S.ro2, dram.ro2), (S.ro3, dram.ro3), (S.fc2, dram.fc2),
                                               (S.fc2b, dram.fc2b))]
        S.late_ones_ok = ctx.enter_context(nc.semaphore("late_ones_ok"))
        S.late_in = ctx.enter_context(nc.semaphore("late_in"))
        attn1_phase(nc, dram, S)
        ffn1_phase(nc, dram, S)


def kernel(**inputs):
    import concourse.bacc as bacc
    from concourse.bass_utils import run_bass_kernel_spmd

    a = {k: np.ascontiguousarray(v) for k, v in inputs.items()}
    nc = bacc.Bacc("TRN2", target_bir_lowering=False, num_devices=1)
    arrays, dram = {}, Names()

    def give(name, x):
        x = np.ascontiguousarray(x)
        arrays["in_" + name] = x
        return nc.dram_tensor("in_" + name, x.shape, mybir.dt.from_np(x.dtype), kind="ExternalInput").ap()

    patches = a["x"].reshape(B, CHANNELS, GRID, PATCH, GRID, PATCH).transpose(1, 3, 5, 0, 2, 4).reshape(-1, 128, B * NP)
    dram.patches = give("patches", patches.transpose(1, 0, 2))
    dram.conv = give("conv", a["L0_tok_conv_w"].reshape(D, -1).T.reshape(-1, 128, D).transpose(1, 0, 2))
    dram.conv_b = give("conv_b", a["L0_tok_conv_b"][None])
    side = 32
    edges = np.arange(1.0 / side, 1.0, 1.0 / side, dtype=np.float32)
    frac = np.arange(0.0, 1.0 - 1e-06, 1.0 / GRID, dtype=np.float32)
    at = np.searchsorted(edges, frac, side="right")
    ids = (at[:, None] * side + at).reshape(-1)
    dram.pos = give("pos", np.concatenate([a["L0_tok_pos_table"][ids]] * 3))
    dram.txt = give("txt", a["txt"])

    def halves(*cols):
        rows = np.concatenate([np.concatenate([m, b[None]]) for m, b in cols], axis=1)
        return rows[0:LO], rows[LO:D + 1]

    z = np.zeros(D, np.float32)
    w0 = halves((a["L0_attn_Wq"], z), (a["L0_attn_Wk"], z), (a["L0_attn_Wv"], a["L0_attn_bv"]),
                (a["L0_attn_Wo"], a["L0_attn_bo"]), (a["L0_ffn_gate_w"].T, a["L0_ffn_gate_b"]))
    dram.w0a, dram.w0b = give("w0a", w0[0]), give("w0b", w0[1])
    c0 = np.stack([a["L0_attn_bq"], a["L0_attn_bk"], a["L0_ffn_scale"]], axis=1)
    dram.c0a, dram.c0b = give("c0a", c0[0:LO]), give("c0b", c0[LO:D])
    dram.mem = give("mem", a["L0_attn_memory"].T)
    def pair_tiles(x):
        x = x.reshape(E // 2, 2, *x.shape[1:])
        return np.concatenate([x[:, 0, ..., 0:LO], x[:, 1, ..., 0:LO], x[:, 0, ..., LO:D], x[:, 1, ..., LO:D]], axis=-1)

    w1 = np.concatenate([a["L0_ffn_w1"], a["L0_ffn_b1"][:, None, :]], axis=1)
    w1 = np.concatenate([pair_tiles(w1[..., 0:I]), pair_tiles(w1[..., I:2 * I])], axis=-1)
    dram.w1a, dram.w1b = give("w1a", w1[:, 0:LO]), give("w1b", w1[:, LO:D + 1])
    w2 = pair_tiles(a["L0_ffn_w2"].transpose(0, 2, 1)).transpose(0, 2, 1).reshape(E // 2, 3, 128, D)
    dram.w2 = give("w2", w2.transpose(0, 2, 1, 3).reshape(E // 2, 128, 3 * D))
    dram.b2 = give("b2", a["L0_ffn_b2"])
    def heads(m, n, wd):
        m = m.reshape(m.shape[0], n, -1)
        return np.concatenate([m, np.zeros((*m.shape[0:2], wd - m.shape[2]), np.float32)], axis=2).reshape(m.shape[0], n * wd)

    qkv = a["L1_attn_w_qkv"].T
    rows = np.concatenate([heads(qkv[:, 0:D], 8, 32), heads(qkv[:, D:2 * D], 8, 32), qkv[:, 2 * D:],
                           a["L1_attn_w_proj"].T], axis=1)
    bias = np.concatenate([np.zeros(512 + D, np.float32), a["L1_attn_b_proj"]])[None]
    GDIM = D // 2
    dram.w1w = give("w1w", np.stack([np.concatenate([rows[0:GDIM], np.zeros_like(bias)]), np.concatenate([rows[GDIM:], bias])], axis=1))
    dram.w1g = give("w1g", np.stack([a["L1_attn_w_g0"].T, a["L1_attn_w_g1"].T], axis=1))
    f = {n[len("L1_ffn_"):]: v for n, v in a.items() if n.startswith("L1_ffn_")}
    none = lambda n: np.zeros(n, np.float32)
    down = f["lra_down"].reshape(D, D).T
    up = f["lra_up"].transpose(0, 2, 1).reshape(D, D)
    w4 = halves((f["r_in_w"].T, none(128)), (heads(f["wq"].T, 12, 32), none(384)), (heads(f["wk"].T, 12, 32), none(384)),
                (f["wv"].T, f["bv"]), (f["wo"].T, f["bo"]), (f["fc1_w"].T, none(768)), (down, none(D)), (up, none(D)))
    dram.w4a, dram.w4b = give("w4a", w4[0]), give("w4b", w4[1])
    per_feature = np.stack([f["r_ln_g"], f["r_ln_b"], f["ln1_g"], f["ln1_b"], f["ln2_g"], f["ln2_b"]], axis=1)
    other = [f["r_in_b"][:, None], f["r_o1_b"][:, None], np.concatenate([f["r_o2_b"], none(64)])[:, None],
             heads(f["bq"][None], 12, 32).reshape(3, 128).T, heads(f["bk"][None], 12, 32).reshape(3, 128).T,
             f["fc1_b"].reshape(6, 128).T]
    dram.c4a = give("c4a", np.concatenate([per_feature[0:LO], *other], axis=1))
    dram.c4b = give("c4b", per_feature[LO:D])
    dram.ro1 = give("ro1", f["r_o1_w"].T.reshape(2, 128, 128).transpose(1, 0, 2))
    dram.ro2 = give("ro2", f["r_o2_w"].T)
    dram.ro3 = give("ro3", np.concatenate([f["r_o3_w"].T, f["r_o3_b"][None]]))
    dram.fc2 = give("fc2", f["fc2_w"].T.reshape(6, 128, D).transpose(1, 0, 2))
    dram.fc2b = give("fc2b", f["fc2_b"][None])
    dram.fw = nc.dram_tensor("fw_scratch", [E, B * N], F32, kind="Internal").ap()
    dram.out = nc.dram_tensor("out_0", [B, N, D], F32, kind="ExternalOutput").ap()
    program(nc, dram)
    r = run_bass_kernel_spmd(nc, [arrays], core_ids=[0])
    return r.results[0]["out_0"]
```

```python
from contextlib import ExitStack

import numpy as np

import concourse.bass as bass
from concourse import mybir

ALU = mybir.AluOpType
ACT = mybir.ActivationFunctionType
AX = mybir.AxisListType
F32 = mybir.dt.float32
F32R = mybir.dt.float32r
U32 = mybir.dt.uint32

B = 16
SIDE, PATCH, CHANNELS = 96, 16, 3
GRID = SIDE // PATCH
NP = GRID * GRID
NT = 77
N = NP + NT
D = 192
LO, HI = 128, D - 128
M = 8
NK = N + M
G = 4
STEPS = B // G
GN = G * N
E, TOPK, I = 16, 4, 192
EPS = 1e-5


class Names:
    pass


class Counted:
    def __init__(self, sem, per):
        self.sem, self.per = sem, per


class W0:
    q, k, v, o, g = 0, D, 2 * D, 3 * D, 4 * D
    cq, ck, cs = 0, 1, 2


class W1:
    q, k, v, o = 0, 256, 512, 512 + D


class W4:
    r, q, k, v, o, f, dn, up = 0, 128, 512, 896, 896 + D, 896 + 2 * D, 1664 + 2 * D, 1664 + 3 * D
    width = 1664 + 4 * D


class C4:
    rg, rb, g1, b1, g2, b2, r, h1, h2, q, k, f = 0, 1, 2, 3, 4, 5, 6, 7, 8, 9, 12, 15


def counted(nc, ctx, name, per):
    return Counted(ctx.enter_context(nc.semaphore(name)), per)


def done(s, it, n):
    return s.sem, s.per * (it + 1) + n + 1


def before(n, ring, per):
    return n - ring if n >= ring else max(m for m in range(per) if m % ring == n % ring) - per


def credit(eng, *sems):
    for s in sems:
        eng.sem_inc(s.sem, s.per)


def settle(eng, S):
    eng.sem_inc(S.settled, 1)


def bc(ap, shape):
    return ap.to_broadcast(shape)


def tok_phase(nc, dram, S):
    KT = CHANNELS * PATCH * PATCH // 128
    PER = 3
    CH = [(b, min(PER, B - b)) for b in range(0, B, PER)]
    with ExitStack() as ctx:
        patches = ctx.enter_context(nc.sbuf_tensor("patches", [128, KT, B * NP], F32))
        conv = ctx.enter_context(nc.sbuf_tensor("conv", [128, KT, D], F32))
        pos = ctx.enter_context(nc.sbuf_tensor("pos", [PER * NP, D], F32))
        convb = ctx.enter_context(nc.sbuf_tensor("convb", [PER * NP, D], F32))
        emb = ctx.enter_context(nc.sbuf_tensor("emb", [PER * NP, len(CH), D], F32))
        ps = [ctx.enter_context(nc.psum_tensor(f"tok_ps{i}", [128, 512], F32)) for i in range(len(CH))]
        sem = lambda n: ctx.enter_context(nc.semaphore(n))
        k_in = [sem(f"tok_in{k}") for k in range(KT)]
        rows_in, posb, emb_ps, emb_ok, h_in = sem("tok_rows"), sem("tok_posb"), sem("tok_ps"), sem("tok_emb"), sem("tok_h")
        ident0 = sem("ident0")
        eb = ctx.enter_context(nc.sbuf_tensor("eb", [E // 2, 768], F32))
        eb_hi, eb_lo = (ctx.enter_context(nc.sbuf_tensor(n, [E // 2, 768], F32R)) for n in ("eb_hi", "eb_lo"))
        eb_in, eb_ok, eb_stored = sem("eb_in"), sem("eb_ok"), sem("eb_stored")
        block = ctx.enter_context(nc.Block())

        @block.sync
        def _(sp):
            for k in range(KT):
                sp.dma_start(patches[:, k, :], dram.patches[:, k, :]).then_inc(k_in[k], 16)
                sp.dma_start(conv[:, k, :], dram.conv[:, k, :]).then_inc(k_in[k], 16)
            sp.dma_start(S.H[NP:N, :, :], dram.txt.rearrange("b t d -> t b d")).then_inc(h_in, 16)
            for c, (b, nb) in enumerate(CH):
                for j in range(nb):
                    sp.wait_ge(emb_ok, c + 1)
                    sp.dma_start(S.H[0:NP, b + j, :], emb[j * NP:(j + 1) * NP, c, :]).then_inc(h_in, 16)
            for n, t in enumerate((eb_hi, eb_lo)):
                sp.wait_ge(eb_ok, n + 2)
                sp.dma_start(dram.eb[:, n, :], t[:].bitcast(F32)).then_inc(eb_stored, 16)
            sp.wait_ge(eb_stored, 32)
            sp.wait_ge(h_in, 16 * (B + 1))

        @block.scalar
        def _(act):
            act.dma_start(pos[:], dram.pos).then_inc(rows_in, 16)
            act.dma_start(convb[:], bc(dram.conv_b, [PER * NP, D])).then_inc(rows_in, 16)
            act.dma_start(eb[:], dram.b1).then_inc(eb_in, 16)
            for t, src in S.loads:
                act.dma_start(t, src).then_inc(S.weights_in, 16)
            act.wait_ge(S.weights_in, 16 * len(S.loads))

        @block.gpsimd
        def _(pool):
            nc.gpsimd.memset(S.ident[:], 0.0).then_inc(ident0, 1)
            pool.wait_ge(ident0, 1)
            nc.gpsimd.affine_select(out=S.ident[:], in_=S.ident[:], compare_op=ALU.not_equal, fill=1.0, base=0,
                                    pattern=[[-1, 128]], channel_multiplier=1).then_inc(S.consts_ok, 1)
            nc.gpsimd.iota(S.iota[:], pattern=[[1, E]], base=0, channel_multiplier=0,
                           allow_small_or_imprecise_dtypes=True).then_inc(S.consts_ok, 1)
            nc.gpsimd.memset(S.mhalf[:], -0.5).then_inc(S.consts_ok, 1)
            for n, t in enumerate(S.ones_rows):
                pool.wait_ge(S.consts_ok, 3 + n)
                nc.gpsimd.memset(t, 1.0).then_inc(S.consts_ok, 1)

        @block.tensor
        def _(pe):
            for k in range(KT):
                pe.wait_ge(k_in[k], 32)
                for c, (b, nb) in enumerate(CH):
                    mm = nc.tensor.matmul(ps[c][0:nb * NP, 0:D], patches[:, k, b * NP:(b + nb) * NP], conv[:, k, :],
                                          start=(k == 0), stop=(k == KT - 1))
                    if k == KT - 1:
                        mm.then_inc(emb_ps, 1)

        @block.vector
        def _(dve):
            dve.wait_ge(rows_in, 32)
            nc.vector.tensor_tensor(pos[:], pos[:], convb[:], ALU.add).then_inc(posb, 1)
            dve.wait_ge(eb_in, 16)
            nv = nc.vector
            nv.tensor_scalar(eb[:, 384:768], eb[:, 384:768], 1.0, None, ALU.add).then_inc(eb_ok, 1)
            dve.wait_ge(eb_ok, 1)
            nv.tensor_copy(eb_hi[:], eb[:]).then_inc(eb_ok, 1)
            dve.wait_ge(eb_ok, 2)
            nv.tensor_tensor(eb_lo[:], eb[:], eb_hi[:].bitcast(F32), ALU.subtract).then_inc(eb_ok, 1)
            dve.wait_ge(posb, 1)
            for c, (b, nb) in enumerate(CH):
                dve.wait_ge(emb_ps, c + 1)
                nc.vector.tensor_tensor(emb[0:nb * NP, c, :], ps[c][0:nb * NP, 0:D], pos[0:nb * NP, :],
                                        ALU.add).then_inc(emb_ok, 1)


class Tiles:

    def __init__(self, nc, ctx, name, banks, readers):
        self.banks, self.readers = banks, readers
        self.filled = counted(nc, ctx, name + "_ps", len(readers))
        self.outs = {e: counted(nc, ctx, f"{name}_{e}_out", readers.count(e)) for e in ("act", "dve")}

    def bank(self, n):
        return self.banks[n % len(self.banks)]

    def out(self, n):
        return self.outs[self.readers[n]].sem

    def copied(self, it, n):
        e = self.readers[n]
        k = self.readers[:n % len(self.readers)].count(e)
        return done(self.outs[e], it, k - (self.outs[e].per if n < 0 else 0))

    def free(self, it, n):
        return self.copied(it, before(n, len(self.banks), len(self.readers)))


def attn0_phase(nc, dram, S):
    with ExitStack() as ctx:
        def sb(name, shape, dt=F32):
            return ctx.enter_context(nc.sbuf_tensor("a0_" + name, shape, dt))

        def sem(name, per):
            return counted(nc, ctx, "a0_" + name, per)

        w = W0
        xn = sb("xn", [N, G, D])
        stats, mv, veps, rstd = sb("stats", [N, G, 6]), sb("mv", [N, G, 2]), sb("veps", [N, G]), sb("rstd", [N, G])
        cat1, cat2 = S.cat1, S.cat2
        q1, q2 = sb("q1", [LO, G, N]), sb("q2", [HI, G, N])
        k1, k2 = sb("k1", [LO, G, NK]), sb("k2", [HI, G, NK])
        v = sb("v", [NK, G, D])
        mx, rs, ri = sb("mx", [N, G]), sb("rs", [N, G]), sb("ri", [N, G])
        p, pT = sb("p", [N, G, NK]), sb("pT", [NK, G, N])
        o1, o2 = sb("o1", [LO, G, N]), S.a0_o2
        stats2, mv2, veps2, rstd2 = sb("stats2", [N, G, 6]), sb("mv2", [N, G, 2]), sb("veps2", [N, G]), sb("rstd2", [N, G])
        x, sq, ssq, veps3, rrms = sb("x", [N, G, D]), sb("sq", [N, D]), sb("ssq", [N, G]), sb("veps3", [N, G]), sb("rrms", [N, G])
        t, tS1, tS2 = sb("t", [N, G, D]), sb("tS1", [LO, G, N]), S.a0_tS2
        g, top, idx, idxf = sb("g", [N, G, E]), sb("top", [N, G, 8]), sb("idx", [N, G, 8], U32), sb("idxf", [N, G, TOPK])
        e4, s4, r4, w4 = sb("e4", [N, G, TOPK]), sb("s4", [N, G]), sb("r4", [N, G]), sb("w4", [N, G, TOPK])
        oh, fw, fwT = sb("oh", [N, G, E, TOPK]), sb("fw", [N, G, E]), sb("fwT", [E, GN])
        bank = [ctx.enter_context(nc.psum_tensor(f"a0_ps{i}", [128, 512], F32)) for i in range(8)]
        X1, X2, Q1, Q2, K1, K2, V0, V1 = range(8)
        proj = Tiles(nc, ctx, "a0_proj", bank[0:3], ["act", "dve", "act", "dve", "dve", "act", "dve", "act"])
        SC, PT, O1, O2, H0, H1 = range(6)
        att = Tiles(nc, ctx, "a0_att", bank[3:6], ["dve", "act", "act", "dve", "dve", "dve"])
        T1, T2, LG, FW = range(4)
        rout = Tiles(nc, ctx, "a0_rout", bank[6:8], ["act", "dve", "dve", "act"])

        stat1_ok, mean1_ok, stat2_ok, mean2_ok = (sem(n, G) for n in ("stat1_ok", "mean1_ok", "stat2_ok", "mean2_ok"))
        veps1_ok, veps2_ok, veps3_ok, rstd1_ok, rstd2_ok, rrms_ok = (sem(n, 1) for n in (
            "veps1_ok", "veps2_ok", "veps3_ok", "rstd1_ok", "rstd2_ok", "rrms_ok"))
        xn_ok, x_ok, ssq_ok, t_ok, hx_ok = sem("xn_ok", G), sem("x_ok", G), sem("ssq_ok", G), sem("t_ok", G), sem("hx_ok", 1)
        mx_ok, exp_ok, sum_ok, rec_ok, p_ok = (sem(n, 1) for n in ("mx_ok", "exp_ok", "sum_ok", "rec_ok", "p_ok"))
        top_ok, idx_ok = sem("top_ok", G), sem("idx_ok", G)
        idxf_ok, e4_ok, e4x_ok, s4_ok, r4_ok, w4_ok, oh_ok, ohw_ok, fw_ok = (sem(n, 1) for n in (
            "idxf_ok", "e4_ok", "e4x_ok", "s4_ok", "r4_ok", "w4_ok", "oh_ok", "ohw_ok", "fw_ok"))
        t_stored, fw_stored = sem("t_stored", 32), sem("fw_stored", 32)
        block = ctx.enter_context(nc.Block())

        def rows(it):
            return S.H[0:N, :, :].rearrange("p b d -> p (b d)")[:, bass.ds(it * (G * D), G * D)].rearrange(
                "p (b d) -> p b d", b=G)

        def images(tile):
            return tile.rearrange("p (g n) -> p g n", g=G)

        def steps(eng, lead, body, tail):
            lead()
            body(0, True, False)
            with eng.Fori(1, STEPS - 1) as it:
                body(it, False, False)
            body(STEPS - 1, False, True)
            tail(STEPS - 1)

        @block.tensor
        def _(pe):
            credit(pe, proj.filled, att.filled, rout.filled)
            pe.wait_ge(S.consts_ok, S.n_consts)
            mm = nc.tensor.matmul

            def transposed(it, tiles, n, src, ok):
                pe.wait_ge(*tiles.free(it, n + 1))
                pe.wait_ge(*tiles.free(it, n))
                for m, c0, c1 in ((n, 0, LO), (n + 1, LO, D)):
                    for j in range(G):
                        if m == n:
                            pe.wait_ge(*done(ok, it, j))
                        i = nc.tensor.transpose(tiles.bank(m)[0:c1 - c0, j * N:(j + 1) * N], src[:, j, c0:c1], S.ident[0:N, 0:N])
                    i.then_inc(tiles.filled.sem, 1)

            def qk(it):
                pe.wait_ge(*proj.copied(it, X1))
                pe.wait_ge(*proj.copied(it, X2))
                for n, col, wd in ((Q1, w.q, N), (K1, w.k, NK)):
                    for half, (c0, c1) in enumerate(((0, LO), (LO, D))):
                        pe.wait_ge(*proj.free(it, n + half))
                        o = images(proj.bank(n + half)[0:c1 - c0, 0:G * wd])
                        mm(o, S.w0a[:, col + c0:col + c1], cat1[:, :, 0:wd], start=True, stop=False)
                        mm(o, S.w0b[0:HI, col + c0:col + c1], cat2[0:HI, :, 0:wd], start=False, stop=True
                           ).then_inc(proj.filled.sem, 1)

            def values(it):
                for h in range(2):
                    pe.wait_ge(*proj.free(it, V0 + h))
                    for j in (2 * h, 2 * h + 1):
                        o = proj.bank(V0 + h)[0:NK, (j % 2) * D:(j % 2 + 1) * D]
                        mm(o, cat1[:, j, :], S.w0a[:, w.v:w.v + D], start=True, stop=False)
                        m = mm(o, cat2[:, j, :], S.w0b[:, w.v:w.v + D], start=False, stop=True)
                    m.then_inc(proj.filled.sem, 1)

            def scores(it):
                pe.wait_ge(*proj.copied(it, K1))
                pe.wait_ge(*proj.copied(it, K2))
                pe.wait_ge(*att.free(it, SC))
                for j in range(G):
                    o = att.bank(SC)[0:N, j * NK:(j + 1) * NK]
                    mm(o, q1[:, j, :], k1[:, j, :], start=True, stop=False)
                    m = mm(o, q2[:, j, :], k2[:, j, :], start=False, stop=True)
                m.then_inc(att.filled.sem, 1)

            def p_transposed(it):
                pe.wait_ge(*done(p_ok, it, 0))
                pe.wait_ge(*att.free(it, PT))
                for j in range(G):
                    m = nc.tensor.transpose(att.bank(PT)[0:NK, j * N:(j + 1) * N], p[:, j, :], S.ident[0:N, 0:N])
                m.then_inc(att.filled.sem, 1)

            def attended(it):
                pe.wait_ge(*att.copied(it, PT))
                pe.wait_ge(*proj.copied(it, V0))
                pe.wait_ge(*proj.copied(it, V1))
                for n, c0, c1 in ((O1, 0, LO), (O2, LO, D)):
                    pe.wait_ge(*att.free(it, n))
                    for j in range(G):
                        m = mm(att.bank(n)[0:c1 - c0, j * N:(j + 1) * N], v[:, j, c0:c1], pT[:, j, :], start=True, stop=True)
                    m.then_inc(att.filled.sem, 1)

            def projected(it):
                pe.wait_ge(*att.copied(it, O1))
                pe.wait_ge(*att.copied(it, O2))
                for h in range(2):
                    pe.wait_ge(*att.free(it, H0 + h))
                    for j in (2 * h, 2 * h + 1):
                        o = att.bank(H0 + h)[0:N, (j % 2) * D:(j % 2 + 1) * D]
                        mm(o, o1[:, j, :], S.w0a[:, w.o:w.o + D], start=True, stop=False)
                        m = mm(o, o2[:, j, :], S.w0b[:, w.o:w.o + D], start=False, stop=True)
                    m.then_inc(att.filled.sem, 1)

            def logits(it):
                pe.wait_ge(*rout.copied(it, T1))
                pe.wait_ge(*rout.copied(it, T2))
                pe.wait_ge(*rout.free(it, LG))
                for j in range(G):
                    o = rout.bank(LG)[0:N, j * E:(j + 1) * E]
                    mm(o, tS1[:, j, :], S.w0a[:, w.g:w.g + E], start=True, stop=False)
                    m = mm(o, tS2[0:HI + 1, j, :], S.w0b[:, w.g:w.g + E], start=False, stop=True)
                m.then_inc(rout.filled.sem, 1)

            def fw_transposed(it):
                pe.wait_ge(*done(fw_ok, it, 0))
                pe.wait_ge(*rout.free(it, FW))
                for j in range(G):
                    m = nc.tensor.transpose(rout.bank(FW)[0:E, j * N:(j + 1) * N], fw[:, j, :], S.ident[0:N, 0:N])
                m.then_inc(rout.filled.sem, 1)

            def lead():
                transposed(0, proj, X1, xn, xn_ok)
                qk(0)
                values(0)

            def body(it, first, last):
                scores(it)
                if not last:
                    transposed(it + 1, proj, X1, xn, xn_ok)
                p_transposed(it)
                if not last:
                    qk(it + 1)
                if not first:
                    transposed(it - 1, rout, T1, t, t_ok)
                attended(it)
                if not first:
                    logits(it - 1)
                if not last:
                    values(it + 1)
                projected(it)
                if not first:
                    fw_transposed(it - 1)

            def tail(it):
                transposed(it, rout, T1, t, t_ok)
                logits(it)
                fw_transposed(it)

            steps(pe, lead, body, tail)

        @block.scalar
        def _(act):
            credit(act, *(ts.outs["act"] for ts in (proj, att, rout)), exp_ok, ssq_ok, e4x_ok)
            cp = nc.scalar.activation

            def x_copy(it):
                act.wait_ge(*done(proj.filled, it, X1))
                cp(cat1[:, :, 0:N], images(proj.bank(X1)[0:LO, 0:GN]), ACT.Copy).then_inc(proj.out(X1), 1)

            def qk_copy(it):
                act.wait_ge(*done(proj.filled, it, Q1))
                act.wait_ge(*done(att.filled, it, SC - att.filled.per))
                cp(q1[:], images(proj.bank(Q1)[0:LO, 0:GN]), ACT.Identity, bias=S.c0a[:, w.cq:w.cq + 1]).then_inc(proj.out(Q1), 1)
                act.wait_ge(*done(proj.filled, it, K2))
                cp(k2[:], images(proj.bank(K2)[0:HI, 0:G * NK]), ACT.Identity, bias=S.c0b[:, w.ck:w.ck + 1]
                   ).then_inc(proj.out(K2), 1)

            def v_copy(it):
                act.wait_ge(*done(proj.filled, it, V1))
                act.wait_ge(*done(att.filled, it, O2 - att.filled.per))
                cp(v[:, 2:4, :], proj.bank(V1)[0:NK, 0:2 * D].rearrange("p (g n) -> p g n", g=2), ACT.Copy
                   ).then_inc(proj.out(V1), 1)

            def exp(it):
                act.wait_ge(*att.copied(it, SC))
                cp(p[:], p[:], ACT.Exp, scale=float(D) ** -0.5).then_inc(exp_ok.sem, 1)

            def p_copy(it):
                act.wait_ge(*done(att.filled, it, PT))
                cp(pT[:], images(att.bank(PT)[0:NK, 0:GN]), ACT.Copy).then_inc(att.out(PT), 1)

            def o_copy(it):
                act.wait_ge(*done(att.filled, it, O1))
                cp(o1[:], images(att.bank(O1)[0:LO, 0:GN]), ACT.Copy).then_inc(att.out(O1), 1)

            def squares(it):
                act.wait_ge(*done(veps3_ok, it, -1))
                for j in range(G):
                    act.wait_ge(*done(x_ok, it, j))
                    act.wait_ge(*done(ssq_ok, it, j - 1))
                    cp(sq[:], x[:, j, :], ACT.Square, accum_out=ssq[:, j:j + 1]).then_inc(ssq_ok.sem, 1)

            def t_copy(it):
                act.wait_ge(*done(rout.filled, it, T1))
                act.wait_ge(*done(rout.filled, it, LG - rout.filled.per))
                act.wait_ge(*done(t_stored, it, -1))
                cp(tS1[:], images(rout.bank(T1)[0:LO, 0:GN]), ACT.Identity, scale=S.c0a[:, w.cs:w.cs + 1]
                   ).then_inc(rout.out(T1), 1)

            def top_exp(it):
                act.wait_ge(*done(e4_ok, it, 0))
                cp(e4[:], e4[:], ACT.Exp).then_inc(e4x_ok.sem, 1)

            def fw_copy(it):
                act.wait_ge(*done(rout.filled, it, FW))
                act.wait_ge(*done(fw_stored, it, -1))
                cp(fwT[:], rout.bank(FW)[0:E, 0:GN], ACT.Copy).then_inc(rout.out(FW), 1)

            def lead():
                x_copy(0)
                qk_copy(0)
                v_copy(0)

            def body(it, first, last):
                exp(it)
                if not last:
                    x_copy(it + 1)
                if not first:
                    squares(it - 1)
                p_copy(it)
                if not last:
                    qk_copy(it + 1)
                if not first:
                    t_copy(it - 1)
                o_copy(it)
                if not first:
                    top_exp(it - 1)
                if not last:
                    v_copy(it + 1)
                if not first:
                    fw_copy(it - 1)

            def tail(it):
                squares(it)
                t_copy(it)
                top_exp(it)
                fw_copy(it)

            steps(act, lead, body, tail)

        @block.gpsimd
        def _(pool):
            credit(pool, veps1_ok, veps2_ok, veps3_ok, rstd1_ok, rstd2_ok, rrms_ok, hx_ok)
            ts, tt = nc.gpsimd.tensor_scalar, nc.gpsimd.tensor_tensor

            def root(it, ok, src, scale, ve, ve_ok, out, out_ok, used):
                pool.wait_ge(*done(ok, it, G - 1))
                settle(pool, S)
                ts(ve[:], src, scale, EPS, ALU.mult, ALU.add).then_inc(ve_ok.sem, 1)
                pool.wait_ge(*done(ve_ok, it, 0))
                pool.wait_ge(*done(used, it, -1))
                tt(out[:], ve[:], S.mhalf[0:N, 0:G], ALU.pow).then_inc(out_ok.sem, 1)

            def root1(it):
                root(it, mean1_ok, mv[:, :, 1], 1.0, veps, veps1_ok, rstd, rstd1_ok, xn_ok)

            def router(it):
                root(it, mean2_ok, mv2[:, :, 1], 1.0, veps2, veps2_ok, rstd2, rstd2_ok, x_ok)

            def router2(it):
                root(it, ssq_ok, ssq[:], 1.0 / D, veps3, veps3_ok, rrms, rrms_ok, t_ok)
                hg = rows(it)
                tt(hg, hg, x[:], ALU.add).then_inc(hx_ok.sem, 1)

            def body(it, first, last):
                if not last:
                    root1(it + 1)
                if not first:
                    router(it - 1)
                    router2(it - 1)

            def tail(it):
                router(it)
                router2(it)

            steps(pool, lambda: root1(0), body, tail)

        @block.vector
        def _(dve):
            credit(dve, stat1_ok, mean1_ok, stat2_ok, mean2_ok, xn_ok, x_ok, t_ok, *(ts.outs["dve"] for ts in (proj, att, rout)),
                   mx_ok, sum_ok, rec_ok, p_ok, top_ok, idx_ok, idxf_ok, e4_ok, s4_ok, r4_ok, w4_ok, oh_ok, ohw_ok, fw_ok)
            nv = nc.vector

            def mean(it, st, m, st_ok, m_ok):
                src = rows(it)
                settle(dve, S)
                for j in range(G):
                    nv.bn_stats(st[:, j, :], src[:, j, :]).then_inc(st_ok.sem, 1)
                dve.wait_ge(*done(st_ok, it, G - 1))
                settle(dve, S)
                for j in range(G):
                    nv.bn_aggr(m[:, j, :], st[:, j, :]).then_inc(m_ok.sem, 1)

            def norm(it, m, m_ok, r, r_ok, out, ok):
                src = rows(it)
                dve.wait_ge(*done(m_ok, it, G - 1))
                dve.wait_ge(*done(r_ok, it, 0))
                for j in range(G):
                    nv.tensor_scalar(out[:, j, :], src[:, j, :], m[:, j, 0:1], r[:, j:j + 1],
                                     ALU.subtract, ALU.mult).then_inc(ok.sem, 1)

            def mean1(it):
                mean(it, stats, mv, stat1_ok, mean1_ok)

            def norm1(it):
                dve.wait_ge(*done(proj.filled, it, X2 - proj.filled.per))
                norm(it, mv, mean1_ok, rstd, rstd1_ok, xn, xn_ok)

            def x_copy(it):
                dve.wait_ge(*done(proj.filled, it, X2))
                nv.tensor_copy(cat2[0:HI, :, 0:N], images(proj.bank(X2)[0:HI, 0:GN])).then_inc(proj.out(X2), 1)

            def qk_copy(it):
                dve.wait_ge(*done(att.filled, it, SC - att.filled.per))
                dve.wait_ge(*done(proj.filled, it, Q2))
                nv.tensor_scalar(q2[:], images(proj.bank(Q2)[0:HI, 0:GN]), S.c0b[:, w.cq:w.cq + 1], None, ALU.add
                                 ).then_inc(proj.out(Q2), 1)
                dve.wait_ge(*done(proj.filled, it, K1))
                nv.tensor_scalar(k1[:], images(proj.bank(K1)[0:LO, 0:G * NK]), S.c0a[:, w.ck:w.ck + 1], None, ALU.add
                                 ).then_inc(proj.out(K1), 1)

            def v_copy(it):
                dve.wait_ge(*done(att.filled, it, O2 - att.filled.per))
                dve.wait_ge(*done(proj.filled, it, V0))
                nv.tensor_copy(v[:, 0:2, :], proj.bank(V0)[0:NK, 0:2 * D].rearrange("p (g n) -> p g n", g=2)
                               ).then_inc(proj.out(V0), 1)

            def softmax_in(it):
                sc = images(att.bank(SC)[0:N, 0:G * NK])
                dve.wait_ge(*done(att.filled, it, SC))
                nv.tensor_reduce(mx[:], sc, AX.X, ALU.max).then_inc(mx_ok.sem, 1)
                dve.wait_ge(*done(mx_ok, it, 0))
                dve.wait_ge(*done(att.filled, it, PT - att.filled.per))
                nv.tensor_tensor(p[:], sc, bc(mx[:].unsqueeze(2), [N, G, NK]), ALU.subtract).then_inc(att.out(SC), 1)

            def softmax_out(it):
                dve.wait_ge(*done(exp_ok, it, 0))
                nv.tensor_reduce(rs[:], p[:], AX.X, ALU.add).then_inc(sum_ok.sem, 1)
                dve.wait_ge(*done(sum_ok, it, 0))
                nv.reciprocal(ri[:], rs[:]).then_inc(rec_ok.sem, 1)
                dve.wait_ge(*done(rec_ok, it, 0))
                nv.tensor_tensor(p[:], p[:], bc(ri[:].unsqueeze(2), [N, G, NK]), ALU.mult).then_inc(p_ok.sem, 1)

            def o_copy(it):
                dve.wait_ge(*done(att.filled, it, O2))
                nv.tensor_copy(o2[0:HI, :, :], images(att.bank(O2)[0:HI, 0:GN])).then_inc(att.out(O2), 1)

            def residual(it):
                hg = rows(it)
                for h in range(2):
                    dve.wait_ge(*done(att.filled, it, H0 + h))
                    nv.tensor_tensor(hg[:, 2 * h:2 * h + 2, :],
                                     att.bank(H0 + h)[0:N, 0:2 * D].rearrange("p (g n) -> p g n", g=2),
                                     hg[:, 2 * h:2 * h + 2, :], ALU.add).then_inc(att.out(H0 + h), 1)

            def mean2(it):
                dve.wait_ge(*att.copied(it, H1))
                mean(it, stats2, mv2, stat2_ok, mean2_ok)

            def norm2(it):
                dve.wait_ge(*done(hx_ok, it, -1))
                norm(it, mv2, mean2_ok, rstd2, rstd2_ok, x, x_ok)

            def rms(it):
                dve.wait_ge(*done(x_ok, it, G - 1))
                dve.wait_ge(*done(rrms_ok, it, 0))
                dve.wait_ge(*done(rout.filled, it, T2 - rout.filled.per))
                for j in range(G):
                    nv.tensor_scalar(t[:, j, :], x[:, j, :], rrms[:, j:j + 1], None, ALU.mult).then_inc(t_ok.sem, 1)

            def t_copy(it):
                dve.wait_ge(*done(rout.filled, it, T2))
                dve.wait_ge(*done(t_stored, it, -1))
                nv.tensor_scalar(tS2[0:HI, :, :], images(rout.bank(T2)[0:HI, 0:GN]), S.c0b[:, w.cs:w.cs + 1], None, ALU.mult
                                 ).then_inc(rout.out(T2), 1)

            def top4(it):
                dve.wait_ge(*done(rout.filled, it, LG))
                nv.tensor_copy(g[:], images(rout.bank(LG)[0:N, 0:G * E])).then_inc(rout.out(LG), 1)
                dve.wait_ge(*rout.copied(it, LG))
                settle(dve, S)
                for j in range(G):
                    nv.max(top[:, j, :], g[:, j, :]).then_inc(top_ok.sem, 1)
                dve.wait_ge(*done(top_ok, it, G - 1))
                nv.tensor_tensor(e4[:], top[:, :, 0:TOPK], bc(top[:, :, 0:1], [N, G, TOPK]), ALU.subtract
                                 ).then_inc(e4_ok.sem, 1)
                for j in range(G):
                    nv.max_index(idx[:, j, :], top[:, j, :], g[:, j, :]).then_inc(idx_ok.sem, 1)
                dve.wait_ge(*done(idx_ok, it, G - 1))
                nv.tensor_copy(idxf[:], idx[:, :, 0:TOPK]).then_inc(idxf_ok.sem, 1)

            def weights(it):
                dve.wait_ge(*done(e4x_ok, it, 0))
                nv.tensor_reduce(s4[:], e4[:], AX.X, ALU.add).then_inc(s4_ok.sem, 1)
                dve.wait_ge(*done(s4_ok, it, 0))
                nv.reciprocal(r4[:], s4[:]).then_inc(r4_ok.sem, 1)
                dve.wait_ge(*done(idxf_ok, it, 0))
                nv.tensor_tensor(oh[:], bc(S.iota[0:N, :].unsqueeze(1).unsqueeze(3), [N, G, E, TOPK]),
                                 bc(idxf[:].unsqueeze(2), [N, G, E, TOPK]), ALU.is_equal).then_inc(oh_ok.sem, 1)
                dve.wait_ge(*done(r4_ok, it, 0))
                nv.tensor_tensor(w4[:], e4[:], bc(r4[:].unsqueeze(2), [N, G, TOPK]), ALU.mult).then_inc(w4_ok.sem, 1)
                dve.wait_ge(*done(oh_ok, it, 0))
                dve.wait_ge(*done(w4_ok, it, 0))
                nv.tensor_tensor(oh[:], oh[:], bc(w4[:].unsqueeze(2), [N, G, E, TOPK]), ALU.mult).then_inc(ohw_ok.sem, 1)
                dve.wait_ge(*done(ohw_ok, it, 0))
                dve.wait_ge(*done(rout.filled, it, FW - rout.filled.per))
                nv.tensor_reduce(fw[:], oh[:], AX.X, ALU.add).then_inc(fw_ok.sem, 1)

            def lead():
                mean1(0)
                norm1(0)
                x_copy(0)
                qk_copy(0)
                v_copy(0)

            def body(it, first, last):
                if not last:
                    mean1(it + 1)
                if not first:
                    mean2(it - 1)
                softmax_in(it)
                if not last:
                    norm1(it + 1)
                softmax_out(it)
                if not first:
                    norm2(it - 1)
                if not last:
                    x_copy(it + 1)
                if not last:
                    qk_copy(it + 1)
                if not first:
                    rms(it - 1)
                    t_copy(it - 1)
                o_copy(it)
                if not first:
                    top4(it - 1)
                if not last:
                    v_copy(it + 1)
                if not first:
                    weights(it - 1)
                residual(it)

            def tail(it):
                mean2(it)
                norm2(it)
                rms(it)
                t_copy(it)
                top4(it)
                weights(it)

            steps(dve, lead, body, tail)

        @block.sync
        def _(sp):
            credit(sp, t_stored, fw_stored)

            def store(it):
                sp.wait_ge(*rout.copied(it, T1))
                settle(sp, S)
                sp.dma_start(S.t1[:, bass.ds(it * GN, GN)], tS1[:].rearrange("p g n -> p (g n)")).then_inc(t_stored.sem, 16)
                sp.wait_ge(*rout.copied(it, T2))
                settle(sp, S)
                sp.dma_start(S.t2[:, bass.ds(it * GN, GN)], tS2[:].rearrange("p g n -> p (g n)")).then_inc(t_stored.sem, 16)
                sp.wait_ge(*rout.copied(it, FW))
                settle(sp, S)
                sp.dma_start(S.fwT[:, bass.ds(it * GN, GN)], fwT[:]).then_inc(fw_stored.sem, 16)
                sp.dma_start(dram.fw[:, bass.ds(it * GN, GN)], fwT[:]).then_inc(fw_stored.sem, 16)

            def body(it, first, last):
                if not first:
                    store(it - 1)

            steps(sp, lambda: None, body, store)
            sp.wait_ge(*done(t_stored, STEPS - 1, 31))
            sp.wait_ge(*done(fw_stored, STEPS - 1, 31))


def experts_phase(nc, dram, S):
    PAIRS, SLOTS, TILES, CHUNKS, HALVES = E // 2, 2, 3, 2, 2
    UNITS = SLOTS * CHUNKS * TILES
    LOOPS = PAIRS // SLOTS
    HB = B // HALVES
    HN = HB * N
    AHEAD = 3
    RING = AHEAD + 1
    ALPHA, LIMIT = 1.702, 7.0
    SIG_LIMIT = float(1.0 / (1.0 + np.exp(-ALPHA * LIMIT)))
    W1 = 2 * TILES * 128
    BH, BL = 64, 96
    with ExitStack() as ctx:
        def sb(name, shape, dt=F32):
            return ctx.enter_context(nc.sbuf_tensor("ex_" + name, shape, dt))

        def sem(name, per):
            return counted(nc, ctx, "ex_" + name, per)

        raw1, raw2, raw3 = sb("raw1", [LO, SLOTS, W1]), sb("raw2", [BL + 1, SLOTS, W1]), sb("raw3", [128, SLOTS, TILES * D])
        h1, l1 = sb("h1", [LO, SLOTS, W1], F32R), sb("l1", [LO, SLOTS, W1], F32R)
        hh2, l2b = sb("hh2", [2 * HI, SLOTS, W1], F32R), sb("l2b", [BL + 1, SLOTS, W1], F32R)
        h3, l3 = sb("h3", [128, SLOTS, TILES * D], F32R), sb("l3", [128, SLOTS, TILES * D], F32R)
        wbc = sb("wbc", [128, SLOTS, TILES, HN])
        th1, tl1 = sb("th1", [LO, B * N], F32R), sb("tl1", [LO, B * N], F32R)
        thl2, th2 = sb("thl2", [2 * HI, B * N], F32R), sb("th2", [BL + 1, B * N], F32R)
        sg, sw, aa, bb = (sb(n, [128, 2, GN]) for n in ("sg", "sw", "aa", "bb"))
        act_f = sb("act_f", [128, 2, GN])
        act_h, act_l = sb("act_h", [128, RING, GN], F32R), sb("act_l", [128, RING, GN], F32R)
        gp = [ctx.enter_context(nc.psum_tensor(f"ex_gps{i}", [128, 512], F32)) for i in range(2)]
        lp = [ctx.enter_context(nc.psum_tensor(f"ex_lps{i}", [128, 512], F32)) for i in range(2)]
        acc = [ctx.enter_context(nc.psum_tensor(f"ex_acc{i}", [128, 512], F32)) for i in range(HB // 2)]

        RAW = 5
        raw_in = [sem(f"raw_in{s}", 16 * RAW) for s in range(SLOTS)]
        wbc_in = [sem(f"wbc_in{s}", 64) for s in range(SLOTS)]
        hi_ok, lo_ok = sem("hi_ok", 4 * SLOTS), sem("lo_ok", 4 * SLOTS)
        g_ps, l_ps, y_ps = sem("g_ps", UNITS), sem("l_ps", UNITS), sem("y_ps", UNITS)
        sig_ok, sw_ok, a_ok, b_ok = sem("sig_ok", UNITS), sem("sw_ok", UNITS), sem("a_ok", UNITS), sem("b_ok", UNITS)
        f_ok, h_ok, l_ok = sem("f_ok", UNITS), sem("h_ok", UNITS), sem("l_ok", UNITS)
        zero_ok, th_ok, tl_ok, h_done = (ctx.enter_context(nc.semaphore(f"ex_{n}")) for n in (
            "zero_ok", "th_ok", "tl_ok", "h_done"))
        block = ctx.enter_context(nc.Block())

        def unit(k):
            k %= UNITS
            return k // (CHUNKS * TILES), k // TILES % CHUNKS, k % TILES

        def chunk(n):
            return slice(n * GN, (n + 1) * GN)

        def half_of(half, last, k):
            return half + (last and k >= UNITS)

        def steps(eng, body):
            for half in range(HALVES):
                first, end = half * LOOPS, (half + 1) * LOOPS
                if half:
                    body(first, half, True, False)
                with eng.Fori(first + (half > 0), end - 1) as it:
                    body(it, half, False, False)
                body(end - 1, half, False, True)

        def final(half, last):
            return last and half == HALVES - 1

        @block.sync
        def _(sp):
            credit(sp, *raw_in, *wbc_in)

            def raw(pair, s):
                p = bass.ds(pair, 1)
                for t, src in ((raw1[:, s, :], dram.w1a[p, :, :]), (raw2[0:HI, s, :], dram.w1b[p, :, :]),
                               (raw2[BH:BH + 1, s, :], dram.eb[p, 0:1, :]), (raw2[BL:BL + 1, s, :], dram.eb[p, 1:2, :]),
                               (raw3[:, s, :], dram.w2[p, :, :])):
                    sp.dma_start(t, src.rearrange("e p n -> (e p) n")).then_inc(raw_in[s].sem, 16)

            def routing(pair, half, s):
                for e, p0, p1, m in ((0, 0, 128, 0), (1, 0, 128, 1), (0, 0, 64, 2), (1, 64, 128, 2)):
                    row = dram.fw[bass.ds(pair * 2 + e, 1), half * HN:(half + 1) * HN]
                    sp.dma_start(wbc[p0:p1, s, m, :], bc(row, [p1 - p0, HN])).then_inc(wbc_in[s].sem, 16)

            sp.wait_ge(zero_ok, 1)
            for s in range(SLOTS):
                raw(s, s)
                routing(s, 0, s)

            def body(it, half, first, last):
                if final(half, last):
                    return
                for s in range(SLOTS):
                    pair = s if last else (it + 1 - half * LOOPS) * SLOTS + s
                    sp.wait_ge(*done(lo_ok, it, 4 * s + 3))
                    settle(sp, S)
                    raw(pair, s)
                    sp.wait_ge(*done(sw_ok, it, (s + 1) * CHUNKS * TILES - 1))
                    settle(sp, S)
                    routing(pair, half + last, s)

            steps(sp, body)

        @block.tensor
        def _(pe):
            credit(pe, g_ps, l_ps, y_ps)
            mm = nc.tensor.matmul

            def second_biases(half):
                for j in range(HB):
                    b = half * HB + j
                    if half and j % 2 == 0:
                        pe.wait_ge(h_done, j // 2 + 1)
                    mm(acc[j // 2][0:N, (j % 2) * D:(j % 2 + 1) * D], S.fwT[:, b * N:(b + 1) * N], S.b2[:],
                       start=(j % 2 == 0), stop=False, skip_group_check=True)

            def up(it, half, k):
                s, c, m = unit(k)
                pe.wait_ge(*done(lo_ok, it, 4 * SLOTS * (k // UNITS) + 4 * s + 3))
                cols = chunk(half * CHUNKS + c)
                for o, ok, free, base in ((gp, g_ps, a_ok, 0), (lp, l_ps, b_ok, TILES * 128)):
                    pe.wait_ge(*done(free, it, k - 2))
                    wc = slice(base + m * 128, base + (m + 1) * 128)
                    parts = [(h1, th1), (h1, tl1), (l1, th1), (hh2, thl2), (l2b, th2)]
                    for n, (wt, x) in enumerate(parts):
                        i = mm(o[k % 2][:, 0:GN], wt[:, s, wc], x[:, cols], start=(n == 0), stop=(n == len(parts) - 1))
                    i.then_inc(ok.sem, 1)

            def down(it, k):
                s, c, m = unit(k)
                pe.wait_ge(*done(h_ok, it, k))
                pe.wait_ge(*done(l_ok, it, k))
                wc = slice(m * D, (m + 1) * D)
                for j in range(G):
                    img = c * G + j
                    o = acc[img // 2][0:N, (img % 2) * D:(img % 2 + 1) * D]
                    x = slice(j * N, (j + 1) * N)
                    for a, wt in ((act_h, h3), (act_h, l3), (act_l, h3)):
                        i = mm(o, a[:, k % RING, x], wt[:, s, wc], start=False, stop=True, skip_group_check=True)
                i.then_inc(y_ps.sem, 1)

            second_biases(0)
            pe.wait_ge(tl_ok, 2)
            up(0, 0, 0)
            pe.wait_ge(tl_ok, 2 * CHUNKS)
            for k in range(1, AHEAD):
                up(0, 0, k)

            def body(it, half, first, last):
                for k in range(UNITS):
                    if last and not final(half, last) and k + AHEAD == UNITS:
                        pe.wait_ge(tl_ok, 2 * CHUNKS * HALVES)
                    if k + AHEAD < UNITS or not final(half, last):
                        up(it, half_of(half, last, k + AHEAD), k + AHEAD)
                    if first and k == 0:
                        second_biases(half)
                    down(it, k)

            steps(pe, body)

        @block.scalar
        def _(act):
            credit(act, sig_ok, h_ok, hi_ok)
            cp = nc.scalar.activation

            def inputs(n):
                for t, src in ((th1, S.t1[:]), (th2, S.t2[:]), (thl2[0:HI, :], S.t2[0:HI, :])):
                    cp(t[:, chunk(n)], src[:, chunk(n)], ACT.Copy).then_inc(th_ok, 1)

            def split(it, s, pieces):
                act.wait_ge(*done(raw_in[s], it, 16 * RAW - 1))
                for h, r in [(h1[:, s, :], raw1[:, s, :]), (hh2[0:HI, s, :], raw2[0:HI, s, :]),
                             (hh2[HI:2 * HI, s, :], raw2[0:HI, s, :]), (h3[:, s, :], raw3[:, s, :])][pieces]:
                    cp(h, r, ACT.Copy).then_inc(hi_ok.sem, 1)

            def sigmoid(it, k):
                act.wait_ge(*done(g_ps, it, k))
                act.wait_ge(*done(sw_ok, it, k - 2))
                cp(sg[:, k % 2, :], gp[k % 2][:, 0:GN], ACT.Sigmoid, scale=ALPHA).then_inc(sig_ok.sem, 1)

            inputs(0)
            split(0, 0, slice(0, 4))
            inputs(1)
            sigmoid(0, 0)
            sigmoid(0, 1)

            def body(it, half, first, last):
                for k in range(UNITS):
                    if k + 2 < UNITS or not final(half, last):
                        sigmoid(it, k + 2)
                    act.wait_ge(*done(f_ok, it, k))
                    act.wait_ge(*done(y_ps, it, k - RING))
                    act.wait_ge(*done(l_ok, it, k - RING))
                    cp(act_h[:, k % RING, :], act_f[:, k % 2, :], ACT.Copy).then_inc(h_ok.sem, 1)
                    if k < 2:
                        act.wait_ge(*done(y_ps, it, -1))
                        split(it, 1, slice(2 * k, 2 * k + 2))
                    if k in (6, 7) and not final(half, last):
                        act.wait_ge(*done(y_ps, it, 5))
                        split(it + 1, 0, slice(2 * k - 12, 2 * k - 10))
                    if last and half == 0 and k in (0, 1):
                        inputs(CHUNKS + k)

            steps(act, body)

        @block.vector
        def _(dve):
            credit(dve, sw_ok, a_ok, b_ok, lo_ok)
            nv = nc.vector

            def inputs(n):
                c = chunk(n)
                dve.wait_ge(th_ok, 3 * n + 1)
                nv.tensor_tensor(tl1[:, c], S.t1[:, c], th1[:, c].bitcast(F32), ALU.subtract).then_inc(tl_ok, 1)
                dve.wait_ge(th_ok, 3 * n + 3)
                nv.tensor_tensor(thl2[HI:2 * HI, c], S.t2[0:HI, c], th2[0:HI, c].bitcast(F32), ALU.subtract).then_inc(tl_ok, 1)

            def split(it, s, pieces):
                for n in pieces:
                    dve.wait_ge(*done(hi_ok, it, 4 * s + n))
                    if n == 2:
                        nv.tensor_copy(l2b[BH:BL + 1, s, :], raw2[BH:BL + 1, s, :]).then_inc(lo_ok.sem, 1)
                        continue
                    l, r, h = {0: (l1[:, s, :], raw1[:, s, :], h1[:, s, :]), 1: (l2b[0:HI, s, :], raw2[0:HI, s, :], hh2[0:HI, s, :]),
                               3: (l3[:, s, :], raw3[:, s, :], h3[:, s, :])}[n]
                    nv.tensor_tensor(l, r, h.bitcast(F32), ALU.subtract).then_inc(lo_ok.sem, 1)

            inputs(0)
            split(0, 0, range(4))
            inputs(1)

            def body(it, half, first, last):
                for k in range(UNITS):
                    s, c, m = unit(k)
                    if m == 0 and c == 0:
                        dve.wait_ge(*done(wbc_in[s], it, 63))
                    dve.wait_ge(*done(sig_ok, it, k))
                    nv.scalar_tensor_tensor(out=sw[:, k % 2, :], in0=sg[:, k % 2, :], scalar=SIG_LIMIT,
                                            in1=wbc[:, s, m, c * GN:(c + 1) * GN], op0=ALU.min, op1=ALU.mult
                                            ).then_inc(sw_ok.sem, 1)
                    dve.wait_ge(*done(l_ps, it, k))
                    dve.wait_ge(*done(f_ok, it, k - 2))
                    nv.tensor_scalar(bb[:, k % 2, :], lp[k % 2][:, 0:GN], LIMIT + 1.0, 1.0 - LIMIT, ALU.min, ALU.max
                                     ).then_inc(b_ok.sem, 1)
                    dve.wait_ge(*done(sw_ok, it, k))
                    nv.scalar_tensor_tensor(out=aa[:, k % 2, :], in0=gp[k % 2][:, 0:GN], scalar=LIMIT,
                                            in1=sw[:, k % 2, :], op0=ALU.min, op1=ALU.mult).then_inc(a_ok.sem, 1)
                    if k in (3, 4):
                        split(it, 1, range(2 * k - 6, 2 * k - 4))
                    if k in (9, 10) and not final(half, last):
                        split(it + 1, 0, range(2 * k - 18, 2 * k - 16))
                    if last and half == 0 and k in (5, 6):
                        inputs(CHUNKS + k - 5)
                    if first and k == AHEAD - 1:
                        take(0)

            def take(half):
                dve.wait_ge(*done(y_ps, (half + 1) * LOOPS - 1, UNITS - 1))
                for q in range(HB // 2):
                    h = S.H[0:N, half * HB + 2 * q:half * HB + 2 * q + 2, :]
                    nv.tensor_tensor(h, acc[q][0:N, 0:2 * D].rearrange("p (g n) -> p g n", g=2), h, ALU.add
                                     ).then_inc(h_done, 1)

            steps(dve, body)
            take(HALVES - 1)

        @block.gpsimd
        def _(pool):
            credit(pool, f_ok, l_ok)
            nc.gpsimd.memset(raw2[BH:BL + 1, :, :], 0.0).then_inc(zero_ok, 1)

            def product(it, k):
                pool.wait_ge(*done(a_ok, it, k))
                pool.wait_ge(*done(h_ok, it, k - 2))
                pool.wait_ge(*done(l_ok, it, k - 2))
                nc.gpsimd.tensor_tensor(act_f[:, k % 2, :], aa[:, k % 2, :], bb[:, k % 2, :], ALU.mult).then_inc(f_ok.sem, 1)

            product(0, 0)

            def body(it, half, first, last):
                for k in range(UNITS):
                    if k + 1 < UNITS or not final(half, last):
                        product(it, k + 1)
                    pool.wait_ge(*done(h_ok, it, k))
                    nc.gpsimd.tensor_tensor(act_l[:, k % RING, :], act_f[:, k % 2, :], act_h[:, k % RING, :].bitcast(F32),
                                            ALU.subtract).then_inc(l_ok.sem, 1)

            steps(pool, body)


def attn1_phase(nc, dram, S):
    HEADS, HD, GROUPS = 8, D // 8, 2
    GD = D // GROUPS
    SCALE = float(HD) ** -0.5
    UNITS = [0, "g0", 1, 2, 3, 4, "g1", 5, 6, 7]
    NU = len(UNITS)
    GROUP_LINEAR, NEXT_NORM = 4, 5
    with ExitStack() as ctx:
        def sb(name, shape, dt=F32):
            return ctx.enter_context(nc.sbuf_tensor("a1_" + name, shape, dt))

        def sem(name, per):
            return counted(nc, ctx, "a1_" + name, per)

        w = W1
        xn = sb("xn", [N, G, D])
        stats, mv, veps, rstd = sb("stats", [N, G, 6]), sb("mv", [N, G, 2]), sb("veps", [N, G]), sb("rstd", [N, G])
        xa, xb, cur = sb("xa", [GD, G, N]), sb("xb", [GD, G, N]), sb("cur", [GD, G, N])
        q, k = sb("q", [128, 2, GN]), sb("k", [128, 2, GN])
        v = S.a1_v
        gq, gk, gv = sb("gq", [GD, GN]), sb("gk", [GD, GN]), sb("gv", [N, G, GD])
        p, pT, mx = sb("p", [N, 2, G, N]), sb("pT", [N, 2, G, N]), sb("mx", [N, 2, G])
        rs, ri = sb("rs", [N, G]), sb("ri", [N, G])
        hx = sb("hx", [GD, GROUPS, GN])
        den, o = sb("den", [N, G, HEADS]), sb("o", [N, G, D])
        out0, out1 = sb("out0", [GD, GN]), S.a1_out1
        bank = [ctx.enter_context(nc.psum_tensor(f"a1_ps{i}", [128, 512], F32)) for i in range(8)]
        A, V, SC, PT, O = bank[0:1], bank[1:3], bank[3:5], bank[5], bank[6:8]

        stat_ok, mean_ok, veps_ok, rstd_ok, xn_ok = sem("stat_ok", 4), sem("mean_ok", 4), sem("veps_ok", 1), sem("rstd_ok", 1), sem("xn_ok", 4)
        a_ps, a_out = sem("a_ps", 5), sem("a_out", 5)
        v_ps, v_out = sem("v_ps", 11), sem("v_out", 11)
        z_ps, z_out = sem("z_ps", 4), sem("z_out", 4)
        sc_ps, mx_ok, sub_ok, exp_ok = sem("sc_ps", NU), sem("mx_ok", NU), sem("sub_ok", NU), sem("exp_ok", NU)
        sum_ok, rec_ok, nrm_ok = sem("sum_ok", 2), sem("rec_ok", 2), sem("nrm_ok", 2)
        pt_ps, pt_out, pv_ps = sem("pt_ps", NU), sem("pt_out", NU), sem("pv_ps", HEADS)
        den_ok, o_ok = sem("den_ok", 2), sem("o_ok", 2)
        block = ctx.enter_context(nc.Block())
        A_X, A_Q, A_K, A_GQ0, A_GQ1 = range(5)
        V_X, V_Q, V_K, V_GK0, V_V, _, V_GV0, V_HX0, V_GK1, V_GV1, V_HX1 = range(11)
        Z_O, _, Z_H, _ = range(4)

        def rows(it):
            return S.H[0:N, :, :].rearrange("p b d -> p (b d)")[:, bass.ds(it * (G * D), G * D)].rearrange(
                "p (b d) -> p b d", b=G)

        def steps(eng, first, body):
            first()
            with eng.Fori(0, STEPS - 1) as it:
                body(it, False)
            body(STEPS - 1, True)

        def images(ap):
            return ap.rearrange("p (g n) -> p g n", g=G)

        @block.sync
        def _(sp):
            for t, src in S.late_loads:
                sp.dma_start(t, src).then_inc(S.late_in, 16)
            sp.wait_ge(S.late_in, 16 * len(S.late_loads))

        @block.tensor
        def _(pe):
            credit(pe, a_ps, v_ps, z_ps, sc_ps, pt_ps, pv_ps)
            mm = nc.tensor.matmul

            def fill(tiles, out, it, n):
                pe.wait_ge(*done(out, it, before(n, len(tiles), out.per)))
                return tiles[n % len(tiles)]

            def linear(o, wcol, cols, xs):
                for i, x in enumerate(xs):
                    m = mm(o, S.w1w[0:GD, i, wcol:wcol + cols], x, start=(i == 0), stop=(i == len(xs) - 1))
                return m

            def group_linear(it, i, x, nq, nk, nv):
                for tiles, ps, out, n, c in ((A, a_ps, a_out, nq, 0), (V, v_ps, v_out, nk, GD)):
                    o = fill(tiles, out, it, n)
                    mm(o[0:GD, 0:GN], S.w1g[0:GD, i, c:c + GD], x[:], start=True, stop=True).then_inc(ps.sem, 1)
                o = fill(V, v_out, it, nv)
                for j in range(G):
                    m = mm(o[0:N, j * GD:(j + 1) * GD], x[:, j, :], S.w1g[0:GD, i, 2 * GD:3 * GD], start=True, stop=True)
                m.then_inc(v_ps.sem, 1)

            def pre(it):
                for tiles, ps, out, n, c in ((A, a_ps, a_out, A_X, 0), (V, v_ps, v_out, V_X, GD)):
                    o = fill(tiles, out, it, n)
                    for j in range(G):
                        if c == 0:
                            pe.wait_ge(*done(xn_ok, it, j))
                        m = nc.tensor.transpose(o[0:GD, j * N:(j + 1) * N], xn[:, j, c:c + GD], S.ident[0:N, 0:N])
                    m.then_inc(ps.sem, 1)
                pe.wait_ge(*done(a_out, it, A_X))
                pe.wait_ge(*done(v_out, it, V_X))
                x = (xa[:], xb[:])
                for n, col in ((0, w.q), (1, w.k)):
                    for t, (tiles, ps, out, nn) in enumerate(((A, a_ps, a_out, A_Q + n), (V, v_ps, v_out, V_Q + n))):
                        linear(fill(tiles, out, it, nn)[:, 0:GN], col + 128 * t, 128, x).then_inc(ps.sem, 1)
                o = fill(A, a_out, it, A_GQ0)
                mm(o[0:GD, 0:GN], S.w1g[0:GD, 0, 0:GD], xa[:], start=True, stop=True).then_inc(a_ps.sem, 1)
                o = fill(V, v_out, it, V_GK0)
                mm(o[0:GD, 0:GN], S.w1g[0:GD, 0, GD:2 * GD], xa[:], start=True, stop=True).then_inc(v_ps.sem, 1)
                for h in range(2):
                    o = fill(V, v_out, it, V_V + h)
                    for j in (2 * h, 2 * h + 1):
                        c = (j % 2) * D
                        mm(o[0:N, c:c + D], xa[:, j, :], S.w1w[0:GD, 0, w.v:w.v + D], start=True, stop=False)
                        m = mm(o[0:N, c:c + D], xb[:, j, :], S.w1w[0:GD, 1, w.v:w.v + D], start=False, stop=True)
                    m.then_inc(v_ps.sem, 1)
                o = fill(V, v_out, it, V_GV0)
                for j in range(G):
                    m = mm(o[0:N, j * GD:(j + 1) * GD], xa[:, j, :], S.w1g[0:GD, 0, 2 * GD:3 * GD], start=True, stop=True)
                m.then_inc(v_ps.sem, 1)

            def scores(it, n):
                u = UNITS[n]
                pe.wait_ge(*done(sub_ok, it, n - 2))
                if n < 2:
                    pe.wait_ge(*done(z_out, it, n - 2))
                o = SC[n % 2]
                if u in ("g0", "g1"):
                    g0 = u == "g0"
                    pe.wait_ge(*done(a_out, it, A_GQ0 if g0 else A_GQ1))
                    pe.wait_ge(*done(v_out, it, V_GK0 if g0 else V_GK1))
                    for j in range(G):
                        c = slice(j * N, (j + 1) * N)
                        m = mm(o[0:N, c], gq[:, c], gk[:, c], start=True, stop=True)
                else:
                    t, r = u // 4, 32 * (u % 4)
                    if t == 0:
                        pe.wait_ge(*done(a_out, it, A_K))
                    else:
                        pe.wait_ge(*done(v_out, it, V_K))
                    for j in range(G):
                        c = slice(j * N, (j + 1) * N)
                        m = mm(o[0:N, c], q[r:r + HD, t, c], k[r:r + HD, t, c], start=True, stop=True,
                               tile_position=(r, 0))
                m.then_inc(sc_ps.sem, 1)

            def turn(it, n):
                u = UNITS[n]
                if u in ("g0", "g1"):
                    pe.wait_ge(*done(nrm_ok, it, int(u == "g1")))
                else:
                    pe.wait_ge(*done(exp_ok, it, n))
                pe.wait_ge(*done(pt_out, it, n - 1))
                for j in range(G):
                    m = nc.tensor.transpose(PT[0:N, j * N:(j + 1) * N], p[:, n % 2, j, :], S.ident[0:N, 0:N])
                m.then_inc(pt_ps.sem, 1)

            def values(it, n):
                u = UNITS[n]
                pe.wait_ge(*done(pt_out, it, n))
                if u in ("g0", "g1"):
                    nn = V_HX0 if u == "g0" else V_HX1
                    pe.wait_ge(*done(v_out, it, V_GV0 if u == "g0" else V_GV1))
                    o = fill(V, v_out, it, nn)
                    for j in range(G):
                        m = mm(o[0:GD, j * N:(j + 1) * N], gv[:, j, :], pT[:, n % 2, j, :], start=True, stop=True)
                    m.then_inc(v_ps.sem, 1)
                    return
                if u == 0:
                    pe.wait_ge(*done(o_ok, it, -1))
                    pe.wait_ge(*done(v_out, it, V_V + 1))
                for j in range(G):
                    c = (j % 2) * HEADS * (HD + 1) + u * (HD + 1)
                    m = mm(O[j // 2][0:N, c:c + HD + 1], pT[:, n % 2, j, :], v[:, j, u, :], start=True, stop=True)
                m.then_inc(pv_ps.sem, 1)

            def tail(it):
                pe.wait_ge(*done(o_ok, it, 1))
                for i in range(GROUPS):
                    pe.wait_ge(*done(sub_ok, it, NU - 1))
                    for j in range(G):
                        m = nc.tensor.transpose(SC[i][0:GD, j * N:(j + 1) * N], o[:, j, i * GD:(i + 1) * GD], S.ident[0:N, 0:N])
                    m.then_inc(z_ps.sem, 1)
                pe.wait_ge(*done(z_out, it, Z_O + 1))
                for h in range(2):
                    for j in (2 * h, 2 * h + 1):
                        c, t = (j % 2) * D, slice(j * N, (j + 1) * N)
                        mm(SC[h][0:N, c:c + D], out0[:, t], S.w1w[0:GD, 0, w.o:w.o + D], start=True, stop=False)
                        m = mm(SC[h][0:N, c:c + D], out1[:, t], S.w1w[:, 1, w.o:w.o + D], start=False, stop=True)
                    m.then_inc(z_ps.sem, 1)

            def body(it, last):
                for n in range(NU + 2):
                    if n < NU:
                        scores(it, n)
                    if 0 <= n - 1 < NU:
                        turn(it, n - 1)
                    if n - 2 >= 0:
                        values(it, n - 2)
                    if n == GROUP_LINEAR:
                        pe.wait_ge(*done(v_out, it, V_HX0))
                        group_linear(it, 1, cur, A_GQ1, V_GK1, V_GV1)
                if not last:
                    pre(it + 1)
                tail(it)

            steps(pe, lambda: pre(0), body)

        @block.scalar
        def _(act):
            credit(act, a_out, exp_ok, pt_out)
            cp = nc.scalar.activation

            def evac(it, n, out, rows_):
                act.wait_ge(*done(a_ps, it, n))
                cp(out, A[n % len(A)][0:rows_, 0:GN], ACT.Copy).then_inc(a_out.sem, 1)

            def pre(it):
                evac(it, A_X, xa[:], GD)
                evac(it, A_Q, q[:, 0, :], 128)
                evac(it, A_K, k[:, 0, :], 128)
                evac(it, A_GQ0, gq[:], GD)

            def body(it, last):
                for n in range(NU + 1):
                    if n < NU:
                        act.wait_ge(*done(sub_ok, it, n))
                        cp(p[:, n % 2, :, :], p[:, n % 2, :, :], ACT.Exp, scale=SCALE).then_inc(exp_ok.sem, 1)
                    if n - 1 >= 0:
                        act.wait_ge(*done(pt_ps, it, n - 1))
                        cp(pT[:, (n - 1) % 2, :, :], PT[0:N, 0:GN], ACT.Copy).then_inc(pt_out.sem, 1)
                    if n == GROUP_LINEAR + 1:
                        evac(it, A_GQ1, gq[:], GD)
                if not last:
                    pre(it + 1)

            steps(act, lambda: pre(0), body)

        @block.gpsimd
        def _(pool):
            credit(pool, veps_ok, rstd_ok)

            def pre(it):
                pool.wait_ge(*done(mean_ok, it, 3))
                settle(pool, S)
                nc.gpsimd.tensor_scalar(veps[:], mv[:, :, 1], 1.0, EPS, ALU.mult, ALU.add).then_inc(veps_ok.sem, 1)
                pool.wait_ge(*done(veps_ok, it, 0))
                nc.gpsimd.tensor_tensor(rstd[:], veps[:], S.mhalf[0:N, 0:G], ALU.pow).then_inc(rstd_ok.sem, 1)

            def body(it, last):
                if not last:
                    pre(it + 1)

            for n, t in enumerate(S.late_ones):
                if n:
                    pool.wait_ge(S.late_ones_ok, n)
                nc.gpsimd.memset(t, 1.0).then_inc(S.late_ones_ok, 1)
            steps(pool, lambda: pre(0), body)

        @block.vector
        def _(dve):
            credit(dve, stat_ok, mean_ok, xn_ok, v_out, z_out, mx_ok, sub_ok, sum_ok, rec_ok, nrm_ok, den_ok, o_ok)
            nv = nc.vector

            def stat(it):
                hg = rows(it)
                settle(dve, S)
                for j in range(G):
                    nv.bn_stats(stats[:, j, :], hg[:, j, :]).then_inc(stat_ok.sem, 1)
                dve.wait_ge(*done(stat_ok, it, 3))
                settle(dve, S)
                for j in range(G):
                    nv.bn_aggr(mv[:, j, :], stats[:, j, :]).then_inc(mean_ok.sem, 1)

            def norm(it):
                hg = rows(it)
                dve.wait_ge(*done(mean_ok, it, 3))
                dve.wait_ge(*done(rstd_ok, it, 0))
                dve.wait_ge(*done(v_ps, it, V_X - v_ps.per))
                for j in range(G):
                    nv.tensor_scalar(xn[:, j, :], hg[:, j, :], mv[:, j, 0:1], rstd[:, j:j + 1],
                                     ALU.subtract, ALU.mult).then_inc(xn_ok.sem, 1)

            def evac(it, n, out, rows_, wd, shape=None):
                dve.wait_ge(*done(v_ps, it, n))
                i = V[n % len(V)][0:rows_, 0:wd]
                nv.tensor_copy(out, i.rearrange(*shape[0:1], **shape[1]) if shape else i).then_inc(v_out.sem, 1)

            per_image = ("p (g n) -> p g n", {"g": G})

            def pre(it):
                evac(it, V_X, xb[:], GD, GN, per_image)
                evac(it, V_Q, q[:, 1, :], 128, GN)
                evac(it, V_K, k[:, 1, :], 128, GN)
                evac(it, V_GK0, gk[:], GD, GN)
                for h in range(2):
                    evac(it, V_V + h, v[:, 2 * h:2 * h + 2, :, 0:HD], N, 2 * D, ("p (g h d) -> p g h d", {"g": 2, "h": HEADS}))
                evac(it, V_GV0, gv[:], N, G * GD, per_image)

            def softmax_in(it, n):
                sc = images(SC[n % 2][0:N, 0:GN])
                dve.wait_ge(*done(sc_ps, it, n))
                nv.tensor_reduce(mx[:, n % 2, :], sc, AX.X, ALU.max).then_inc(mx_ok.sem, 1)
                dve.wait_ge(*done(mx_ok, it, n))
                dve.wait_ge(*done(pt_ps, it, n - 2))
                nv.tensor_tensor(p[:, n % 2, :, :], sc, bc(mx[:, n % 2, :].unsqueeze(2), [N, G, N]), ALU.subtract
                                 ).then_inc(sub_ok.sem, 1)

            def normalise(it, n, i):
                pp = p[:, n % 2, :, :]
                dve.wait_ge(*done(exp_ok, it, n))
                nv.tensor_reduce(rs[:], pp, AX.X, ALU.add).then_inc(sum_ok.sem, 1)
                dve.wait_ge(*done(sum_ok, it, i))
                nv.reciprocal(ri[:], rs[:]).then_inc(rec_ok.sem, 1)
                dve.wait_ge(*done(rec_ok, it, i))
                nv.tensor_tensor(pp, pp, bc(ri[:].unsqueeze(2), [N, G, N]), ALU.mult).then_inc(nrm_ok.sem, 1)

            def first():
                stat(0)
                norm(0)
                pre(0)

            def body(it, last):
                hg = rows(it)
                for n in range(NU + 2):
                    if n < NU:
                        softmax_in(it, n)
                        if UNITS[n] in ("g0", "g1"):
                            normalise(it, n, int(UNITS[n] == "g1"))
                    if n == 3:
                        dve.wait_ge(*done(v_ps, it, V_HX0))
                        hx0 = V[V_HX0 % len(V)][0:GD, 0:GN]
                        nv.tensor_tensor(cur[:], images(hx0), xb[:], ALU.add)
                        nv.tensor_copy(hx[:, 0, :], hx0).then_inc(v_out.sem, 1)
                    if n == GROUP_LINEAR + 1:
                        evac(it, V_GK1, gk[:], GD, GN)
                        evac(it, V_GV1, gv[:], N, G * GD, per_image)
                    if n == NEXT_NORM and not last:
                        stat(it + 1)
                    if n == NEXT_NORM + 2 and not last:
                        norm(it + 1)
                    if n == 8:
                        evac(it, V_HX1, hx[:, 1, :], GD, GN)
                dve.wait_ge(*done(pv_ps, it, HEADS - 1))
                for h in range(2):
                    oo = O[h][0:N, 0:2 * HEADS * (HD + 1)].rearrange("p (g h d) -> p g h d", g=2, h=HEADS)
                    nv.reciprocal(den[:, 2 * h:2 * h + 2, :], oo[:, :, :, HD]).then_inc(den_ok.sem, 1)
                for h in range(2):
                    oo = O[h][0:N, 0:2 * HEADS * (HD + 1)].rearrange("p (g h d) -> p g h d", g=2, h=HEADS)
                    dve.wait_ge(*done(den_ok, it, h))
                    if h == 0:
                        dve.wait_ge(*done(z_ps, it, Z_O + 1 - z_ps.per))
                    nv.tensor_tensor(o[:, 2 * h:2 * h + 2, :].rearrange("p g (h d) -> p g h d", h=HEADS), oo[:, :, :, 0:HD],
                                     bc(den[:, 2 * h:2 * h + 2, :].unsqueeze(3), [N, 2, HEADS, HD]), ALU.mult
                                     ).then_inc(o_ok.sem, 1)
                if not last:
                    pre(it + 1)
                for i, out in enumerate((out0[:], out1[0:GD, :])):
                    dve.wait_ge(*done(z_ps, it, Z_O + i))
                    nv.tensor_tensor(out, SC[i][0:GD, 0:GN], hx[:, i, :], ALU.add).then_inc(z_out.sem, 1)
                for h in range(2):
                    dve.wait_ge(*done(z_ps, it, Z_H + h))
                    hh = hg[:, 2 * h:2 * h + 2, :]
                    nv.tensor_tensor(hh, SC[h][0:N, 0:2 * D].rearrange("p (g n) -> p g n", g=2), hh, ALU.add
                                     ).then_inc(z_out.sem, 1)

            steps(dve, first, body)


def ffn1_phase(nc, dram, S):
    HEADS, HD, MLP, RHD = 12, D // 12, 768, 128
    NU, KF = HEADS, MLP // 128
    NEXT_NORM = 2
    with ExitStack() as ctx:
        def sb(name, shape, dt=F32):
            return ctx.enter_context(nc.sbuf_tensor("f_" + name, shape, dt))

        def sem(name, per):
            return counted(nc, ctx, "f_" + name, per)

        w, c = W4, C4
        stats, mv, veps, rstd = sb("stats", [N, 3, G, 6]), sb("mv", [N, 3, G, 2]), sb("veps", [N, 3, G]), sb("rstd", [N, 3, G])
        xnext, x, z, hh, y = (sb(n, [N, G, D]) for n in ("xnext", "x", "z", "hh", "y"))
        xa1, xa2, r1, r2 = sb("xa1", [LO, G, N]), S.f_xa2, sb("r1", [LO, GN]), sb("r2", [HI, GN])
        e, gm, gs = sb("e", [RHD, G, N]), sb("gm", [RHD, G]), sb("gs", [RHD, G])
        h1, h2 = sb("h1", [RHD, GN]), S.f_h2
        logit, bits, nbits, sel = sb("logit", [N, G, 4]), sb("bits", [N, G, 2]), sb("nbits", [N, G, 2]), sb("sel", [N, G, 3])
        q, k, v = sb("q", [128, 3, GN]), sb("k", [128, 3, GN]), S.f_v
        p, pT, mx = sb("p", [N, 2, G, N]), sb("pT", [N, 2, G, N]), sb("mx", [N, 2, G])
        den, o = sb("den", [N, G, HEADS]), sb("o", [N, G, D])
        o1, o2 = sb("o1", [LO, GN]), S.f_o2
        xf1, xf2, ff = sb("xf1", [LO, GN]), sb("xf2", [HI, GN]), sb("ff", [128, KF, GN])
        u1, u2, dn, d1, d2 = sb("u1", [LO, GN]), sb("u2", [HI, GN]), sb("dn", [N, G, 3, D // 3]), sb("d1", [LO, GN]), sb("d2", [HI, GN])
        bank = [ctx.enter_context(nc.psum_tensor(f"f_ps{i}", [128, 512], F32)) for i in range(8)]
        A, V, SC, PT, O = bank[0:1], bank[1:3], bank[3:5], bank[5], bank[6:8]
        ZA, ZV = (SC[0], PT, O[0]), (SC[1], O[1])

        stat_ok, mean_ok = [sem(f"stat_ok{i}", 4) for i in range(3)], [sem(f"mean_ok{i}", 4) for i in range(3)]
        veps_ok, rstd_ok = [sem(f"veps_ok{i}", 1) for i in range(3)], [sem(f"rstd_ok{i}", 1) for i in range(3)]
        x_ok, z_ok, y_ok, xcopy_ok, hx_ok = sem("x_ok", 4), sem("z_ok", 4), sem("y_ok", 4), sem("xcopy_ok", 1), sem("hx_ok", 1)
        a_ps, a_out, v_ps, v_out = sem("a_ps", 7), sem("a_out", 7), sem("v_ps", 7), sem("v_out", 7)
        za_ps, za_out, zv_ps, zv_out = sem("za_ps", 10), sem("za_out", 10), sem("zv_ps", 12), sem("zv_out", 12)
        gm_ok, gs_ok, bit_ok, nb_ok, sel_ok = sem("gm_ok", 1), sem("gs_ok", 1), sem("bit_ok", 2), sem("nb_ok", 1), sem("sel_ok", 3)
        sc_ps, mx_ok, sub_ok, exp_ok = sem("sc_ps", NU), sem("mx_ok", NU), sem("sub_ok", NU), sem("exp_ok", NU)
        pt_ps, pt_out, pv_ps = sem("pt_ps", NU), sem("pt_out", NU), sem("pv_ps", NU)
        den_ok, o_ok = sem("den_ok", 2), sem("o_ok", 2)
        hh_ok, out_ok = sem("hh_ok", 4), sem("out_ok", 4)
        stored = sem("stored", 16)
        block = ctx.enter_context(nc.Block())
        A_Z, A_Q0, A_Q2, A_K1, A_R, A_H1, A_H2 = range(7)
        V_Z, V_Q1, V_K0, V_K2, V_V, _, V_L = range(7)
        ZA_O, ZA_Y, ZA_F, ZA_U, ZA_D = 0, 1, 2, 8, 9
        ZV_O, ZV_WO, ZV_Y, ZV_F, ZV_U, ZV_DN, ZV_D, ZV_UP = 0, 1, 3, 4, 6, 7, 9, 10

        def rows(it):
            return S.H[0:N, :, :].rearrange("p b d -> p (b d)")[:, bass.ds(it * (G * D), G * D)].rearrange(
                "p (b d) -> p b d", b=G)

        def steps(eng, first, body):
            first()
            with eng.Fori(0, STEPS - 1) as it:
                body(it, False)
            body(STEPS - 1, True)

        def images(ap, g=G):
            return ap.rearrange("p (g n) -> p g n", g=g)

        @block.sync
        def _(sp):
            credit(sp, stored)

            def body(it, last):
                sp.wait_ge(*done(zv_out, it, ZV_UP + 1))
                settle(sp, S)
                sp.dma_start(dram.out[bass.ds(it * G, G), :, :].rearrange("b t d -> t b d"), rows(it)).then_inc(stored.sem, 16)

            steps(sp, lambda: None, body)
            sp.wait_ge(*done(stored, STEPS - 1, 15))

        @block.tensor
        def _(pe):
            credit(pe, a_ps, v_ps, za_ps, zv_ps, sc_ps, pt_ps, pv_ps)
            mm = nc.tensor.matmul

            def fill(tiles, out, it, n, ready=-100):
                pe.wait_ge(*done(out, it, max(before(n, len(tiles), out.per), ready)))
                return tiles[n % len(tiles)]

            def linear(o, lo, hi, xs):
                mm(o, lo, xs[0], start=True, stop=False)
                return mm(o, hi, xs[1], start=False, stop=True)

            def cols(col, n):
                return S.w4a[:, col:col + n], S.w4b[0:HI, col:col + n]

            def transposed(o, src, c0, c1, ok, it):
                if ok is None:
                    settle(pe, S)
                for j in range(G):
                    if ok is not None:
                        pe.wait_ge(*done(ok, it, j))
                    m = nc.tensor.transpose(o[0:c1 - c0, j * N:(j + 1) * N], src[:, j, c0:c1], S.ident[0:N, 0:N])
                return m

            def by_image(o, h, lo, hi, col, hi_rows):
                for j in (2 * h, 2 * h + 1):
                    t = slice(j * N, (j + 1) * N)
                    m = linear(o[0:N, (j % 2) * D:(j % 2 + 1) * D], lo[:, t], hi[:, t],
                               (S.w4a[:, col:col + D], S.w4b[0:hi_rows, col:col + D]))
                return m

            def pre1(it):
                transposed(fill(A, a_out, it, A_Z), z, 0, LO, z_ok, it).then_inc(a_ps.sem, 1)
                transposed(fill(V, v_out, it, V_Z), z, LO, D, None, it).then_inc(v_ps.sem, 1)
                pe.wait_ge(*done(a_out, it, A_Z))
                pe.wait_ge(*done(v_out, it, V_Z))
                xs = (xa1[:], xa2[0:HI, :])
                for n, a, col in ((A_Q0, True, w.q), (V_Q1, False, w.q + 128), (A_Q2, True, w.q + 256),
                                  (V_K0, False, w.k), (A_K1, True, w.k + 128), (V_K2, False, w.k + 256)):
                    o_ = fill(A, a_out, it, n) if a else fill(V, v_out, it, n)
                    linear(o_[:, 0:GN], *cols(col, 128), xs).then_inc((a_ps if a else v_ps).sem, 1)

            def pre2(it):
                linear(fill(A, a_out, it, A_R)[:, 0:GN], *cols(w.r, RHD), (r1[:], r2[:])).then_inc(a_ps.sem, 1)
                xaf = (xa1[:].rearrange("p g n -> p (g n)"), xa2[:])
                for h in range(2):
                    by_image(fill(V, v_out, it, V_V + h), h, *xaf, w.v, HI + 1).then_inc(v_ps.sem, 1)

            def pre3(it):
                pe.wait_ge(*done(a_out, it, A_R))
                pe.wait_ge(*done(gs_ok, it, 0))
                o_ = fill(A, a_out, it, A_H1)[:, 0:GN]
                mm(o_, S.ro1[:, 0, :], e[:], start=True, stop=False)
                mm(images(o_), S.ro1[:, 1, :], bc(gs[:].unsqueeze(2), [RHD, G, N]), start=False, stop=True).then_inc(a_ps.sem, 1)

            def pre4(it):
                pe.wait_ge(*done(a_out, it, A_H1))
                o_ = fill(A, a_out, it, A_H2)[0:RHD // 2, 0:GN]
                mm(o_, S.ro2[:], h1[:], start=True, stop=True).then_inc(a_ps.sem, 1)

            def logits(it):
                pe.wait_ge(*done(a_out, it, A_H2))
                o_ = fill(V, v_out, it, V_L)
                for j in range(G):
                    m = mm(o_[0:N, 4 * j:4 * j + 4], h2[:, j * N:(j + 1) * N], S.ro3[:], start=True, stop=True)
                m.then_inc(v_ps.sem, 1)

            def scores(it, n):
                pe.wait_ge(*done(sub_ok, it, n - 2))
                if n == 0:
                    pe.wait_ge(*done(za_out, it, -1))
                    pe.wait_ge(*done(zv_out, it, -1))
                    pe.wait_ge(*done(a_out, it, A_K1))
                    pe.wait_ge(*done(v_out, it, V_K2))
                t, r = n // 4, 32 * (n % 4)
                for j in range(G):
                    s = slice(j * N, (j + 1) * N)
                    m = mm(SC[n % 2][0:N, s], q[r:r + HD, t, s], k[r:r + HD, t, s], start=True, stop=True, tile_position=(r, 0))
                m.then_inc(sc_ps.sem, 1)

            def turn(it, n):
                pe.wait_ge(*done(exp_ok, it, n))
                pe.wait_ge(*done(pt_out, it, n - 1))
                for j in range(G):
                    m = nc.tensor.transpose(PT[0:N, j * N:(j + 1) * N], p[:, n % 2, j, :], S.ident[0:N, 0:N])
                m.then_inc(pt_ps.sem, 1)

            def values(it, n):
                pe.wait_ge(*done(pt_out, it, n))
                if n == 0:
                    pe.wait_ge(*done(v_out, it, V_V + 1))
                for j in range(G):
                    cc = (j % 2) * HEADS * (HD + 1) + n * (HD + 1)
                    m = mm(O[j // 2][0:N, cc:cc + HD + 1], pT[:, n % 2, j, :], v[:, j, n, :], start=True, stop=True)
                m.then_inc(pv_ps.sem, 1)

            def tail_heads(it):
                pe.wait_ge(*done(sub_ok, it, NU - 1))
                pe.wait_ge(*done(o_ok, it, 1))
                transposed(fill(ZA, za_out, it, ZA_O), o, 0, LO, None, it).then_inc(za_ps.sem, 1)
                transposed(fill(ZV, zv_out, it, ZV_O), o, LO, D, None, it).then_inc(zv_ps.sem, 1)

            def tail_wo(it):
                pe.wait_ge(*done(za_out, it, ZA_O))
                for h in range(2):
                    by_image(fill(ZV, zv_out, it, ZV_WO + h, ZV_O), h, o1[:], o2[:], w.o, HI + 1).then_inc(zv_ps.sem, 1)

            def tail_mlp(it):
                transposed(fill(ZA, za_out, it, ZA_Y), y, 0, LO, y_ok, it).then_inc(za_ps.sem, 1)
                transposed(fill(ZV, zv_out, it, ZV_Y), y, LO, D, None, it).then_inc(zv_ps.sem, 1)
                pe.wait_ge(*done(zv_out, it, ZV_Y))
                for f in range(KF):
                    linear(fill(ZA, za_out, it, ZA_F + f, ZA_Y)[:, 0:GN], *cols(w.f + 128 * f, 128), (xf1[:], xf2[:])).then_inc(za_ps.sem, 1)
                for h in range(2):
                    o_ = fill(ZV, zv_out, it, ZV_F + h)
                    for j in (2 * h, 2 * h + 1):
                        oo = o_[0:N, (j % 2) * D:(j % 2 + 1) * D]
                        mm(oo, S.ones1[:], S.fc2b[:], start=True, stop=False)
                        for f in range(KF):
                            if h == 0 and j == 0:
                                pe.wait_ge(*done(za_out, it, ZA_F + f))
                            m = mm(oo, ff[:, f, j * N:(j + 1) * N], S.fc2[:, f, :], start=False, stop=(f == KF - 1))
                    m.then_inc(zv_ps.sem, 1)

            def tail_lra(it):
                transposed(fill(ZA, za_out, it, ZA_U), hh, 0, LO, out_ok, it).then_inc(za_ps.sem, 1)
                transposed(fill(ZV, zv_out, it, ZV_U), hh, LO, D, None, it).then_inc(zv_ps.sem, 1)
                pe.wait_ge(*done(za_out, it, ZA_U))
                for h in range(2):
                    by_image(fill(ZV, zv_out, it, ZV_DN + h, ZV_U), h, u1[:], u2[:], w.dn, HI).then_inc(zv_ps.sem, 1)
                pe.wait_ge(*done(zv_out, it, ZV_DN + 1))
                dd = dn[:].rearrange("p g k r -> p g (k r)")
                transposed(fill(ZA, za_out, it, ZA_D), dd, 0, LO, None, it).then_inc(za_ps.sem, 1)
                transposed(fill(ZV, zv_out, it, ZV_D), dd, LO, D, None, it).then_inc(zv_ps.sem, 1)
                pe.wait_ge(*done(za_out, it, ZA_D))
                for h in range(2):
                    by_image(fill(ZV, zv_out, it, ZV_UP + h, ZV_D), h, d1[:], d2[:], w.up, HI).then_inc(zv_ps.sem, 1)

            def first():
                pre1(0)
                pre2(0)
                pre3(0)
                pre4(0)

            def body(it, last):
                for n in range(NU + 2):
                    if n < NU:
                        scores(it, n)
                    if n == 1:
                        logits(it)
                    if 0 <= n - 1 < NU:
                        turn(it, n - 1)
                    if n - 2 >= 0:
                        values(it, n - 2)
                if not last:
                    pre1(it + 1)
                tail_heads(it)
                if not last:
                    pre2(it + 1)
                tail_wo(it)
                if not last:
                    pre3(it + 1)
                    pre4(it + 1)
                tail_mlp(it)
                tail_lra(it)

            steps(pe, first, body)

        @block.scalar
        def _(act):
            credit(act, a_out, za_out, exp_ok, pt_out)
            cp = nc.scalar.activation

            def one(it, n, out, rows_, func, **kw):
                act.wait_ge(*done(a_ps, it, n))
                cp(out, A[n % len(A)][0:rows_, 0:GN], func, **kw).then_inc(a_out.sem, 1)

            def za(it, n, out, rows_, func=ACT.Copy, **kw):
                act.wait_ge(*done(za_ps, it, n))
                cp(out, ZA[n % len(ZA)][0:rows_, 0:GN], func, **kw).then_inc(za_out.sem, 1)

            def col(i):
                return S.c4a[:, i:i + 1]

            def pre1(it):
                act.wait_ge(*done(a_ps, it, A_Z))
                cp(r1[:], A[0][0:LO, 0:GN], ACT.Identity, scale=col(c.rg), bias=col(c.rb))
                cp(xa1[:], images(A[0][0:LO, 0:GN]), ACT.Identity, scale=col(c.g1), bias=col(c.b1)).then_inc(a_out.sem, 1)
                one(it, A_Q0, q[:, 0, :], 128, ACT.Identity, bias=col(c.q))
                one(it, A_Q2, q[:, 2, :], 128, ACT.Identity, bias=col(c.q + 2))
                one(it, A_K1, k[:, 1, :], 128, ACT.Identity, bias=col(c.k + 1))

            def pre2(it):
                act.wait_ge(*done(a_ps, it, A_R))
                act.wait_ge(*done(gm_ok, it, -1))
                cp(e[:], images(A[0][0:RHD, 0:GN]), ACT.Gelu, bias=col(c.r)).then_inc(a_out.sem, 1)

            def pre3(it):
                one(it, A_H1, h1[:], RHD, ACT.Gelu, bias=col(c.h1))

            def pre4(it):
                act.wait_ge(*done(a_ps, it, A_H2))
                cp(h2[0:RHD // 2, :], A[0][0:RHD // 2, 0:GN], ACT.Gelu, bias=S.c4a[0:RHD // 2, c.h2:c.h2 + 1]).then_inc(a_out.sem, 1)

            def first():
                pre1(0)
                pre2(0)
                pre3(0)
                pre4(0)

            def body(it, last):
                for n in range(NU + 1):
                    if n < NU:
                        act.wait_ge(*done(sub_ok, it, n))
                        cp(p[:, n % 2, :, :], p[:, n % 2, :, :], ACT.Exp, scale=float(HD) ** -0.5).then_inc(exp_ok.sem, 1)
                    if n - 1 >= 0:
                        act.wait_ge(*done(pt_ps, it, n - 1))
                        cp(pT[:, (n - 1) % 2, :, :], PT[0:N, 0:GN], ACT.Copy).then_inc(pt_out.sem, 1)
                if not last:
                    pre1(it + 1)
                za(it, ZA_O, o1[:], LO)
                if not last:
                    pre2(it + 1)
                    pre3(it + 1)
                    pre4(it + 1)
                za(it, ZA_Y, xf1[:], LO, ACT.Identity, scale=col(c.g2), bias=col(c.b2))
                for f in range(KF):
                    za(it, ZA_F + f, ff[:, f, :], 128, ACT.Gelu, bias=col(c.f + f))
                za(it, ZA_U, u1[:], LO)
                za(it, ZA_D, d1[:], LO)

            steps(act, first, body)

        @block.gpsimd
        def _(pool):
            credit(pool, *veps_ok, *rstd_ok, xcopy_ok, hx_ok)

            def power(it, i):
                pool.wait_ge(*done(mean_ok[i], it, 3))
                settle(pool, S)
                nc.gpsimd.tensor_scalar(veps[:, i, :], mv[:, i, :, 1], 1.0, EPS, ALU.mult, ALU.add).then_inc(veps_ok[i].sem, 1)
                pool.wait_ge(*done(veps_ok[i], it, 0))
                nc.gpsimd.tensor_tensor(rstd[:, i, :], veps[:, i, :], S.mhalf[0:N, 0:G], ALU.pow).then_inc(rstd_ok[i].sem, 1)

            def first():
                power(0, 0)
                power(0, 1)
                pool.wait_ge(*done(x_ok, 0, 3))
                nc.gpsimd.tensor_copy(x[:], xnext[:]).then_inc(xcopy_ok.sem, 1)

            def body(it, last):
                if not last:
                    power(it + 1, 0)
                    power(it + 1, 1)
                    pool.wait_ge(*done(hh_ok, it, 3))
                    settle(pool, S)
                    nc.gpsimd.tensor_copy(x[:], xnext[:]).then_inc(xcopy_ok.sem, 1)
                power(it, 2)
                pool.wait_ge(*done(out_ok, it, 3))
                hg = rows(it)
                nc.gpsimd.tensor_tensor(hg, hg, hh[:], ALU.add).then_inc(hx_ok.sem, 1)

            steps(pool, first, body)

        @block.vector
        def _(dve):
            credit(dve, *stat_ok, *mean_ok, x_ok, z_ok, y_ok, v_out, zv_out, gm_ok, gs_ok, bit_ok, nb_ok, sel_ok, mx_ok, sub_ok,
                   den_ok, o_ok, hh_ok, out_ok)
            nv = nc.vector

            def stat(it, i, src):
                settle(dve, S)
                for j in range(G):
                    nv.bn_stats(stats[:, i, j, :], src[:, j, :]).then_inc(stat_ok[i].sem, 1)
                dve.wait_ge(*done(stat_ok[i], it, 3))
                settle(dve, S)
                for j in range(G):
                    nv.bn_aggr(mv[:, i, j, :], stats[:, i, j, :]).then_inc(mean_ok[i].sem, 1)

            def norm(it, i, src, out, ok):
                dve.wait_ge(*done(mean_ok[i], it, 3))
                dve.wait_ge(*done(rstd_ok[i], it, 0))
                for j in range(G):
                    nv.tensor_scalar(out[:, j, :], src[:, j, :], mv[:, i, j, 0:1], rstd[:, i, j:j + 1],
                                     ALU.subtract, ALU.mult).then_inc(ok.sem, 1)

            def one(it, n, out, rows_, b=None):
                dve.wait_ge(*done(v_ps, it, n))
                i = V[n % len(V)][0:rows_, 0:GN]
                nv.tensor_scalar(out, i, b, None, ALU.add).then_inc(v_out.sem, 1)

            def col(i):
                return S.c4a[:, i:i + 1]

            def colb(i):
                return S.c4b[:, i:i + 1]

            def pre1(it):
                dve.wait_ge(*done(v_ps, it, V_Z))
                zz = V[V_Z % len(V)][0:HI, 0:GN]
                nv.tensor_scalar(r2[:], zz, colb(c.rg), colb(c.rb), ALU.mult, ALU.add)
                nv.tensor_scalar(xa2[0:HI, :], zz, colb(c.g1), colb(c.b1), ALU.mult, ALU.add).then_inc(v_out.sem, 1)
                one(it, V_Q1, q[:, 1, :], 128, col(c.q + 1))
                one(it, V_K0, k[:, 0, :], 128, col(c.k))
                one(it, V_K2, k[:, 2, :], 128, col(c.k + 2))

            def pre2(it):
                for h in range(2):
                    dve.wait_ge(*done(v_ps, it, V_V + h))
                    nv.tensor_copy(v[:, 2 * h:2 * h + 2, :, 0:HD], V[(V_V + h) % len(V)][0:N, 0:2 * D].rearrange(
                        "p (g h d) -> p g h d", g=2, h=HEADS)).then_inc(v_out.sem, 1)

            def pre3(it):
                dve.wait_ge(*done(a_out, it, A_R))
                nv.tensor_reduce(gm[:], e[:, :, 1:N], AX.X, ALU.add).then_inc(gm_ok.sem, 1)
                dve.wait_ge(*done(gm_ok, it, 0))
                nv.tensor_scalar(gs[:], gm[:], 1.0 / (N - 1), None, ALU.mult).then_inc(gs_ok.sem, 1)

            def router(it):
                dve.wait_ge(*done(v_ps, it, V_L))
                nv.tensor_copy(logit[:], V[V_L % len(V)][0:N, 0:4 * G].rearrange("p (g n) -> p g n", g=G)).then_inc(v_out.sem, 1)
                dve.wait_ge(*done(v_out, it, V_L))
                pair = logit[:].rearrange("p g (b t) -> p g b t", t=2)
                nv.tensor_tensor(bits[:], pair[:, :, :, 1], pair[:, :, :, 0], ALU.is_gt).then_inc(bit_ok.sem, 1)
                dve.wait_ge(*done(bit_ok, it, 0))
                nv.memset(bits[0:1, :, :], 1.0).then_inc(bit_ok.sem, 1)
                dve.wait_ge(*done(bit_ok, it, 1))
                nv.tensor_scalar(nbits[:], bits[:], -1.0, 1.0, ALU.mult, ALU.add).then_inc(nb_ok.sem, 1)
                dve.wait_ge(*done(nb_ok, it, 0))
                for i, (a_, b_) in enumerate(((nbits, nbits), (nbits, bits), (bits, nbits))):
                    nv.tensor_tensor(sel[:, :, i], a_[:, :, 0], b_[:, :, 1], ALU.mult).then_inc(sel_ok.sem, 1)

            def softmax_in(it, n):
                sc = images(SC[n % 2][0:N, 0:GN])
                dve.wait_ge(*done(sc_ps, it, n))
                nv.tensor_reduce(mx[:, n % 2, :], sc, AX.X, ALU.max).then_inc(mx_ok.sem, 1)
                dve.wait_ge(*done(mx_ok, it, n))
                dve.wait_ge(*done(pt_ps, it, n - 2))
                nv.tensor_tensor(p[:, n % 2, :, :], sc, bc(mx[:, n % 2, :].unsqueeze(2), [N, G, N]), ALU.subtract
                                 ).then_inc(sub_ok.sem, 1)

            def zv(it, n, wd, g):
                dve.wait_ge(*done(zv_ps, it, n))
                t = ZV[n % len(ZV)]
                return t[0:N, 0:wd].rearrange("p (g n) -> p g n", g=g) if g else t[0:HI, 0:wd]

            def first():
                hg = rows(0)
                stat(0, 0, hg)
                norm(0, 0, hg, xnext, x_ok)
                dve.wait_ge(*done(x_ok, 0, 3))
                stat(0, 1, xnext)
                norm(0, 1, xnext, z, z_ok)
                pre1(0)
                pre2(0)
                pre3(0)

            def body(it, last):
                hg = rows(it)
                for n in range(NU):
                    softmax_in(it, n)
                    if n == 1:
                        router(it)
                    if not last:
                        if n == NEXT_NORM:
                            stat(it + 1, 0, rows(it + 1))
                        if n == NEXT_NORM + 2:
                            dve.wait_ge(*done(xcopy_ok, it, 0))
                            norm(it + 1, 0, rows(it + 1), xnext, x_ok)
                            dve.wait_ge(*done(x_ok, it + 1, 3))
                            stat(it + 1, 1, xnext)
                        if n == NEXT_NORM + 4:
                            norm(it + 1, 1, xnext, z, z_ok)
                dve.wait_ge(*done(pv_ps, it, NU - 1))
                for h in range(2):
                    oo = O[h][0:N, 0:2 * HEADS * (HD + 1)].rearrange("p (g h d) -> p g h d", g=2, h=HEADS)
                    nv.reciprocal(den[:, 2 * h:2 * h + 2, :], oo[:, :, :, HD]).then_inc(den_ok.sem, 1)
                for h in range(2):
                    oo = O[h][0:N, 0:2 * HEADS * (HD + 1)].rearrange("p (g h d) -> p g h d", g=2, h=HEADS)
                    dve.wait_ge(*done(den_ok, it, h))
                    nv.tensor_tensor(o[:, 2 * h:2 * h + 2, :].rearrange("p g (h d) -> p g h d", h=HEADS), oo[:, :, :, 0:HD],
                                     bc(den[:, 2 * h:2 * h + 2, :].unsqueeze(3), [N, 2, HEADS, HD]), ALU.mult
                                     ).then_inc(o_ok.sem, 1)
                if not last:
                    pre1(it + 1)
                t = zv(it, ZV_O, GN, 0)
                nv.tensor_copy(o2[0:HI, :], t).then_inc(zv_out.sem, 1)
                if not last:
                    pre2(it + 1)
                dve.wait_ge(*done(xcopy_ok, it, 0))
                for h in range(2):
                    t = zv(it, ZV_WO + h, 2 * D, 2)
                    for j in (2 * h, 2 * h + 1):
                        nv.scalar_tensor_tensor(out=hh[:, j, :], in0=t[:, j % 2, :], scalar=bits[:, j, 0:1], in1=x[:, j, :],
                                                op0=ALU.mult, op1=ALU.add).then_inc(hh_ok.sem, 1)
                    dve.wait_ge(*done(hh_ok, it, 2 * h + 1))
                    dve.sem_inc(zv_out.sem, 1)
                stat(it, 2, hh)
                if not last:
                    pre3(it + 1)
                norm(it, 2, hh, y, y_ok)
                t = zv(it, ZV_Y, GN, 0)
                nv.tensor_scalar(xf2[:], t, colb(c.g2), colb(c.b2), ALU.mult, ALU.add).then_inc(zv_out.sem, 1)
                for h in range(2):
                    t = zv(it, ZV_F + h, 2 * D, 2)
                    for j in (2 * h, 2 * h + 1):
                        nv.scalar_tensor_tensor(out=hh[:, j, :], in0=t[:, j % 2, :], scalar=bits[:, j, 1:2], in1=hh[:, j, :],
                                                op0=ALU.mult, op1=ALU.add).then_inc(out_ok.sem, 1)
                    dve.wait_ge(*done(out_ok, it, 2 * h + 1))
                    dve.sem_inc(zv_out.sem, 1)
                t = zv(it, ZV_U, GN, 0)
                nv.tensor_copy(u2[:], t).then_inc(zv_out.sem, 1)
                for h in range(2):
                    t = zv(it, ZV_DN + h, 2 * D, 2).rearrange("p g (k r) -> p g k r", k=3)
                    nv.tensor_tensor(dn[:, 2 * h:2 * h + 2, :, :], t, bc(sel[:, 2 * h:2 * h + 2, :].unsqueeze(3),
                                     [N, 2, 3, D // 3]), ALU.mult).then_inc(zv_out.sem, 1)
                t = zv(it, ZV_D, GN, 0)
                nv.tensor_copy(d2[:], t).then_inc(zv_out.sem, 1)
                dve.wait_ge(*done(hx_ok, it, 0))
                for h in range(2):
                    t = zv(it, ZV_UP + h, 2 * D, 2)
                    hj = hg[:, 2 * h:2 * h + 2, :]
                    nv.tensor_tensor(hj, t, hj, ALU.add).then_inc(zv_out.sem, 1)

            steps(dve, first, body)


def program(nc, dram):
    with ExitStack() as ctx:
        def sb(name, shape, dt=F32):
            return ctx.enter_context(nc.sbuf_tensor(name, shape, dt))

        S = Names()
        S.H = sb("H", [128, B, D])
        S.ident, S.iota, S.mhalf = sb("ident", [128, 128]), sb("iota", [128, E]), sb("mhalf", [128, 8])
        S.consts_ok = ctx.enter_context(nc.semaphore("consts_ok"))
        S.settled = ctx.enter_context(nc.semaphore("settled"))
        S.weights_in = ctx.enter_context(nc.semaphore("weights_in"))
        o0 = dram.w0a.shape[1]
        S.w0a, S.w0b = sb("w0a", [LO, o0]), sb("w0b", [HI + 1, o0])
        S.c0a, S.c0b = sb("c0a", [LO, 3]), sb("c0b", [HI, 3])
        S.cat1, S.cat2 = sb("cat1", [LO, G, NK]), sb("cat2", [HI + 1, G, NK])
        S.a0_o2, S.a0_tS2 = sb("a0_o2", [HI + 1, G, N]), sb("a0_tS2", [HI + 33, G, N])
        S.t1, S.t2, S.fwT = sb("t1", [LO, B * N]), sb("t2", [HI + 33, B * N]), sb("fwT", [E, B * N])
        S.w1w, S.w1g = sb("w1w", [D // 2 + 1, 2, 512 + 2 * D]), sb("w1g", [D // 2, 2, 3 * D // 2])
        S.a1_v, S.a1_out1 = sb("a1_v", [N, G, 8, D // 8 + 1]), sb("a1_out1", [D // 2 + 1, GN])
        S.ones_rows = [S.a1_v[:, :, :, D // 8:D // 8 + 1], S.a1_out1[D // 2:D // 2 + 1, :],
                       S.cat2[HI:HI + 1, :, :], S.a0_o2[HI:HI + 1, :, :], S.a0_tS2[HI:HI + 33, :, :]]
        S.b2 = sb("b2", [E, D])
        S.n_consts = 3 + len(S.ones_rows)
        S.loads = [(S.w0a[:], dram.w0a), (S.w0b[:], dram.w0b), (S.c0a[:], dram.c0a), (S.c0b[:], dram.c0b)]
        S.loads += [(S.cat1[:, j, N:NK], dram.mem[0:LO, :]) for j in range(G)]
        S.loads += [(S.cat2[0:HI, j, N:NK], dram.mem[LO:D, :]) for j in range(G)]
        S.loads += [(S.b2[:], dram.b2), (S.w1w[:], dram.w1w), (S.w1g[:], dram.w1g)]
        tok_phase(nc, dram, S)
        attn0_phase(nc, dram, S)
        experts_phase(nc, dram, S)
        S.w4a, S.w4b = sb("w4a", [LO, W4.width]), sb("w4b", [HI + 1, W4.width])
        S.c4a, S.c4b = sb("c4a", [LO, 21]), sb("c4b", [HI, 6])
        S.ro1, S.ro2, S.ro3 = sb("ro1", [128, 2, 128]), sb("ro2", [128, 64]), sb("ro3", [65, 4])
        S.fc2, S.fc2b, S.ones1 = sb("fc2", [128, 6, D]), sb("fc2b", [1, D]), sb("ones1", [1, N])
        S.f_xa2, S.f_o2, S.f_h2 = sb("f_xa2", [HI + 1, GN]), sb("f_o2", [HI + 1, GN]), sb("f_h2", [65, GN])
        S.f_v = sb("f_v", [N, G, 12, D // 12 + 1])
        S.late_ones = [S.f_xa2[HI:HI + 1, :], S.f_o2[HI:HI + 1, :], S.f_h2[64:65, :], S.f_v[:, :, :, D // 12:D // 12 + 1],
                       S.ones1[:]]
        S.late_loads = [(t[:], d) for t, d in ((S.w4a, dram.w4a), (S.w4b, dram.w4b), (S.c4a, dram.c4a), (S.c4b, dram.c4b),
                                               (S.ro1, dram.ro1), (S.ro2, dram.ro2), (S.ro3, dram.ro3), (S.fc2, dram.fc2),
                                               (S.fc2b, dram.fc2b))]
        S.late_ones_ok = ctx.enter_context(nc.semaphore("late_ones_ok"))
        S.late_in = ctx.enter_context(nc.semaphore("late_in"))
        attn1_phase(nc, dram, S)
        ffn1_phase(nc, dram, S)


def kernel(**inputs):
    import concourse.bacc as bacc
    from concourse.bass_utils import run_bass_kernel_spmd

    a = {k: np.ascontiguousarray(v) for k, v in inputs.items()}
    nc = bacc.Bacc("TRN2", target_bir_lowering=False, num_devices=1)
    arrays, dram = {}, Names()

    def give(name, x):
        x = np.ascontiguousarray(x)
        arrays["in_" + name] = x
        return nc.dram_tensor("in_" + name, x.shape, mybir.dt.from_np(x.dtype), kind="ExternalInput").ap()

    patches = a["x"].reshape(B, CHANNELS, GRID, PATCH, GRID, PATCH).transpose(1, 3, 5, 0, 2, 4).reshape(-1, 128, B * NP)
    dram.patches = give("patches", patches.transpose(1, 0, 2))
    dram.conv = give("conv", a["L0_tok_conv_w"].reshape(D, -1).T.reshape(-1, 128, D).transpose(1, 0, 2))
    dram.conv_b = give("conv_b", a["L0_tok_conv_b"][None])
    side = 32
    edges = np.arange(1.0 / side, 1.0, 1.0 / side, dtype=np.float32)
    frac = np.arange(0.0, 1.0 - 1e-06, 1.0 / GRID, dtype=np.float32)
    at = np.searchsorted(edges, frac, side="right")
    ids = (at[:, None] * side + at).reshape(-1)
    dram.pos = give("pos", np.concatenate([a["L0_tok_pos_table"][ids]] * 3))
    dram.txt = give("txt", a["txt"])

    def halves(*cols):
        rows = np.concatenate([np.concatenate([m, b[None]]) for m, b in cols], axis=1)
        return rows[0:LO], rows[LO:D + 1]

    z = np.zeros(D, np.float32)
    w0 = halves((a["L0_attn_Wq"], z), (a["L0_attn_Wk"], z), (a["L0_attn_Wv"], a["L0_attn_bv"]),
                (a["L0_attn_Wo"], a["L0_attn_bo"]), (a["L0_ffn_gate_w"].T, a["L0_ffn_gate_b"]))
    dram.w0a, dram.w0b = give("w0a", w0[0]), give("w0b", w0[1])
    c0 = np.stack([a["L0_attn_bq"], a["L0_attn_bk"], a["L0_ffn_scale"]], axis=1)
    dram.c0a, dram.c0b = give("c0a", c0[0:LO]), give("c0b", c0[LO:D])
    dram.mem = give("mem", a["L0_attn_memory"].T)
    def pair_tiles(x):
        x = x.reshape(E // 2, 2, *x.shape[1:])
        return np.concatenate([x[:, 0, ..., 0:LO], x[:, 1, ..., 0:LO], x[:, 0, ..., LO:D], x[:, 1, ..., LO:D]], axis=-1)

    w1 = np.concatenate([a["L0_ffn_w1"], a["L0_ffn_b1"][:, None, :]], axis=1)
    w1 = np.concatenate([pair_tiles(w1[..., 0:I]), pair_tiles(w1[..., I:2 * I])], axis=-1)
    dram.w1a, dram.w1b, dram.b1 = give("w1a", w1[:, 0:LO]), give("w1b", w1[:, LO:D]), give("b1", w1[:, D])
    w2 = pair_tiles(a["L0_ffn_w2"].transpose(0, 2, 1)).transpose(0, 2, 1).reshape(E // 2, 3, 128, D)
    dram.w2 = give("w2", w2.transpose(0, 2, 1, 3).reshape(E // 2, 128, 3 * D))
    dram.b2 = give("b2", a["L0_ffn_b2"])
    def heads(m, n, wd):
        m = m.reshape(m.shape[0], n, -1)
        return np.concatenate([m, np.zeros((*m.shape[0:2], wd - m.shape[2]), np.float32)], axis=2).reshape(m.shape[0], n * wd)

    qkv = a["L1_attn_w_qkv"].T
    rows = np.concatenate([heads(qkv[:, 0:D], 8, 32), heads(qkv[:, D:2 * D], 8, 32), qkv[:, 2 * D:],
                           a["L1_attn_w_proj"].T], axis=1)
    bias = np.concatenate([np.zeros(512 + D, np.float32), a["L1_attn_b_proj"]])[None]
    GDIM = D // 2
    dram.w1w = give("w1w", np.stack([np.concatenate([rows[0:GDIM], np.zeros_like(bias)]), np.concatenate([rows[GDIM:], bias])], axis=1))
    dram.w1g = give("w1g", np.stack([a["L1_attn_w_g0"].T, a["L1_attn_w_g1"].T], axis=1))
    f = {n[len("L1_ffn_"):]: v for n, v in a.items() if n.startswith("L1_ffn_")}
    none = lambda n: np.zeros(n, np.float32)
    down = f["lra_down"].reshape(D, D).T
    up = f["lra_up"].transpose(0, 2, 1).reshape(D, D)
    w4 = halves((f["r_in_w"].T, none(128)), (heads(f["wq"].T, 12, 32), none(384)), (heads(f["wk"].T, 12, 32), none(384)),
                (f["wv"].T, f["bv"]), (f["wo"].T, f["bo"]), (f["fc1_w"].T, none(768)), (down, none(D)), (up, none(D)))
    dram.w4a, dram.w4b = give("w4a", w4[0]), give("w4b", w4[1])
    per_feature = np.stack([f["r_ln_g"], f["r_ln_b"], f["ln1_g"], f["ln1_b"], f["ln2_g"], f["ln2_b"]], axis=1)
    other = [f["r_in_b"][:, None], f["r_o1_b"][:, None], np.concatenate([f["r_o2_b"], none(64)])[:, None],
             heads(f["bq"][None], 12, 32).reshape(3, 128).T, heads(f["bk"][None], 12, 32).reshape(3, 128).T,
             f["fc1_b"].reshape(6, 128).T]
    dram.c4a = give("c4a", np.concatenate([per_feature[0:LO], *other], axis=1))
    dram.c4b = give("c4b", per_feature[LO:D])
    dram.ro1 = give("ro1", f["r_o1_w"].T.reshape(2, 128, 128).transpose(1, 0, 2))
    dram.ro2 = give("ro2", f["r_o2_w"].T)
    dram.ro3 = give("ro3", np.concatenate([f["r_o3_w"].T, f["r_o3_b"][None]]))
    dram.fc2 = give("fc2", f["fc2_w"].T.reshape(6, 128, D).transpose(1, 0, 2))
    dram.fc2b = give("fc2b", f["fc2_b"][None])
    dram.eb = nc.dram_tensor("eb_scratch", [E // 2, 2, 768], F32, kind="Internal").ap()
    dram.fw = nc.dram_tensor("fw_scratch", [E, B * N], F32, kind="Internal").ap()
    dram.out = nc.dram_tensor("out_0", [B, N, D], F32, kind="ExternalOutput").ap()
    program(nc, dram)
    r = run_bass_kernel_spmd(nc, [arrays], core_ids=[0])
    return r.results[0]["out_0"]
```

```python
from contextlib import ExitStack

import numpy as np

import concourse.bass as bass
from concourse import mybir

ALU = mybir.AluOpType
ACT = mybir.ActivationFunctionType
AX = mybir.AxisListType
F32 = mybir.dt.float32
F32R = mybir.dt.float32r
U32 = mybir.dt.uint32

B = 16
SIDE, PATCH, CHANNELS = 96, 16, 3
GRID = SIDE // PATCH
NP = GRID * GRID
NT = 77
N = NP + NT
D = 192
LO, HI = 128, D - 128
M = 8
NK = N + M
G = 4
STEPS = B // G
GN = G * N
E, TOPK, I = 16, 4, 192
EPS = 1e-5


class Names:
    pass


class Counted:
    def __init__(self, sem, per):
        self.sem, self.per = sem, per


class W0:
    q, k, v, o, g = 0, D, 2 * D, 3 * D, 4 * D
    cq, ck, cs = 0, 1, 2


class W1:
    q, k, v, o = 0, 256, 512, 512 + D


class W4:
    r, q, k, v, o, f = 0, 128, 128 + D, 128 + 2 * D, 128 + 3 * D, 128 + 4 * D
    dn, up = 896 + 4 * D, 896 + 5 * D
    width = 896 + 6 * D


class C4:
    rg, rb, g1, b1, g2, b2, r, h1, h2, q, k, mask, f = 0, 1, 2, 3, 4, 5, 6, 7, 8, 9, 11, 13, 19


def counted(nc, ctx, name, per):
    return Counted(ctx.enter_context(nc.semaphore(name)), per)


def done(s, it, n):
    return s.sem, s.per * (it + 1) + n + 1


def before(n, ring, per):
    return n - ring if n >= ring else max(m for m in range(per) if m % ring == n % ring) - per


def credit(eng, *sems):
    for s in sems:
        eng.sem_inc(s.sem, s.per)


def settle(eng, S):
    eng.sem_inc(S.settled, 1)


def bc(ap, shape):
    return ap.to_broadcast(shape)


def tok_phase(nc, dram, S):
    KT = CHANNELS * PATCH * PATCH // 128
    PER = 3
    CH = [(b, min(PER, B - b)) for b in range(0, B, PER)]
    with ExitStack() as ctx:
        patches = ctx.enter_context(nc.sbuf_tensor("patches", [128, KT, B * NP], F32))
        conv = ctx.enter_context(nc.sbuf_tensor("conv", [128, KT, D], F32))
        pos = ctx.enter_context(nc.sbuf_tensor("pos", [PER * NP, D], F32))
        convb = ctx.enter_context(nc.sbuf_tensor("convb", [PER * NP, D], F32))
        emb = ctx.enter_context(nc.sbuf_tensor("emb", [PER * NP, len(CH), D], F32))
        ps = [ctx.enter_context(nc.psum_tensor(f"tok_ps{i}", [128, 512], F32)) for i in range(len(CH))]
        sem = lambda n: ctx.enter_context(nc.semaphore(n))
        k_in = [sem(f"tok_in{k}") for k in range(KT)]
        rows_in, posb, emb_ps, emb_ok, h_in = sem("tok_rows"), sem("tok_posb"), sem("tok_ps"), sem("tok_emb"), sem("tok_h")
        ident0 = sem("ident0")
        eb = ctx.enter_context(nc.sbuf_tensor("eb", [E // 2, 768], F32))
        eb_hi, eb_lo = (ctx.enter_context(nc.sbuf_tensor(n, [E // 2, 768], F32R)) for n in ("eb_hi", "eb_lo"))
        eb_moved, eb_ok = sem("eb_moved"), sem("eb_ok")
        block = ctx.enter_context(nc.Block())

        @block.sync
        def _(sp):
            for k in range(KT):
                sp.dma_start(patches[:, k, :], dram.patches[:, k, :]).then_inc(k_in[k], 16)
                sp.dma_start(conv[:, k, :], dram.conv[:, k, :]).then_inc(k_in[k], 16)
            sp.dma_start(S.H[NP:N, :, :], dram.txt.rearrange("b t d -> t b d")).then_inc(h_in, 16)
            for c, (b, nb) in enumerate(CH):
                for j in range(nb):
                    sp.wait_ge(emb_ok, c + 1)
                    sp.dma_start(S.H[0:NP, b + j, :], emb[j * NP:(j + 1) * NP, c, :]).then_inc(h_in, 16)
            for n, t in enumerate((eb_hi, eb_lo)):
                sp.wait_ge(eb_ok, n + 2)
                sp.dma_start(dram.eb[:, n, :], t[:].bitcast(F32)).then_inc(eb_moved, 16)
            sp.wait_ge(eb_moved, 48)
            sp.wait_ge(h_in, 16 * (B + 1))

        @block.scalar
        def _(act):
            act.dma_start(pos[:], dram.pos).then_inc(rows_in, 16)
            act.dma_start(convb[:], bc(dram.conv_b, [PER * NP, D])).then_inc(rows_in, 16)
            act.dma_start(eb[:], dram.b1).then_inc(eb_moved, 16)
            for t, src in S.loads:
                act.dma_start(t, src).then_inc(S.weights_in, 16)
            act.wait_ge(S.weights_in, 16 * len(S.loads))

        @block.gpsimd
        def _(pool):
            nc.gpsimd.memset(S.ident[:], 0.0).then_inc(ident0, 1)
            pool.wait_ge(ident0, 1)
            nc.gpsimd.affine_select(out=S.ident[:], in_=S.ident[:], compare_op=ALU.not_equal, fill=1.0, base=0,
                                    pattern=[[-1, 128]], channel_multiplier=1).then_inc(S.consts_ok, 1)
            nc.gpsimd.iota(S.iota[:], pattern=[[1, E]], base=0, channel_multiplier=0,
                           allow_small_or_imprecise_dtypes=True).then_inc(S.consts_ok, 1)
            nc.gpsimd.memset(S.mhalf[:], -0.5).then_inc(S.consts_ok, 1)
            for n, (t, value) in enumerate(S.fills):
                pool.wait_ge(S.consts_ok, 3 + n)
                nc.gpsimd.memset(t, value).then_inc(S.consts_ok, 1)

        @block.tensor
        def _(pe):
            for k in range(KT):
                pe.wait_ge(k_in[k], 32)
                for c, (b, nb) in enumerate(CH):
                    mm = nc.tensor.matmul(ps[c][0:nb * NP, 0:D], patches[:, k, b * NP:(b + nb) * NP], conv[:, k, :],
                                          start=(k == 0), stop=(k == KT - 1))
                    if k == KT - 1:
                        mm.then_inc(emb_ps, 1)

        @block.vector
        def _(dve):
            dve.wait_ge(rows_in, 32)
            nc.vector.tensor_tensor(pos[:], pos[:], convb[:], ALU.add).then_inc(posb, 1)
            dve.wait_ge(eb_moved, 16)
            nv = nc.vector
            nv.tensor_scalar(eb[:, 384:768], eb[:, 384:768], 1.0, None, ALU.add).then_inc(eb_ok, 1)
            dve.wait_ge(eb_ok, 1)
            nv.tensor_copy(eb_hi[:], eb[:]).then_inc(eb_ok, 1)
            dve.wait_ge(eb_ok, 2)
            nv.tensor_tensor(eb_lo[:], eb[:], eb_hi[:].bitcast(F32), ALU.subtract).then_inc(eb_ok, 1)
            dve.wait_ge(posb, 1)
            for c, (b, nb) in enumerate(CH):
                dve.wait_ge(emb_ps, c + 1)
                nc.vector.tensor_tensor(emb[0:nb * NP, c, :], ps[c][0:nb * NP, 0:D], pos[0:nb * NP, :],
                                        ALU.add).then_inc(emb_ok, 1)


class Tiles:

    def __init__(self, nc, ctx, name, banks, readers):
        self.banks, self.readers = banks, readers
        self.filled = counted(nc, ctx, name + "_ps", len(readers))
        self.outs = {e: counted(nc, ctx, f"{name}_{e}_out", readers.count(e)) for e in ("act", "dve")}

    def bank(self, n):
        return self.banks[n % len(self.banks)]

    def out(self, n):
        return self.outs[self.readers[n]].sem

    def copied(self, it, n):
        e = self.readers[n]
        k = self.readers[:n % len(self.readers)].count(e)
        return done(self.outs[e], it, k - (self.outs[e].per if n < 0 else 0))

    def free(self, it, n):
        return self.copied(it, before(n, len(self.banks), len(self.readers)))


class X:
    pairs, slots, tiles = E // 2, 2, 3
    W1 = 2 * tiles * 128
    BH, BL = 64, 96
    RAW = 5


def experts_memory(nc, ctx, S):
    def sb(name, shape, dt=F32):
        return ctx.enter_context(nc.sbuf_tensor("ex_" + name, shape, dt))

    S.raw1, S.raw2 = sb("raw1", [LO, X.slots, X.W1]), sb("raw2", [X.BL + 1, X.slots, X.W1])
    S.raw3 = sb("raw3", [128, X.slots, X.tiles * D])
    S.h1, S.l1 = sb("h1", [LO, X.slots, X.W1], F32R), sb("l1", [LO, X.slots, X.W1], F32R)
    S.hh2, S.l2b = sb("hh2", [2 * HI, X.slots, X.W1], F32R), sb("l2b", [X.BL + 1, X.slots, X.W1], F32R)
    S.h3, S.l3 = sb("h3", [128, X.slots, X.tiles * D], F32R), sb("l3", [128, X.slots, X.tiles * D], F32R)
    S.th1, S.tl1 = sb("th1", [LO, B * N], F32R), sb("tl1", [LO, B * N], F32R)
    S.thl2, S.th2 = sb("thl2", [2 * HI, B * N], F32R), sb("th2", [X.BL + 1, B * N], F32R)
    S.raw_first, S.raw_second, S.hi_first, S.lo_first, S.th_ok, S.tl_ok = (ctx.enter_context(nc.semaphore("ex_" + n)) for n in (
        "raw_first", "raw_second", "hi_first", "lo_first", "th_ok", "tl_ok"))


def load_pair(sp, dram, S, pair, s, sem):
    p = bass.ds(pair, 1)
    for t, src in ((S.raw1[:, s, :], dram.w1a[p, :, :]), (S.raw2[0:HI, s, :], dram.w1b[p, :, :]),
                   (S.raw2[X.BH:X.BH + 1, s, :], dram.eb[p, 0:1, :]), (S.raw2[X.BL:X.BL + 1, s, :], dram.eb[p, 1:2, :]),
                   (S.raw3[:, s, :], dram.w2[p, :, :])):
        sp.dma_start(t, src.rearrange("e p n -> (e p) n")).then_inc(sem, 16)


def weights_hi(nc, S, s, pieces, sem):
    for h, r in [(S.h1[:, s, :], S.raw1[:, s, :]), (S.hh2[0:HI, s, :], S.raw2[0:HI, s, :]),
                 (S.hh2[HI:2 * HI, s, :], S.raw2[0:HI, s, :]), (S.h3[:, s, :], S.raw3[:, s, :])][pieces]:
        nc.scalar.activation(h, r, ACT.Copy).then_inc(sem, 1)


def weights_lo(nc, S, s, n, sem):
    if n == 2:
        nc.vector.tensor_copy(S.l2b[X.BH:X.BL + 1, s, :], S.raw2[X.BH:X.BL + 1, s, :]).then_inc(sem, 1)
        return
    l, r, h = {0: (S.l1[:, s, :], S.raw1[:, s, :], S.h1[:, s, :]), 1: (S.l2b[0:HI, s, :], S.raw2[0:HI, s, :], S.hh2[0:HI, s, :]),
               3: (S.l3[:, s, :], S.raw3[:, s, :], S.h3[:, s, :])}[n]
    nc.vector.tensor_tensor(l, r, h.bitcast(F32), ALU.subtract).then_inc(sem, 1)


def inputs_hi(nc, S, n):
    c = slice(n * GN, (n + 1) * GN)
    for t, src in ((S.th1, S.t1[:]), (S.th2, S.t2[:]), (S.thl2[0:HI, :], S.t2[0:HI, :])):
        nc.scalar.activation(t[:, c], src[:, c], ACT.Copy).then_inc(S.th_ok, 1)


def inputs_lo(nc, dve, S, n):
    c = slice(n * GN, (n + 1) * GN)
    dve.wait_ge(S.th_ok, 3 * n + 1)
    nc.vector.tensor_tensor(S.tl1[:, c], S.t1[:, c], S.th1[:, c].bitcast(F32), ALU.subtract).then_inc(S.tl_ok, 1)
    dve.wait_ge(S.th_ok, 3 * n + 3)
    nc.vector.tensor_tensor(S.thl2[HI:2 * HI, c], S.t2[0:HI, c], S.th2[0:HI, c].bitcast(F32), ALU.subtract).then_inc(S.tl_ok, 1)


EARLY = 3 * G + 2


def early_stat(nc, dve, S, n, src):
    if n:
        dve.wait_ge(S.early_ok, EARLY * n)
    for j in range(G):
        nc.vector.bn_stats(S.e_stats[:, j, :], src[:, j, :]).then_inc(S.early_ok, 1)
    dve.wait_ge(S.early_ok, EARLY * n + G)
    for j in range(G):
        nc.vector.bn_aggr(S.e_mv[:, j, :], S.e_stats[:, j, :]).then_inc(S.early_ok, 1)


def early_root(nc, pool, S, n):
    pool.wait_ge(S.early_ok, EARLY * n + 2 * G)
    nc.gpsimd.tensor_scalar(S.e_veps[:], S.e_mv[:, :, 1], 1.0, EPS, ALU.mult, ALU.add).then_inc(S.early_ok, 1)
    pool.wait_ge(S.early_ok, EARLY * n + 2 * G + 1)
    nc.gpsimd.tensor_tensor(S.e_rstd[:], S.e_veps[:], S.mhalf[0:N, 0:G], ALU.pow).then_inc(S.early_ok, 1)


def early_norm(nc, dve, S, n, src, out):
    dve.wait_ge(S.early_ok, EARLY * n + 2 * G + 2)
    for j in range(G):
        nc.vector.tensor_scalar(out[:, j, :], src[:, j, :], S.e_mv[:, j, 0:1], S.e_rstd[:, j:j + 1],
                                ALU.subtract, ALU.mult).then_inc(S.early_ok, 1)


def attn0_phase(nc, dram, S):
    with ExitStack() as ctx:
        def sb(name, shape, dt=F32):
            return ctx.enter_context(nc.sbuf_tensor("a0_" + name, shape, dt))

        def sem(name, per):
            return counted(nc, ctx, "a0_" + name, per)

        w = W0
        xn = sb("xn", [N, G, D])
        stats, mv, veps, rstd = sb("stats", [N, G, 6]), sb("mv", [N, G, 2]), sb("veps", [N, G]), sb("rstd", [N, G])
        cat1, cat2 = S.cat1, S.cat2
        q1, q2 = sb("q1", [LO, G, N]), sb("q2", [HI, G, N])
        k1, k2 = sb("k1", [LO, G, NK]), sb("k2", [HI, G, NK])
        v = sb("v", [NK, G, D])
        mx, rs, ri = sb("mx", [N, G]), sb("rs", [N, G]), sb("ri", [N, G])
        p, pT = sb("p", [N, G, NK]), sb("pT", [NK, G, N])
        o1, o2 = sb("o1", [LO, G, N]), S.a0_o2
        stats2, mv2, veps2, rstd2 = sb("stats2", [N, G, 6]), sb("mv2", [N, G, 2]), sb("veps2", [N, G]), sb("rstd2", [N, G])
        x, sq, ssq, veps3, rrms = sb("x", [N, G, D]), sb("sq", [N, D]), sb("ssq", [N, G]), sb("veps3", [N, G]), sb("rrms", [N, G])
        t, tS1, tS2 = sb("t", [N, G, D]), sb("tS1", [LO, G, N]), S.a0_tS2
        g, top, idx, idxf = sb("g", [N, G, E]), sb("top", [N, G, 8]), sb("idx", [N, G, 8], U32), sb("idxf", [N, G, TOPK])
        e4, s4, r4, w4 = sb("e4", [N, G, TOPK]), sb("s4", [N, G]), sb("r4", [N, G]), sb("w4", [N, G, TOPK])
        oh, fw, fwT = sb("oh", [N, G, E, TOPK]), sb("fw", [N, G, E]), sb("fwT", [E, GN])
        bank = [ctx.enter_context(nc.psum_tensor(f"a0_ps{i}", [128, 512], F32)) for i in range(8)]
        X1, X2, Q1, Q2, K1, K2, V0, V1 = range(8)
        proj = Tiles(nc, ctx, "a0_proj", bank[0:3], ["act", "dve", "act", "dve", "dve", "act", "dve", "act"])
        SC, PT, O1, O2, H0, H1 = range(6)
        att = Tiles(nc, ctx, "a0_att", bank[3:6], ["dve", "act", "act", "dve", "dve", "dve"])
        T1, T2, LG, FW = range(4)
        rout = Tiles(nc, ctx, "a0_rout", bank[6:8], ["act", "dve", "dve", "act"])

        stat1_ok, mean1_ok, stat2_ok, mean2_ok = (sem(n, G) for n in ("stat1_ok", "mean1_ok", "stat2_ok", "mean2_ok"))
        veps1_ok, veps2_ok, veps3_ok, rstd1_ok, rstd2_ok, rrms_ok = (sem(n, 1) for n in (
            "veps1_ok", "veps2_ok", "veps3_ok", "rstd1_ok", "rstd2_ok", "rrms_ok"))
        xn_ok, x_ok, ssq_ok, t_ok, hx_ok = sem("xn_ok", G), sem("x_ok", G), sem("ssq_ok", G), sem("t_ok", G), sem("hx_ok", 1)
        mx_ok, exp_ok, sum_ok, rec_ok, p_ok = (sem(n, 1) for n in ("mx_ok", "exp_ok", "sum_ok", "rec_ok", "p_ok"))
        top_ok, idx_ok = sem("top_ok", G), sem("idx_ok", G)
        idxf_ok, e4_ok, e4x_ok, s4_ok, r4_ok, w4_ok, oh_ok, ohw_ok, fw_ok = (sem(n, 1) for n in (
            "idxf_ok", "e4_ok", "e4x_ok", "s4_ok", "r4_ok", "w4_ok", "oh_ok", "ohw_ok", "fw_ok"))
        t_stored, fw_stored = sem("t_stored", 32), sem("fw_stored", 32)
        block = ctx.enter_context(nc.Block())

        def rows(it):
            return S.H[0:N, :, :].rearrange("p b d -> p (b d)")[:, bass.ds(it * (G * D), G * D)].rearrange(
                "p (b d) -> p b d", b=G)

        def images(tile):
            return tile.rearrange("p (g n) -> p g n", g=G)

        def steps(eng, lead, body, tail):
            lead()
            body(0, True, False)
            with eng.Fori(1, STEPS - 1) as it:
                body(it, False, False)
            body(STEPS - 1, False, True)
            tail(STEPS - 1)

        @block.tensor
        def _(pe):
            credit(pe, proj.filled, att.filled, rout.filled)
            pe.wait_ge(S.consts_ok, S.n_consts)
            mm = nc.tensor.matmul

            def transposed(it, tiles, n, src, ok):
                pe.wait_ge(*tiles.free(it, n + 1))
                pe.wait_ge(*tiles.free(it, n))
                for m, c0, c1 in ((n, 0, LO), (n + 1, LO, D)):
                    for j in range(G):
                        if m == n:
                            pe.wait_ge(*done(ok, it, j))
                        i = nc.tensor.transpose(tiles.bank(m)[0:c1 - c0, j * N:(j + 1) * N], src[:, j, c0:c1], S.ident[0:N, 0:N])
                    i.then_inc(tiles.filled.sem, 1)

            def qk(it):
                pe.wait_ge(*proj.copied(it, X1))
                pe.wait_ge(*proj.copied(it, X2))
                for n, col, wd in ((Q1, w.q, N), (K1, w.k, NK)):
                    for half, (c0, c1) in enumerate(((0, LO), (LO, D))):
                        pe.wait_ge(*proj.free(it, n + half))
                        o = images(proj.bank(n + half)[0:c1 - c0, 0:G * wd])
                        mm(o, S.w0a[:, col + c0:col + c1], cat1[:, :, 0:wd], start=True, stop=False)
                        mm(o, S.w0b[0:HI, col + c0:col + c1], cat2[0:HI, :, 0:wd], start=False, stop=True
                           ).then_inc(proj.filled.sem, 1)

            def values(it):
                for h in range(2):
                    pe.wait_ge(*proj.free(it, V0 + h))
                    for j in (2 * h, 2 * h + 1):
                        o = proj.bank(V0 + h)[0:NK, (j % 2) * D:(j % 2 + 1) * D]
                        mm(o, cat1[:, j, :], S.w0a[:, w.v:w.v + D], start=True, stop=False)
                        m = mm(o, cat2[:, j, :], S.w0b[:, w.v:w.v + D], start=False, stop=True)
                    m.then_inc(proj.filled.sem, 1)

            def scores(it):
                pe.wait_ge(*proj.copied(it, K1))
                pe.wait_ge(*proj.copied(it, K2))
                pe.wait_ge(*att.free(it, SC))
                for j in range(G):
                    o = att.bank(SC)[0:N, j * NK:(j + 1) * NK]
                    mm(o, q1[:, j, :], k1[:, j, :], start=True, stop=False)
                    m = mm(o, q2[:, j, :], k2[:, j, :], start=False, stop=True)
                m.then_inc(att.filled.sem, 1)

            def p_transposed(it):
                pe.wait_ge(*done(p_ok, it, 0))
                pe.wait_ge(*att.free(it, PT))
                for j in range(G):
                    m = nc.tensor.transpose(att.bank(PT)[0:NK, j * N:(j + 1) * N], p[:, j, :], S.ident[0:N, 0:N])
                m.then_inc(att.filled.sem, 1)

            def attended(it):
                pe.wait_ge(*att.copied(it, PT))
                pe.wait_ge(*proj.copied(it, V0))
                pe.wait_ge(*proj.copied(it, V1))
                for n, c0, c1 in ((O1, 0, LO), (O2, LO, D)):
                    pe.wait_ge(*att.free(it, n))
                    for j in range(G):
                        m = mm(att.bank(n)[0:c1 - c0, j * N:(j + 1) * N], v[:, j, c0:c1], pT[:, j, :], start=True, stop=True)
                    m.then_inc(att.filled.sem, 1)

            def projected(it):
                pe.wait_ge(*att.copied(it, O1))
                pe.wait_ge(*att.copied(it, O2))
                for h in range(2):
                    pe.wait_ge(*att.free(it, H0 + h))
                    for j in (2 * h, 2 * h + 1):
                        o = att.bank(H0 + h)[0:N, (j % 2) * D:(j % 2 + 1) * D]
                        mm(o, o1[:, j, :], S.w0a[:, w.o:w.o + D], start=True, stop=False)
                        m = mm(o, o2[:, j, :], S.w0b[:, w.o:w.o + D], start=False, stop=True)
                    m.then_inc(att.filled.sem, 1)

            def logits(it):
                pe.wait_ge(*rout.copied(it, T1))
                pe.wait_ge(*rout.copied(it, T2))
                pe.wait_ge(*rout.free(it, LG))
                for j in range(G):
                    o = rout.bank(LG)[0:N, j * E:(j + 1) * E]
                    mm(o, tS1[:, j, :], S.w0a[:, w.g:w.g + E], start=True, stop=False)
                    m = mm(o, tS2[0:HI + 1, j, :], S.w0b[:, w.g:w.g + E], start=False, stop=True)
                m.then_inc(rout.filled.sem, 1)

            def fw_transposed(it):
                pe.wait_ge(*done(fw_ok, it, 0))
                pe.wait_ge(*rout.free(it, FW))
                for j in range(G):
                    m = nc.tensor.transpose(rout.bank(FW)[0:E, j * N:(j + 1) * N], fw[:, j, :], S.ident[0:N, 0:N])
                m.then_inc(rout.filled.sem, 1)

            def lead():
                transposed(0, proj, X1, xn, xn_ok)
                qk(0)

            def body(it, first, last):
                scores(it)
                values(it)
                if not last:
                    transposed(it + 1, proj, X1, xn, xn_ok)
                p_transposed(it)
                if not last:
                    qk(it + 1)
                if not first:
                    transposed(it - 1, rout, T1, t, t_ok)
                attended(it)
                if not first:
                    logits(it - 1)
                projected(it)
                if not first:
                    fw_transposed(it - 1)

            def tail(it):
                transposed(it, rout, T1, t, t_ok)
                logits(it)
                fw_transposed(it)

            steps(pe, lead, body, tail)

        @block.scalar
        def _(act):
            credit(act, *(ts.outs["act"] for ts in (proj, att, rout)), exp_ok, ssq_ok, e4x_ok)
            cp = nc.scalar.activation

            def x_copy(it):
                act.wait_ge(*done(proj.filled, it, X1))
                cp(cat1[:, :, 0:N], images(proj.bank(X1)[0:LO, 0:GN]), ACT.Copy).then_inc(proj.out(X1), 1)

            def qk_copy(it):
                act.wait_ge(*done(proj.filled, it, Q1))
                act.wait_ge(*done(att.filled, it, SC - att.filled.per))
                cp(q1[:], images(proj.bank(Q1)[0:LO, 0:GN]), ACT.Identity, bias=S.c0a[:, w.cq:w.cq + 1]).then_inc(proj.out(Q1), 1)
                act.wait_ge(*done(proj.filled, it, K2))
                cp(k2[:], images(proj.bank(K2)[0:HI, 0:G * NK]), ACT.Identity, bias=S.c0b[:, w.ck:w.ck + 1]
                   ).then_inc(proj.out(K2), 1)

            def v_copy(it):
                act.wait_ge(*done(proj.filled, it, V1))
                act.wait_ge(*done(att.filled, it, O2 - att.filled.per))
                cp(v[:, 2:4, :], proj.bank(V1)[0:NK, 0:2 * D].rearrange("p (g n) -> p g n", g=2), ACT.Copy
                   ).then_inc(proj.out(V1), 1)

            def exp(it):
                act.wait_ge(*att.copied(it, SC))
                cp(p[:], p[:], ACT.Exp, scale=float(D) ** -0.5).then_inc(exp_ok.sem, 1)

            def p_copy(it):
                act.wait_ge(*done(att.filled, it, PT))
                cp(pT[:], images(att.bank(PT)[0:NK, 0:GN]), ACT.Copy).then_inc(att.out(PT), 1)

            def o_copy(it):
                act.wait_ge(*done(att.filled, it, O1))
                cp(o1[:], images(att.bank(O1)[0:LO, 0:GN]), ACT.Copy).then_inc(att.out(O1), 1)

            def squares(it):
                act.wait_ge(*done(veps3_ok, it, -1))
                for j in range(G):
                    act.wait_ge(*done(x_ok, it, j))
                    act.wait_ge(*done(ssq_ok, it, j - 1))
                    cp(sq[:], x[:, j, :], ACT.Square, accum_out=ssq[:, j:j + 1]).then_inc(ssq_ok.sem, 1)

            def t_copy(it):
                act.wait_ge(*done(rout.filled, it, T1))
                act.wait_ge(*done(rout.filled, it, LG - rout.filled.per))
                act.wait_ge(*done(t_stored, it, -1))
                cp(tS1[:], images(rout.bank(T1)[0:LO, 0:GN]), ACT.Identity, scale=S.c0a[:, w.cs:w.cs + 1]
                   ).then_inc(rout.out(T1), 1)

            def top_exp(it):
                act.wait_ge(*done(e4_ok, it, 0))
                cp(e4[:], e4[:], ACT.Exp).then_inc(e4x_ok.sem, 1)

            def fw_copy(it):
                act.wait_ge(*done(rout.filled, it, FW))
                act.wait_ge(*done(fw_stored, it, -1))
                cp(fwT[:], rout.bank(FW)[0:E, 0:GN], ACT.Copy).then_inc(rout.out(FW), 1)

            def lead():
                x_copy(0)
                qk_copy(0)

            def body(it, first, last):
                v_copy(it)
                exp(it)
                if not last:
                    x_copy(it + 1)
                if not first:
                    squares(it - 1)
                p_copy(it)
                if not last:
                    qk_copy(it + 1)
                if not first:
                    t_copy(it - 1)
                o_copy(it)
                if not first:
                    top_exp(it - 1)
                if not first:
                    fw_copy(it - 1)

            def tail(it):
                act.wait_ge(S.raw_first, 1 + 16 * X.RAW)
                weights_hi(nc, S, 0, slice(0, 4), S.hi_first)
                squares(it)
                act.wait_ge(*done(t_stored, 0, 31))
                inputs_hi(nc, S, 0)
                t_copy(it)
                act.wait_ge(*done(t_stored, 1, 31))
                inputs_hi(nc, S, 1)
                top_exp(it)
                fw_copy(it)

            steps(act, lead, body, tail)

        @block.gpsimd
        def _(pool):
            credit(pool, veps1_ok, veps2_ok, veps3_ok, rstd1_ok, rstd2_ok, rrms_ok, hx_ok)
            ts, tt = nc.gpsimd.tensor_scalar, nc.gpsimd.tensor_tensor
            nc.gpsimd.memset(S.raw2[X.BH:X.BL + 1, :, :], 0.0).then_inc(S.raw_first, 1)
            pool.wait_ge(S.raw_first, 1)

            def root(it, ok, src, scale, ve, ve_ok, out, out_ok, used):
                pool.wait_ge(*done(ok, it, G - 1))
                settle(pool, S)
                ts(ve[:], src, scale, EPS, ALU.mult, ALU.add).then_inc(ve_ok.sem, 1)
                pool.wait_ge(*done(ve_ok, it, 0))
                pool.wait_ge(*done(used, it, -1))
                tt(out[:], ve[:], S.mhalf[0:N, 0:G], ALU.pow).then_inc(out_ok.sem, 1)

            def root1(it):
                root(it, mean1_ok, mv[:, :, 1], 1.0, veps, veps1_ok, rstd, rstd1_ok, xn_ok)

            def router(it):
                root(it, mean2_ok, mv2[:, :, 1], 1.0, veps2, veps2_ok, rstd2, rstd2_ok, x_ok)

            def router2(it):
                root(it, ssq_ok, ssq[:], 1.0 / D, veps3, veps3_ok, rrms, rrms_ok, t_ok)
                hg = rows(it)
                tt(hg, hg, x[:], ALU.add).then_inc(hx_ok.sem, 1)

            def body(it, first, last):
                if not last:
                    root1(it + 1)
                if not first:
                    router(it - 1)
                    router2(it - 1)

            def tail(it):
                router(it)
                router2(it)

            steps(pool, lambda: root1(0), body, tail)

        @block.vector
        def _(dve):
            credit(dve, stat1_ok, mean1_ok, stat2_ok, mean2_ok, xn_ok, x_ok, t_ok, *(ts.outs["dve"] for ts in (proj, att, rout)),
                   mx_ok, sum_ok, rec_ok, p_ok, top_ok, idx_ok, idxf_ok, e4_ok, s4_ok, r4_ok, w4_ok, oh_ok, ohw_ok, fw_ok)
            nv = nc.vector

            def mean(it, st, m, st_ok, m_ok):
                src = rows(it)
                settle(dve, S)
                for j in range(G):
                    nv.bn_stats(st[:, j, :], src[:, j, :]).then_inc(st_ok.sem, 1)
                dve.wait_ge(*done(st_ok, it, G - 1))
                settle(dve, S)
                for j in range(G):
                    nv.bn_aggr(m[:, j, :], st[:, j, :]).then_inc(m_ok.sem, 1)

            def norm(it, m, m_ok, r, r_ok, out, ok):
                src = rows(it)
                dve.wait_ge(*done(m_ok, it, G - 1))
                dve.wait_ge(*done(r_ok, it, 0))
                for j in range(G):
                    nv.tensor_scalar(out[:, j, :], src[:, j, :], m[:, j, 0:1], r[:, j:j + 1],
                                     ALU.subtract, ALU.mult).then_inc(ok.sem, 1)

            def mean1(it):
                mean(it, stats, mv, stat1_ok, mean1_ok)

            def norm1(it):
                dve.wait_ge(*done(proj.filled, it, X2 - proj.filled.per))
                norm(it, mv, mean1_ok, rstd, rstd1_ok, xn, xn_ok)

            def x_copy(it):
                dve.wait_ge(*done(proj.filled, it, X2))
                nv.tensor_copy(cat2[0:HI, :, 0:N], images(proj.bank(X2)[0:HI, 0:GN])).then_inc(proj.out(X2), 1)

            def qk_copy(it):
                dve.wait_ge(*done(att.filled, it, SC - att.filled.per))
                dve.wait_ge(*done(proj.filled, it, Q2))
                nv.tensor_scalar(q2[:], images(proj.bank(Q2)[0:HI, 0:GN]), S.c0b[:, w.cq:w.cq + 1], None, ALU.add
                                 ).then_inc(proj.out(Q2), 1)
                dve.wait_ge(*done(proj.filled, it, K1))
                nv.tensor_scalar(k1[:], images(proj.bank(K1)[0:LO, 0:G * NK]), S.c0a[:, w.ck:w.ck + 1], None, ALU.add
                                 ).then_inc(proj.out(K1), 1)

            def v_copy(it):
                dve.wait_ge(*done(att.filled, it, O2 - att.filled.per))
                dve.wait_ge(*done(proj.filled, it, V0))
                nv.tensor_copy(v[:, 0:2, :], proj.bank(V0)[0:NK, 0:2 * D].rearrange("p (g n) -> p g n", g=2)
                               ).then_inc(proj.out(V0), 1)

            def softmax_in(it):
                sc = images(att.bank(SC)[0:N, 0:G * NK])
                dve.wait_ge(*done(att.filled, it, SC))
                nv.tensor_reduce(mx[:], sc, AX.X, ALU.max).then_inc(mx_ok.sem, 1)
                dve.wait_ge(*done(mx_ok, it, 0))
                dve.wait_ge(*done(att.filled, it, PT - att.filled.per))
                nv.tensor_tensor(p[:], sc, bc(mx[:].unsqueeze(2), [N, G, NK]), ALU.subtract).then_inc(att.out(SC), 1)

            def softmax_out(it):
                dve.wait_ge(*done(exp_ok, it, 0))
                nv.tensor_reduce(rs[:], p[:], AX.X, ALU.add).then_inc(sum_ok.sem, 1)
                dve.wait_ge(*done(sum_ok, it, 0))
                nv.reciprocal(ri[:], rs[:]).then_inc(rec_ok.sem, 1)
                dve.wait_ge(*done(rec_ok, it, 0))
                nv.tensor_tensor(p[:], p[:], bc(ri[:].unsqueeze(2), [N, G, NK]), ALU.mult).then_inc(p_ok.sem, 1)

            def o_copy(it):
                dve.wait_ge(*done(att.filled, it, O2))
                nv.tensor_copy(o2[0:HI, :, :], images(att.bank(O2)[0:HI, 0:GN])).then_inc(att.out(O2), 1)

            def residual(it):
                hg = rows(it)
                for h in range(2):
                    dve.wait_ge(*done(att.filled, it, H0 + h))
                    nv.tensor_tensor(hg[:, 2 * h:2 * h + 2, :],
                                     att.bank(H0 + h)[0:N, 0:2 * D].rearrange("p (g n) -> p g n", g=2),
                                     hg[:, 2 * h:2 * h + 2, :], ALU.add).then_inc(att.out(H0 + h), 1)

            def mean2(it):
                dve.wait_ge(*att.copied(it, H1))
                mean(it, stats2, mv2, stat2_ok, mean2_ok)

            def norm2(it):
                dve.wait_ge(*done(hx_ok, it, -1))
                norm(it, mv2, mean2_ok, rstd2, rstd2_ok, x, x_ok)

            def rms(it):
                dve.wait_ge(*done(x_ok, it, G - 1))
                dve.wait_ge(*done(rrms_ok, it, 0))
                dve.wait_ge(*done(rout.filled, it, T2 - rout.filled.per))
                for j in range(G):
                    nv.tensor_scalar(t[:, j, :], x[:, j, :], rrms[:, j:j + 1], None, ALU.mult).then_inc(t_ok.sem, 1)

            def t_copy(it):
                dve.wait_ge(*done(rout.filled, it, T2))
                dve.wait_ge(*done(t_stored, it, -1))
                nv.tensor_scalar(tS2[0:HI, :, :], images(rout.bank(T2)[0:HI, 0:GN]), S.c0b[:, w.cs:w.cs + 1], None, ALU.mult
                                 ).then_inc(rout.out(T2), 1)

            def top4(it):
                dve.wait_ge(*done(rout.filled, it, LG))
                nv.tensor_copy(g[:], images(rout.bank(LG)[0:N, 0:G * E])).then_inc(rout.out(LG), 1)
                dve.wait_ge(*rout.copied(it, LG))
                settle(dve, S)
                for j in range(G):
                    nv.max(top[:, j, :], g[:, j, :]).then_inc(top_ok.sem, 1)
                dve.wait_ge(*done(top_ok, it, G - 1))
                nv.tensor_tensor(e4[:], top[:, :, 0:TOPK], bc(top[:, :, 0:1], [N, G, TOPK]), ALU.subtract
                                 ).then_inc(e4_ok.sem, 1)
                for j in range(G):
                    nv.max_index(idx[:, j, :], top[:, j, :], g[:, j, :]).then_inc(idx_ok.sem, 1)
                dve.wait_ge(*done(idx_ok, it, G - 1))
                nv.tensor_copy(idxf[:], idx[:, :, 0:TOPK]).then_inc(idxf_ok.sem, 1)

            def weights(it):
                dve.wait_ge(*done(e4x_ok, it, 0))
                nv.tensor_reduce(s4[:], e4[:], AX.X, ALU.add).then_inc(s4_ok.sem, 1)
                dve.wait_ge(*done(s4_ok, it, 0))
                nv.reciprocal(r4[:], s4[:]).then_inc(r4_ok.sem, 1)
                dve.wait_ge(*done(idxf_ok, it, 0))
                nv.tensor_tensor(oh[:], bc(S.iota[0:N, :].unsqueeze(1).unsqueeze(3), [N, G, E, TOPK]),
                                 bc(idxf[:].unsqueeze(2), [N, G, E, TOPK]), ALU.is_equal).then_inc(oh_ok.sem, 1)
                dve.wait_ge(*done(r4_ok, it, 0))
                nv.tensor_tensor(w4[:], e4[:], bc(r4[:].unsqueeze(2), [N, G, TOPK]), ALU.mult).then_inc(w4_ok.sem, 1)
                dve.wait_ge(*done(oh_ok, it, 0))
                dve.wait_ge(*done(w4_ok, it, 0))
                nv.tensor_tensor(oh[:], oh[:], bc(w4[:].unsqueeze(2), [N, G, E, TOPK]), ALU.mult).then_inc(ohw_ok.sem, 1)
                dve.wait_ge(*done(ohw_ok, it, 0))
                dve.wait_ge(*done(rout.filled, it, FW - rout.filled.per))
                nv.tensor_reduce(fw[:], oh[:], AX.X, ALU.add).then_inc(fw_ok.sem, 1)

            def lead():
                mean1(0)
                norm1(0)
                x_copy(0)
                qk_copy(0)

            def body(it, first, last):
                if not last:
                    mean1(it + 1)
                if not last:
                    norm1(it + 1)
                softmax_in(it)
                v_copy(it)
                softmax_out(it)
                if not last:
                    x_copy(it + 1)
                if not first:
                    mean2(it - 1)
                if not first:
                    norm2(it - 1)
                if not last:
                    qk_copy(it + 1)
                if not first:
                    rms(it - 1)
                    t_copy(it - 1)
                o_copy(it)
                if not first:
                    top4(it - 1)
                if not first:
                    weights(it - 1)
                residual(it)

            def first_weights(*pieces):
                for n in pieces:
                    dve.wait_ge(S.hi_first, n + 1)
                    weights_lo(nc, S, 0, n, S.lo_first)

            def tail(it):
                mean2(it)
                norm2(it)
                first_weights(0, 1)
                rms(it)
                inputs_lo(nc, dve, S, 0)
                t_copy(it)
                first_weights(2, 3)
                top4(it)
                weights(it)
                inputs_lo(nc, dve, S, 1)

            steps(dve, lead, body, tail)

        @block.sync
        def _(sp):
            credit(sp, t_stored, fw_stored)
            sp.wait_ge(S.raw_first, 1)
            load_pair(sp, dram, S, 0, 0, S.raw_first)
            load_pair(sp, dram, S, 1, 1, S.raw_second)

            def store(it):
                sp.wait_ge(*rout.copied(it, T1))
                settle(sp, S)
                sp.dma_start(S.t1[:, bass.ds(it * GN, GN)], tS1[:].rearrange("p g n -> p (g n)")).then_inc(t_stored.sem, 16)
                sp.wait_ge(*rout.copied(it, T2))
                settle(sp, S)
                sp.dma_start(S.t2[:, bass.ds(it * GN, GN)], tS2[:].rearrange("p g n -> p (g n)")).then_inc(t_stored.sem, 16)
                sp.wait_ge(*rout.copied(it, FW))
                settle(sp, S)
                sp.dma_start(S.fwT[:, bass.ds(it * GN, GN)], fwT[:]).then_inc(fw_stored.sem, 16)
                sp.dma_start(dram.fw[:, bass.ds(it * GN, GN)], fwT[:]).then_inc(fw_stored.sem, 16)

            def body(it, first, last):
                if not first:
                    store(it - 1)

            steps(sp, lambda: None, body, store)
            sp.wait_ge(S.raw_second, 16 * X.RAW)
            sp.wait_ge(*done(t_stored, STEPS - 1, 31))
            sp.wait_ge(*done(fw_stored, STEPS - 1, 31))


def experts_phase(nc, dram, S):
    PAIRS, SLOTS, TILES, CHUNKS, HALVES = X.pairs, X.slots, X.tiles, 2, 2
    UNITS = SLOTS * CHUNKS * TILES
    LOOPS = PAIRS // SLOTS
    HB = B // HALVES
    HN = HB * N
    AHEAD = 3
    RING = AHEAD + 1
    ALPHA, LIMIT = 1.702, 7.0
    SIG_LIMIT = float(1.0 / (1.0 + np.exp(-ALPHA * LIMIT)))
    with ExitStack() as ctx:
        def sb(name, shape, dt=F32):
            return ctx.enter_context(nc.sbuf_tensor("ex_" + name, shape, dt))

        def sem(name, per):
            return counted(nc, ctx, "ex_" + name, per)

        wbc = sb("wbc", [128, SLOTS, TILES, HN])
        sg, sw, aa, bb = (sb(n, [128, 2, GN]) for n in ("sg", "sw", "aa", "bb"))
        act_f = sb("act_f", [128, 2, GN])
        act_h, act_l = sb("act_h", [128, RING, GN], F32R), sb("act_l", [128, RING, GN], F32R)
        gp = [ctx.enter_context(nc.psum_tensor(f"ex_gps{i}", [128, 512], F32)) for i in range(2)]
        lp = [ctx.enter_context(nc.psum_tensor(f"ex_lps{i}", [128, 512], F32)) for i in range(2)]
        acc = [ctx.enter_context(nc.psum_tensor(f"ex_acc{i}", [128, 512], F32)) for i in range(HB // 2)]

        raw_in = [sem(f"raw_in{s}", 16 * X.RAW) for s in range(SLOTS)]
        wbc_in = [sem(f"wbc_in{s}", 64) for s in range(SLOTS)]
        hi_ok, lo_ok = sem("hi_ok", 4 * SLOTS), sem("lo_ok", 4 * SLOTS)
        g_ps, l_ps, y_ps = sem("g_ps", UNITS), sem("l_ps", UNITS), sem("y_ps", UNITS)
        sig_ok, sw_ok, a_ok, b_ok = sem("sig_ok", UNITS), sem("sw_ok", UNITS), sem("a_ok", UNITS), sem("b_ok", UNITS)
        f_ok, h_ok, l_ok = sem("f_ok", UNITS), sem("h_ok", UNITS), sem("l_ok", UNITS)
        h_done = ctx.enter_context(nc.semaphore("ex_h_done"))
        block = ctx.enter_context(nc.Block())

        def unit(k):
            k %= UNITS
            return k // (CHUNKS * TILES), k // TILES % CHUNKS, k % TILES

        def chunk(n):
            return slice(n * GN, (n + 1) * GN)

        def half_of(half, last, k):
            return half + (last and k >= UNITS)

        def steps(eng, body):
            for half in range(HALVES):
                first, end = half * LOOPS, (half + 1) * LOOPS
                if half:
                    body(first, half, True, False)
                with eng.Fori(first + (half > 0), end - 1) as it:
                    body(it, half, False, False)
                body(end - 1, half, False, True)

        def final(half, last):
            return last and half == HALVES - 1

        @block.sync
        def _(sp):
            credit(sp, *raw_in, *wbc_in)

            def routing(pair, half, s):
                for e, p0, p1, m in ((0, 0, 128, 0), (1, 0, 128, 1), (0, 0, 64, 2), (1, 64, 128, 2)):
                    row = dram.fw[bass.ds(pair * 2 + e, 1), half * HN:(half + 1) * HN]
                    sp.dma_start(wbc[p0:p1, s, m, :], bc(row, [p1 - p0, HN])).then_inc(wbc_in[s].sem, 16)

            for s in range(SLOTS):
                sp.sem_inc(raw_in[s].sem, raw_in[s].per)
                routing(s, 0, s)

            def body(it, half, first, last):
                if final(half, last):
                    return
                for s in range(SLOTS):
                    pair = s if last else (it + 1 - half * LOOPS) * SLOTS + s
                    sp.wait_ge(*done(lo_ok, it, 4 * s + 3))
                    settle(sp, S)
                    load_pair(sp, dram, S, pair, s, raw_in[s].sem)
                    sp.wait_ge(*done(sw_ok, it, (s + 1) * CHUNKS * TILES - 1))
                    settle(sp, S)
                    routing(pair, half + last, s)

            steps(sp, body)

        @block.tensor
        def _(pe):
            credit(pe, g_ps, l_ps, y_ps)
            mm = nc.tensor.matmul

            def second_biases(half):
                for j in range(HB):
                    b = half * HB + j
                    if half and j % 2 == 0:
                        pe.wait_ge(h_done, j // 2 + 1)
                    mm(acc[j // 2][0:N, (j % 2) * D:(j % 2 + 1) * D], S.fwT[:, b * N:(b + 1) * N], S.b2[:],
                       start=(j % 2 == 0), stop=False, skip_group_check=True)

            def up(it, half, k):
                s, c, m = unit(k)
                pe.wait_ge(*done(lo_ok, it, 4 * SLOTS * (k // UNITS) + 4 * s + 3))
                cols = chunk(half * CHUNKS + c)
                for o, ok, free, base in ((gp, g_ps, a_ok, 0), (lp, l_ps, b_ok, TILES * 128)):
                    pe.wait_ge(*done(free, it, k - 2))
                    wc = slice(base + m * 128, base + (m + 1) * 128)
                    parts = [(S.h1, S.th1), (S.h1, S.tl1), (S.l1, S.th1), (S.hh2, S.thl2), (S.l2b, S.th2)]
                    for n, (wt, x) in enumerate(parts):
                        i = mm(o[k % 2][:, 0:GN], wt[:, s, wc], x[:, cols], start=(n == 0), stop=(n == len(parts) - 1))
                    i.then_inc(ok.sem, 1)

            def down(it, k):
                s, c, m = unit(k)
                pe.wait_ge(*done(h_ok, it, k))
                pe.wait_ge(*done(l_ok, it, k))
                wc = slice(m * D, (m + 1) * D)
                for j in range(G):
                    img = c * G + j
                    o = acc[img // 2][0:N, (img % 2) * D:(img % 2 + 1) * D]
                    x = slice(j * N, (j + 1) * N)
                    for a, wt in ((act_h, S.h3), (act_h, S.l3), (act_l, S.h3)):
                        i = mm(o, a[:, k % RING, x], wt[:, s, wc], start=False, stop=True, skip_group_check=True)
                i.then_inc(y_ps.sem, 1)

            for k in range(AHEAD):
                if k == 1:
                    second_biases(0)
                up(0, 0, k)

            def body(it, half, first, last):
                for k in range(UNITS):
                    if last and not final(half, last) and k + AHEAD == UNITS:
                        pe.wait_ge(S.tl_ok, 2 * CHUNKS * HALVES)
                    if k + AHEAD < UNITS or not final(half, last):
                        up(it, half_of(half, last, k + AHEAD), k + AHEAD)
                    if first and k == 0:
                        second_biases(half)
                    down(it, k)

            steps(pe, body)

        @block.scalar
        def _(act):
            credit(act, sig_ok, h_ok, hi_ok)
            cp = nc.scalar.activation

            def split(it, s, pieces):
                act.wait_ge(*done(raw_in[s], it, 16 * X.RAW - 1))
                weights_hi(nc, S, s, pieces, hi_ok.sem)

            def sigmoid(it, k):
                act.wait_ge(*done(g_ps, it, k))
                act.wait_ge(*done(sw_ok, it, k - 2))
                cp(sg[:, k % 2, :], gp[k % 2][:, 0:GN], ACT.Sigmoid, scale=ALPHA).then_inc(sig_ok.sem, 1)

            act.sem_inc(hi_ok.sem, 4)
            sigmoid(0, 0)
            sigmoid(0, 1)

            def body(it, half, first, last):
                for k in range(UNITS):
                    if k + 2 < UNITS or not final(half, last):
                        sigmoid(it, k + 2)
                    act.wait_ge(*done(f_ok, it, k))
                    act.wait_ge(*done(y_ps, it, k - RING))
                    act.wait_ge(*done(l_ok, it, k - RING))
                    cp(act_h[:, k % RING, :], act_f[:, k % 2, :], ACT.Copy).then_inc(h_ok.sem, 1)
                    if k < 2:
                        act.wait_ge(*done(y_ps, it, -1))
                        split(it, 1, slice(2 * k, 2 * k + 2))
                    if k in (6, 7) and not final(half, last):
                        act.wait_ge(*done(y_ps, it, 5))
                        split(it + 1, 0, slice(2 * k - 12, 2 * k - 10))
                    if last and half == 0 and k in (0, 1):
                        inputs_hi(nc, S, CHUNKS + k)

            steps(act, body)

        @block.vector
        def _(dve):
            credit(dve, sw_ok, a_ok, b_ok, lo_ok)
            nv = nc.vector

            def split(it, s, pieces):
                for n in pieces:
                    dve.wait_ge(*done(hi_ok, it, 4 * s + n))
                    weights_lo(nc, S, s, n, lo_ok.sem)

            dve.sem_inc(lo_ok.sem, 4)

            def body(it, half, first, last):
                for k in range(UNITS):
                    s, c, m = unit(k)
                    if m == 0 and c == 0:
                        dve.wait_ge(*done(wbc_in[s], it, 63))
                    dve.wait_ge(*done(sig_ok, it, k))
                    nv.scalar_tensor_tensor(out=sw[:, k % 2, :], in0=sg[:, k % 2, :], scalar=SIG_LIMIT,
                                            in1=wbc[:, s, m, c * GN:(c + 1) * GN], op0=ALU.min, op1=ALU.mult
                                            ).then_inc(sw_ok.sem, 1)
                    dve.wait_ge(*done(l_ps, it, k))
                    dve.wait_ge(*done(f_ok, it, k - 2))
                    nv.tensor_scalar(bb[:, k % 2, :], lp[k % 2][:, 0:GN], LIMIT + 1.0, 1.0 - LIMIT, ALU.min, ALU.max
                                     ).then_inc(b_ok.sem, 1)
                    dve.wait_ge(*done(sw_ok, it, k))
                    nv.scalar_tensor_tensor(out=aa[:, k % 2, :], in0=gp[k % 2][:, 0:GN], scalar=LIMIT,
                                            in1=sw[:, k % 2, :], op0=ALU.min, op1=ALU.mult).then_inc(a_ok.sem, 1)
                    if k in (3, 4):
                        split(it, 1, range(2 * k - 6, 2 * k - 4))
                    if k in (9, 10) and not final(half, last):
                        split(it + 1, 0, range(2 * k - 18, 2 * k - 16))
                    if last and half == 0 and k in (5, 6):
                        inputs_lo(nc, dve, S, CHUNKS + k - 5)
                    if first and k == AHEAD - 1:
                        take(0)

            def take(half):
                dve.wait_ge(*done(y_ps, (half + 1) * LOOPS - 1, UNITS - 1))
                for q in range(HB // 2):
                    h = S.H[0:N, half * HB + 2 * q:half * HB + 2 * q + 2, :]
                    nv.tensor_tensor(h, acc[q][0:N, 0:2 * D].rearrange("p (g n) -> p g n", g=2), h, ALU.add
                                     ).then_inc(h_done, 1)

            steps(dve, body)
            take(HALVES - 1)

        @block.gpsimd
        def _(pool):
            credit(pool, f_ok, l_ok)

            def product(it, k):
                pool.wait_ge(*done(a_ok, it, k))
                pool.wait_ge(*done(h_ok, it, k - 2))
                pool.wait_ge(*done(l_ok, it, k - 2))
                nc.gpsimd.tensor_tensor(act_f[:, k % 2, :], aa[:, k % 2, :], bb[:, k % 2, :], ALU.mult).then_inc(f_ok.sem, 1)

            product(0, 0)

            def body(it, half, first, last):
                for k in range(UNITS):
                    if k + 1 < UNITS or not final(half, last):
                        product(it, k + 1)
                    pool.wait_ge(*done(h_ok, it, k))
                    nc.gpsimd.tensor_tensor(act_l[:, k % RING, :], act_f[:, k % 2, :], act_h[:, k % RING, :].bitcast(F32),
                                            ALU.subtract).then_inc(l_ok.sem, 1)

            steps(pool, body)


def attn1_phase(nc, dram, S):
    HEADS, HD, GROUPS = 8, D // 8, 2
    GD = D // GROUPS
    SCALE = float(HD) ** -0.5
    UNITS = ["g0", 0, 1, 2, 3, 4, "g1", 5, 6, 7]
    NU = len(UNITS)
    HQ = 4
    NQ = HEADS // HQ
    AHEAD = 2
    SLOTS = NU // 2
    with ExitStack() as ctx:
        def sb(name, shape, dt=F32):
            return ctx.enter_context(nc.sbuf_tensor("a1_" + name, shape, dt))

        def sem(name, per):
            return counted(nc, ctx, "a1_" + name, per)

        w = W1
        xn = sb("xn", [N, G, D])
        stats, mv, veps, rstd = sb("stats", [N, G, 6]), sb("mv", [N, G, 2]), sb("veps", [N, G]), sb("rstd", [N, G])
        xa, xb, cur = sb("xa", [GD, G, N]), sb("xb", [GD, G, N]), sb("cur", [GD, G, N])
        q, k = sb("q", [128, 2, GN]), sb("k", [128, 2, GN])
        v = S.a1_v
        gq, gk, gv = sb("gq", [GD, GN]), sb("gk", [GD, GN]), sb("gv", [N, G, GD])
        p, pT, mx = sb("p", [N, SLOTS, G, N]), sb("pT", [N, 2, G, N]), sb("mx", [N, 2, G])
        rs, ri = sb("rs", [N, G]), sb("ri", [N, G])
        hx = sb("hx", [GD, GROUPS, GN])
        ot, den, o = sb("ot", [128, GN]), sb("den", [N, G, HQ]), sb("o", [N, G, D])
        out0, out1 = sb("out0", [GD, GN]), S.a1_out1
        bank = [ctx.enter_context(nc.psum_tensor(f"a1_ps{i}", [128, 512], F32)) for i in range(8)]
        PT, O = bank[2], bank[3]
        units = Tiles(nc, ctx, "a1_units", bank[0:2], ["dve"] * NU)
        X1, X2, GQ0, GK0, Q0, K0, Q1, K1, V0, V1, GV0 = range(11)
        proj = Tiles(nc, ctx, "a1_proj", bank[4:6], ["act", "dve", "act", "act", "act", "dve", "act", "dve", "dve", "act", "dve"])
        HX0, GQ1, GK1, GV1, HX1, O1, O2, HH0, HH1 = range(9)
        group = Tiles(nc, ctx, "a1_group", bank[6:8], ["dve", "act", "act", "dve", "act", "dve", "dve", "dve", "dve"])

        stat_ok, mean_ok, veps_ok, rstd_ok, xn_ok = sem("stat_ok", G), sem("mean_ok", G), sem("veps_ok", 1), sem("rstd_ok", 1), sem("xn_ok", G)
        mx_ok, exp_ok = sem("mx_ok", NU), sem("exp_ok", NU)
        sum_ok, rec_ok, nrm_ok = sem("sum_ok", 2), sem("rec_ok", 2), sem("nrm_ok", 2)
        pt_ps, pt_out, pv_ps = sem("pt_ps", NU), sem("pt_out", NU), sem("pv_ps", HEADS)
        ot_ok, back_ps, den_ok, o_ok = (sem(n, NQ) for n in ("ot_ok", "back_ps", "den_ok", "o_ok"))
        block = ctx.enter_context(nc.Block())

        def unit(it, n):
            return (it + 1, n - NU) if n >= NU else (it, n)

        def rows(it):
            return S.H[0:N, :, :].rearrange("p b d -> p (b d)")[:, bass.ds(it * (G * D), G * D)].rearrange(
                "p (b d) -> p b d", b=G)

        def steps(eng, lead, body, tail):
            lead()
            body(0, True, False)
            with eng.Fori(1, STEPS - 1) as it:
                body(it, False, False)
            body(STEPS - 1, False, True)
            tail(STEPS - 1)

        def images(ap):
            return ap.rearrange("p (g n) -> p g n", g=G)

        @block.sync
        def _(sp):
            for t, src in S.late_loads:
                sp.dma_start(t, src).then_inc(S.late_in, 16)
            sp.wait_ge(S.late_in, 16 * len(S.late_loads))

        @block.tensor
        def _(pe):
            credit(pe, proj.filled, group.filled, units.filled, pt_ps, pv_ps, back_ps)
            mm = nc.tensor.matmul

            def transposed(it, tiles, n, src, ok):
                pe.wait_ge(*tiles.free(it, n + 1))
                pe.wait_ge(*tiles.free(it, n))
                for i in range(GROUPS):
                    for j in range(G):
                        if i == 0 and ok is not None:
                            pe.wait_ge(*done(ok, it, j))
                        m = nc.tensor.transpose(tiles.bank(n + i)[0:GD, j * N:(j + 1) * N], src[:, j, i * GD:(i + 1) * GD],
                                                S.ident[0:N, 0:N])
                    m.then_inc(tiles.filled.sem, 1)

            def group_qk(it, tiles, n, i, x):
                for m, c in ((n, 0), (n + 1, GD)):
                    pe.wait_ge(*tiles.free(it, m))
                    mm(tiles.bank(m)[0:GD, 0:GN], S.w1g[0:GD, i, c:c + GD], x[:], start=True, stop=True).then_inc(tiles.filled.sem, 1)

            def group_v(it, tiles, n, i, x):
                pe.wait_ge(*tiles.free(it, n))
                for j in range(G):
                    m = mm(tiles.bank(n)[0:N, j * GD:(j + 1) * GD], x[:, j, :], S.w1g[0:GD, i, 2 * GD:3 * GD], start=True, stop=True)
                m.then_inc(tiles.filled.sem, 1)

            def pre_x(it):
                transposed(it, proj, X1, xn, xn_ok)

            def pre_group(it):
                pe.wait_ge(*proj.copied(it, X2))
                pe.wait_ge(*proj.copied(it, X1))
                group_qk(it, proj, GQ0, 0, xa)

            def pre_qk(it, t):
                for n, col in ((Q0 + 2 * t, w.q), (K0 + 2 * t, w.k)):
                    pe.wait_ge(*proj.free(it, n))
                    for i, x in enumerate((xa, xb)):
                        m = mm(proj.bank(n)[:, 0:GN], S.w1w[0:GD, i, col + 128 * t:col + 128 * (t + 1)], x[:],
                               start=(i == 0), stop=(i == 1))
                    m.then_inc(proj.filled.sem, 1)

            def pre_v(it):
                for h in range(2):
                    pe.wait_ge(*proj.free(it, V0 + h))
                    for j in (2 * h, 2 * h + 1):
                        o_ = proj.bank(V0 + h)[0:N, (j % 2) * D:(j % 2 + 1) * D]
                        mm(o_, xa[:, j, :], S.w1w[0:GD, 0, w.v:w.v + D], start=True, stop=False)
                        m = mm(o_, xb[:, j, :], S.w1w[0:GD, 1, w.v:w.v + D], start=False, stop=True)
                    m.then_inc(proj.filled.sem, 1)

            def second_group(it):
                pe.wait_ge(*group.copied(it, HX0))
                group_qk(it, group, GQ1, 1, cur)
                group_v(it, group, GV1, 1, cur)

            def scores(it, n):
                u = UNITS[n]
                o_ = units.bank(n)
                if u == "g0":
                    pe.wait_ge(*proj.copied(it, GK0))
                elif u == "g1":
                    pe.wait_ge(*group.copied(it, GK1))
                elif u % HQ == 0:
                    pe.wait_ge(*proj.copied(it, Q0 + 2 * (u // HQ)))
                    pe.wait_ge(*proj.copied(it, K0 + 2 * (u // HQ)))
                pe.wait_ge(*units.free(it, n))
                for j in range(G):
                    c = slice(j * N, (j + 1) * N)
                    if u in ("g0", "g1"):
                        m = mm(o_[0:N, c], gq[:, c], gk[:, c], start=True, stop=True)
                    else:
                        t, r = u // 4, 32 * (u % 4)
                        m = mm(o_[0:N, c], q[r:r + HD, t, c], k[r:r + HD, t, c], start=True, stop=True, tile_position=(r, 0))
                m.then_inc(units.filled.sem, 1)

            def turn(it, n):
                u = UNITS[n]
                if u in ("g0", "g1"):
                    pe.wait_ge(*done(nrm_ok, it, int(u == "g1")))
                else:
                    pe.wait_ge(*done(exp_ok, it, n))
                pe.wait_ge(*done(pt_out, it, n - 1))
                for j in range(G):
                    m = nc.tensor.transpose(PT[0:N, j * N:(j + 1) * N], p[:, n % SLOTS, j, :], S.ident[0:N, 0:N])
                m.then_inc(pt_ps.sem, 1)

            def values(it, n):
                u = UNITS[n]
                pe.wait_ge(*done(pt_out, it, n))
                if u in ("g0", "g1"):
                    tile = HX0 if u == "g0" else HX1
                    pe.wait_ge(*(proj.copied(it, GV0) if u == "g0" else group.copied(it, GV1)))
                    pe.wait_ge(*group.free(it, tile))
                    for j in range(G):
                        m = mm(group.bank(tile)[0:GD, j * N:(j + 1) * N], gv[:, j, :], pT[:, n % 2, j, :], start=True, stop=True)
                    m.then_inc(group.filled.sem, 1)
                    return
                if u == 0:
                    pe.wait_ge(*proj.copied(it, V0))
                    pe.wait_ge(*proj.copied(it, V1))
                if u % HQ == 0:
                    pe.wait_ge(*done(o_ok, it, u // HQ - 1))
                r = 32 * (u % HQ)
                for j in range(G):
                    m = mm(O[r:r + 32, j * N:(j + 1) * N], v[:, j, u, :], pT[:, n % 2, j, :], start=True, stop=True,
                           tile_position=(0, r))
                m.then_inc(pv_ps.sem, 1)

            def back(it, g):
                pe.wait_ge(*done(ot_ok, it, g))
                for j in range(G):
                    m = nc.tensor.transpose(O[0:N, j * 128:(j + 1) * 128], ot[:, j * N:(j + 1) * N], S.ident[:])
                m.then_inc(back_ps.sem, 1)

            def late_o(it):
                pe.wait_ge(*done(o_ok, it, NQ - 1))
                transposed(it, group, O1, o, None)

            def late_h(it):
                pe.wait_ge(*group.copied(it, O2))
                for h in range(2):
                    if h:
                        pe.wait_ge(*group.free(it, HH0 + h))
                    for j in (2 * h, 2 * h + 1):
                        o_, t = group.bank(HH0 + h)[0:N, (j % 2) * D:(j % 2 + 1) * D], slice(j * N, (j + 1) * N)
                        mm(o_, out0[:, t], S.w1w[0:GD, 0, w.o:w.o + D], start=True, stop=False)
                        m = mm(o_, out1[:, t], S.w1w[:, 1, w.o:w.o + D], start=False, stop=True)
                    m.then_inc(group.filled.sem, 1)

            def lead():
                pre_x(0)
                pre_group(0)
                pre_qk(0, 0)
                for n in range(AHEAD):
                    scores(0, n)
                pre_qk(0, 1)
                pre_v(0)
                group_v(0, proj, GV0, 0, xa)

            def body(it, first, last):
                for n in range(NU):
                    if n + AHEAD < NU or not last:
                        scores(*unit(it, n + AHEAD))
                    if n == 6:
                        back(it, 0)
                    turn(it, n)
                    if n == 0 and not first:
                        late_o(it - 1)
                    if n == 1 and not first:
                        late_h(it - 1)
                    if n == 3:
                        second_group(it)
                    if n == 4 and not last:
                        pre_x(it + 1)
                    if n == 5 and not last:
                        pre_group(it + 1)
                    if n == 6 and not last:
                        pre_qk(it + 1, 0)
                    if n == 8 and not last:
                        pre_qk(it + 1, 1)
                    if n > 0:
                        values(it, n - 1)
                values(it, NU - 1)
                if not last:
                    pre_v(it + 1)
                back(it, 1)
                if not last:
                    group_v(it + 1, proj, GV0, 0, xa)

            def tail(it):
                late_o(it)
                late_h(it)

            steps(pe, lead, body, tail)

        @block.scalar
        def _(act):
            credit(act, proj.outs["act"], group.outs["act"], exp_ok, pt_out, ot_ok)
            cp = nc.scalar.activation

            def evac(it, tiles, n, out, rows_):
                act.wait_ge(*done(tiles.filled, it, n))
                cp(out, tiles.bank(n)[0:rows_, 0:GN], ACT.Copy).then_inc(tiles.out(n), 1)

            def pre_v(it):
                act.wait_ge(*done(proj.filled, it, V1))
                cp(v[:, 2:4, :, 0:HD], proj.bank(V1)[0:N, 0:2 * D].rearrange("p (g h d) -> p g h d", g=2, h=HEADS), ACT.Copy
                   ).then_inc(proj.out(V1), 1)

            def exp(it, n):
                act.wait_ge(*units.copied(it, n))
                pp = p[:, n % SLOTS, :, :]
                cp(pp, pp, ACT.Exp, scale=SCALE).then_inc(exp_ok.sem, 1)

            def outputs(it, g):
                act.wait_ge(*done(pv_ps, it, HQ * g + HQ - 1))
                act.wait_ge(*done(back_ps, it, g - 1))
                cp(ot[:], O[:, 0:GN], ACT.Copy).then_inc(ot_ok.sem, 1)

            def lead():
                evac(0, proj, X1, xa[:], GD)
                evac(0, proj, GQ0, gq[:], GD)
                evac(0, proj, GK0, gk[:], GD)
                evac(0, proj, Q0, q[:, 0, :], 128)
                for n in range(AHEAD):
                    exp(0, n)
                evac(0, proj, Q1, q[:, 1, :], 128)
                pre_v(0)

            def body(it, first, last):
                for n in range(NU):
                    act.wait_ge(*done(pt_ps, it, n))
                    cp(pT[:, n % 2, :, :], PT[0:N, 0:GN], ACT.Copy).then_inc(pt_out.sem, 1)
                    if n + AHEAD < NU or not last:
                        exp(*unit(it, n + AHEAD))
                    if n == 3:
                        evac(it, group, GQ1, gq[:], GD)
                        evac(it, group, GK1, gk[:], GD)
                    if n == 4 and not last:
                        evac(it + 1, proj, X1, xa[:], GD)
                    if n == 5 and not last:
                        evac(it + 1, proj, GQ0, gq[:], GD)
                        evac(it + 1, proj, GK0, gk[:], GD)
                    if n == 5:
                        outputs(it, 0)
                    if n == 6 and not last:
                        evac(it + 1, proj, Q0, q[:, 0, :], 128)
                    if n == 7:
                        evac(it, group, HX1, hx[:, 1, :], GD)
                    if n == 8 and not last:
                        evac(it + 1, proj, Q1, q[:, 1, :], 128)
                outputs(it, 1)
                if not last:
                    pre_v(it + 1)

            steps(act, lead, body, lambda it: None)

        @block.gpsimd
        def _(pool):
            credit(pool, veps_ok, rstd_ok)

            def power(it):
                pool.wait_ge(*done(mean_ok, it, G - 1))
                settle(pool, S)
                nc.gpsimd.tensor_scalar(veps[:], mv[:, :, 1], 1.0, EPS, ALU.mult, ALU.add).then_inc(veps_ok.sem, 1)
                pool.wait_ge(*done(veps_ok, it, 0))
                nc.gpsimd.tensor_tensor(rstd[:], veps[:], S.mhalf[0:N, 0:G], ALU.pow).then_inc(rstd_ok.sem, 1)

            def body(it, first, last):
                if not last:
                    power(it + 1)
                else:
                    early_root(nc, pool, S, 0)
                    early_root(nc, pool, S, 1)

            for n, (t, value) in enumerate(S.late_fill):
                if n:
                    pool.wait_ge(S.late_fill_ok, n)
                nc.gpsimd.memset(t, value).then_inc(S.late_fill_ok, 1)
            steps(pool, lambda: power(0), body, lambda it: None)

        @block.vector
        def _(dve):
            credit(dve, stat_ok, mean_ok, xn_ok, proj.outs["dve"], group.outs["dve"], units.outs["dve"], mx_ok, sum_ok, rec_ok,
                   nrm_ok, den_ok, o_ok)
            nv = nc.vector

            def evac(it, tiles, n, out, ap):
                dve.wait_ge(*done(tiles.filled, it, n))
                nv.tensor_copy(out, ap).then_inc(tiles.out(n), 1)

            def stat(it):
                hg = rows(it)
                settle(dve, S)
                for j in range(G):
                    nv.bn_stats(stats[:, j, :], hg[:, j, :]).then_inc(stat_ok.sem, 1)
                dve.wait_ge(*done(stat_ok, it, G - 1))
                settle(dve, S)
                for j in range(G):
                    nv.bn_aggr(mv[:, j, :], stats[:, j, :]).then_inc(mean_ok.sem, 1)

            def norm(it):
                hg = rows(it)
                dve.wait_ge(*done(mean_ok, it, G - 1))
                dve.wait_ge(*done(rstd_ok, it, 0))
                dve.wait_ge(*done(proj.filled, it, X2 - proj.filled.per))
                for j in range(G):
                    nv.tensor_scalar(xn[:, j, :], hg[:, j, :], mv[:, j, 0:1], rstd[:, j:j + 1],
                                     ALU.subtract, ALU.mult).then_inc(xn_ok.sem, 1)

            def pre_x(it):
                evac(it, proj, X2, xb[:], images(proj.bank(X2)[0:GD, 0:GN]))

            def pre_k(it, t):
                evac(it, proj, K0 + 2 * t, k[:, t, :], proj.bank(K0 + 2 * t)[:, 0:GN])

            def pre_v(it):
                evac(it, proj, V0, v[:, 0:2, :, 0:HD], proj.bank(V0)[0:N, 0:2 * D].rearrange("p (g h d) -> p g h d", g=2, h=HEADS))

            def pre_gv(it):
                evac(it, proj, GV0, gv[:], images(proj.bank(GV0)[0:N, 0:G * GD]))

            def softmax_in(it, n):
                sc = images(units.bank(n)[0:N, 0:GN])
                dve.wait_ge(*done(units.filled, it, n))
                nv.tensor_reduce(mx[:, n % 2, :], sc, AX.X, ALU.max).then_inc(mx_ok.sem, 1)
                dve.wait_ge(*done(mx_ok, it, n))
                dve.wait_ge(*done(pt_ps, it, n - SLOTS))
                nv.tensor_tensor(p[:, n % SLOTS, :, :], sc, bc(mx[:, n % 2, :].unsqueeze(2), [N, G, N]), ALU.subtract
                                 ).then_inc(units.out(n), 1)

            def normalise(it, i):
                n = UNITS.index("g1" if i else "g0")
                pp = p[:, n % SLOTS, :, :]
                dve.wait_ge(*done(exp_ok, it, n))
                nv.tensor_reduce(rs[:], pp, AX.X, ALU.add).then_inc(sum_ok.sem, 1)
                dve.wait_ge(*done(sum_ok, it, i))
                nv.reciprocal(ri[:], rs[:]).then_inc(rec_ok.sem, 1)
                dve.wait_ge(*done(rec_ok, it, i))
                nv.tensor_tensor(pp, pp, bc(ri[:].unsqueeze(2), [N, G, N]), ALU.mult).then_inc(nrm_ok.sem, 1)

            def first_result(it):
                dve.wait_ge(*done(group.filled, it, HX0))
                hx0 = group.bank(HX0)[0:GD, 0:GN]
                nv.tensor_tensor(cur[:], images(hx0), xb[:], ALU.add)
                nv.tensor_copy(hx[:, 0, :], hx0).then_inc(group.out(HX0), 1)

            def divide(it, g):
                tile = O[0:N, :].rearrange("p (g h d) -> p g h d", g=G, h=HQ)
                dve.wait_ge(*done(back_ps, it, g))
                nv.reciprocal(den[:], tile[:, :, :, HD]).then_inc(den_ok.sem, 1)
                dve.wait_ge(*done(den_ok, it, g))
                if g == 0:
                    dve.wait_ge(*done(group.filled, it - 1, O2))
                nv.tensor_tensor(o[:, :, g * HQ * HD:(g + 1) * HQ * HD].rearrange("p g (h d) -> p g h d", h=HQ),
                                 tile[:, :, :, 0:HD], bc(den[:].unsqueeze(3), [N, G, HQ, HD]), ALU.mult).then_inc(o_ok.sem, 1)

            def late_o(it):
                dve.wait_ge(*group.copied(it, HX1))
                for i, out in enumerate((out0[:], out1[0:GD, :])):
                    dve.wait_ge(*done(group.filled, it, O1 + i))
                    nv.tensor_tensor(out, group.bank(O1 + i)[0:GD, 0:GN], hx[:, i, :], ALU.add).then_inc(group.out(O1 + i), 1)

            def late_h(it):
                for h in range(2):
                    dve.wait_ge(*done(group.filled, it, HH0 + h))
                    hh = rows(it)[:, 2 * h:2 * h + 2, :]
                    nv.tensor_tensor(hh, group.bank(HH0 + h)[0:N, 0:2 * D].rearrange("p (g n) -> p g n", g=2), hh, ALU.add
                                     ).then_inc(group.out(HH0 + h), 1)

            def lead():
                stat(0)
                norm(0)
                pre_x(0)
                pre_k(0, 0)
                for n in range(AHEAD):
                    softmax_in(0, n)
                normalise(0, 0)
                pre_k(0, 1)
                pre_v(0)
                pre_gv(0)

            def body(it, first, last):
                for n in range(NU):
                    if n + AHEAD < NU or not last:
                        softmax_in(*unit(it, n + AHEAD))
                    if n == 0 and not first:
                        late_o(it - 1)
                    if n == 0 and not last:
                        stat(it + 1)
                    if n == 1 and last:
                        dve.wait_ge(*group.copied(0, HH0 + 1))
                        early_stat(nc, dve, S, 0, S.H[0:N, 0:G, :])
                    if n == 1 and not first:
                        late_h(it - 1)
                    if n == 3 and last:
                        early_norm(nc, dve, S, 0, S.H[0:N, 0:G, :], S.e_x)
                    if n == 4 and last:
                        early_stat(nc, dve, S, 1, S.e_x)
                    if n == 7 and last:
                        early_norm(nc, dve, S, 1, S.e_x, S.e_z)
                    if n == 2:
                        first_result(it)
                    if n == 2 and not last:
                        norm(it + 1)
                    if n == 3:
                        evac(it, group, GV1, gv[:], images(group.bank(GV1)[0:N, 0:G * GD]))
                    if n == 4 and not last:
                        pre_x(it + 1)
                    if n == 5:
                        normalise(it, 1)
                    if n == 6:
                        divide(it, 0)
                    if n == 6 and not last:
                        pre_k(it + 1, 0)
                    if n == 8 and not last:
                        pre_k(it + 1, 1)
                    if n == 9 and not last:
                        normalise(it + 1, 0)
                if not last:
                    pre_v(it + 1)
                divide(it, 1)
                if not last:
                    pre_gv(it + 1)

            def tail(it):
                late_o(it)
                late_h(it)

            steps(dve, lead, body, tail)


def ffn1_phase(nc, dram, S):
    HEADS, HD, MLP, RHD = 12, D // 12, 768, 128
    NU, KF = HEADS, MLP // 128
    TF, TH = D // 2, HEADS // 2
    HQ = 4
    NQ = HEADS // HQ
    AHEAD = 2
    with ExitStack() as ctx:
        def sb(name, shape, dt=F32):
            return ctx.enter_context(nc.sbuf_tensor("f_" + name, shape, dt))

        def sem(name, per):
            return counted(nc, ctx, "f_" + name, per)

        w, c = W4, C4
        stats, mv, veps, rstd = sb("stats", [N, 3, G, 6]), sb("mv", [N, 3, G, 2]), sb("veps", [N, 3, G]), sb("rstd", [N, 3, G])
        xnext, xmid, x = S.e_x, sb("xmid", [N, G, D]), sb("x", [N, G, D])
        z, hh, y = S.e_z, sb("hh", [N, G, D]), sb("y", [N, G, D])
        xa1, xa2, r1, r2 = sb("xa1", [LO, G, N]), S.f_xa2, sb("r1", [LO, GN]), sb("r2", [HI, GN])
        e, gm, gs = sb("e", [RHD, G, N]), sb("gm", [RHD, G]), sb("gs", [RHD, G])
        h1, h2 = sb("h1", [RHD, GN]), S.f_h2
        logit, bits, nbits, sel = sb("logit", [N, G, 4]), sb("bits", [N, G, 2]), sb("nbits", [N, G, 2]), sb("sel", [N, G, 3])
        q, qh, k, v = sb("q", [TF, 2, GN]), sb("qh", [TF, HEADS, GN]), sb("k", [TF, 2, GN]), S.f_v
        p, pT, mx = sb("p", [N, AHEAD + 1, G, N]), sb("pT", [N, 2, G, N]), sb("mx", [N, 2, G])
        ot, den, o = sb("ot", [128, 2, GN]), sb("den", [N, G, HQ]), sb("o", [N, G, D])
        o1, o2 = sb("o1", [LO, GN]), S.f_o2
        xf1, xf2, ff = sb("xf1", [LO, GN]), sb("xf2", [HI, GN]), sb("ff", [128, KF, GN])
        u1, u2, dn, d1, d2 = sb("u1", [LO, GN]), sb("u2", [HI, GN]), sb("dn", [N, G, 3, D // 3]), sb("d1", [LO, GN]), sb("d2", [HI, GN])
        bank = [ctx.enter_context(nc.psum_tensor(f"f_ps{i}", [128, 512], F32)) for i in range(8)]
        PT, O = bank[2], bank[3]
        units = Tiles(nc, ctx, "f_units", bank[0:2], ["dve"] * NU)
        Z1, Z2, R, H1, H2, Q0, K0, Q1, K1, V0, V1, LG = range(12)
        proj = Tiles(nc, ctx, "f_proj", bank[4:6], ["act", "dve", "act", "act", "act", "act", "dve", "act", "dve", "act", "dve", "dve"])
        O1, O2, WO, Y1, Y2, F, FO, U1, U2, DN, D1, D2, UP = 0, 1, 2, 4, 5, 6, 12, 14, 15, 16, 18, 19, 20
        late = Tiles(nc, ctx, "f_late", bank[6:8], ["act", "dve", "dve", "dve", "act", "dve"] + ["act"] * KF + ["dve", "dve", "act", "dve"]
                     + ["dve", "dve", "act", "dve", "dve", "dve"])

        stat_ok, mean_ok = [sem(f"stat_ok{i}", G) for i in range(3)], [sem(f"mean_ok{i}", G) for i in range(3)]
        veps_ok, rstd_ok = [sem(f"veps_ok{i}", 1) for i in range(3)], [sem(f"rstd_ok{i}", 1) for i in range(3)]
        x_ok, z_ok, y_ok = sem("x_ok", G), sem("z_ok", G), sem("y_ok", G)
        xmid_ok, xlast_ok, hx_ok = sem("xmid_ok", 1), sem("xlast_ok", 1), sem("hx_ok", 1)
        gm_ok, gs_ok, bit_ok, nb_ok, sel_ok = sem("gm_ok", 1), sem("gs_ok", 1), sem("bit_ok", 2), sem("nb_ok", 1), sem("sel_ok", 3)
        head_ok = [sem("head_act_ok", HEADS // 2), sem("head_pool_ok", HEADS // 2)]
        mx_ok, exp_ok = sem("mx_ok", NU), sem("exp_ok", NU)
        pt_ps, pt_out, pv_ps = sem("pt_ps", NU), sem("pt_out", NU), sem("pv_ps", NU)
        ot_ok, back_ps, den_ok, o_ok = (sem(n, NQ) for n in ("ot_ok", "back_ps", "den_ok", "o_ok"))
        hh_ok, out_ok = sem("hh_ok", G), sem("out_ok", G)
        stored = sem("stored", 16)
        block = ctx.enter_context(nc.Block())

        def unit(it, n):
            return (it + 1, n - NU) if n >= NU else (it, n)

        def rows(it):
            return S.H[0:N, :, :].rearrange("p b d -> p (b d)")[:, bass.ds(it * (G * D), G * D)].rearrange(
                "p (b d) -> p b d", b=G)

        def steps(eng, lead, body, tail):
            lead()
            body(0, True, False)
            with eng.Fori(1, STEPS - 1) as it:
                body(it, False, False)
            body(STEPS - 1, False, True)
            tail(STEPS - 1)

        def images(ap, g=G):
            return ap.rearrange("p (g n) -> p g n", g=g)

        @block.sync
        def _(sp):
            credit(sp, stored)

            def store(it):
                sp.wait_ge(*late.copied(it, UP + 1))
                settle(sp, S)
                sp.dma_start(dram.out[bass.ds(it * G, G), :, :].rearrange("b t d -> t b d"), rows(it)).then_inc(stored.sem, 16)

            def body(it, first, last):
                if not first:
                    store(it - 1)

            steps(sp, lambda: None, body, store)
            sp.wait_ge(*done(stored, STEPS - 1, 15))

        @block.tensor
        def _(pe):
            credit(pe, proj.filled, late.filled, units.filled, pt_ps, pv_ps, back_ps)
            mm = nc.tensor.matmul

            def linear(o, lo, hi, xs):
                mm(o, lo, xs[0], start=True, stop=False)
                return mm(o, hi, xs[1], start=False, stop=True)

            def cols(col, n):
                return S.w4a[:, col:col + n], S.w4b[0:HI, col:col + n]

            def transposed(it, tiles, n, src, ok):
                pe.wait_ge(*tiles.free(it, n + 1))
                pe.wait_ge(*tiles.free(it, n))
                for m, c0, c1 in ((n, 0, LO), (n + 1, LO, D)):
                    for j in range(G):
                        if m == n and ok is not None:
                            pe.wait_ge(*done(ok, it, j))
                        i = nc.tensor.transpose(tiles.bank(m)[0:c1 - c0, j * N:(j + 1) * N], src[:, j, c0:c1], S.ident[0:N, 0:N])
                    i.then_inc(tiles.filled.sem, 1)

            def by_image(o, h, lo, hi, col, hi_rows):
                for j in (2 * h, 2 * h + 1):
                    t = slice(j * N, (j + 1) * N)
                    m = linear(o[0:N, (j % 2) * D:(j % 2 + 1) * D], lo[:, t], hi[:, t],
                               (S.w4a[:, col:col + D], S.w4b[0:hi_rows, col:col + D]))
                return m

            def pre_z(it):
                transposed(it, proj, Z1, z, z_ok)

            def pre_features(it):
                pe.wait_ge(*proj.copied(it, Z1))
                pe.wait_ge(*proj.copied(it, Z2))
                pe.wait_ge(*proj.free(it, R))
                linear(proj.bank(R)[:, 0:GN], *cols(w.r, RHD), (r1[:], r2[:])).then_inc(proj.filled.sem, 1)

            def pre_router1(it):
                pe.wait_ge(*done(gs_ok, it, 0))
                pe.wait_ge(*proj.copied(it, R))
                o = proj.bank(H1)[:, 0:GN]
                mm(o, S.ro1[:, 0, :], e[:], start=True, stop=False)
                mm(images(o), S.ro1[:, 1, :], bc(gs[:].unsqueeze(2), [RHD, G, N]), start=False, stop=True
                   ).then_inc(proj.filled.sem, 1)

            def pre_router2(it):
                pe.wait_ge(*proj.copied(it, H1))
                mm(proj.bank(H2)[0:RHD // 2, 0:GN], S.ro2[:], h1[:], start=True, stop=True).then_inc(proj.filled.sem, 1)

            def pre_qk(it, t):
                for n, col in ((Q0 + 2 * t, w.q), (K0 + 2 * t, w.k)):
                    pe.wait_ge(*proj.free(it, n))
                    linear(proj.bank(n)[0:TF, 0:GN], *cols(col + TF * t, TF), (xa1[:], xa2[0:HI, :])).then_inc(proj.filled.sem, 1)

            def pre_v(it):
                for h in range(2):
                    pe.wait_ge(*proj.free(it, V0 + h))
                    by_image(proj.bank(V0 + h), h, xa1[:].rearrange("p g n -> p (g n)"), xa2[:], w.v, HI + 1
                             ).then_inc(proj.filled.sem, 1)

            def pre_logits(it):
                pe.wait_ge(*proj.copied(it, H2))
                pe.wait_ge(*proj.free(it, LG))
                for j in range(G):
                    m = mm(proj.bank(LG)[0:N, 4 * j:4 * j + 4], h2[:, j * N:(j + 1) * N], S.ro3[:], start=True, stop=True)
                m.then_inc(proj.filled.sem, 1)

            def scores(it, n):
                if n % TH == 0:
                    pe.wait_ge(*proj.copied(it, K0 + 2 * (n // TH)))
                pe.wait_ge(*done(head_ok[n % 2], it, n // 2))
                pe.wait_ge(*units.free(it, n))
                for j in range(G):
                    s = slice(j * N, (j + 1) * N)
                    m = mm(units.bank(n)[0:N, s], qh[:, n, s], k[:, n // TH, s], start=True, stop=True)
                m.then_inc(units.filled.sem, 1)

            def turn(it, n):
                pe.wait_ge(*done(exp_ok, it, n))
                pe.wait_ge(*done(pt_out, it, n - 1))
                for j in range(G):
                    m = nc.tensor.transpose(PT[0:N, j * N:(j + 1) * N], p[:, n % (AHEAD + 1), j, :], S.ident[0:N, 0:N])
                m.then_inc(pt_ps.sem, 1)

            def values(it, n):
                pe.wait_ge(*done(pt_out, it, n))
                if n == 0:
                    pe.wait_ge(*proj.copied(it, V0))
                    pe.wait_ge(*proj.copied(it, V1))
                if n % HQ == 0:
                    pe.wait_ge(*done(o_ok, it, n // HQ - 1))
                r = 32 * (n % HQ)
                for j in range(G):
                    m = mm(O[r:r + 32, j * N:(j + 1) * N], v[:, j, n, :], pT[:, n % 2, j, :], start=True, stop=True,
                           tile_position=(0, r))
                m.then_inc(pv_ps.sem, 1)

            def back(it, g):
                pe.wait_ge(*done(ot_ok, it, g))
                for j in range(G):
                    m = nc.tensor.transpose(O[0:N, j * 128:(j + 1) * 128], ot[:, g % 2, j * N:(j + 1) * N], S.ident[:])
                m.then_inc(back_ps.sem, 1)

            def late_o(it):
                pe.wait_ge(*done(o_ok, it, NQ - 1))
                transposed(it, late, O1, o, None)

            def late_wo(it):
                pe.wait_ge(*late.copied(it, O2))
                pe.wait_ge(*late.copied(it, O1))
                for h in range(2):
                    by_image(late.bank(WO + h), h, o1[:], o2[:], w.o, HI + 1).then_inc(late.filled.sem, 1)

            def late_y(it):
                transposed(it, late, Y1, y, y_ok)

            def late_features(it, f):
                if f == 0:
                    pe.wait_ge(*late.copied(it, Y2))
                    pe.wait_ge(*late.copied(it, Y1))
                else:
                    pe.wait_ge(*late.free(it, F + f))
                linear(late.bank(F + f)[:, 0:GN], *cols(w.f + 128 * f, 128), (xf1[:], xf2[:])).then_inc(late.filled.sem, 1)

            def late_mlp(it, h):
                pe.wait_ge(*late.copied(it, F + KF - 1))
                if h:
                    pe.wait_ge(*late.free(it, FO + h))
                for j in (2 * h, 2 * h + 1):
                    o = late.bank(FO + h)[0:N, (j % 2) * D:(j % 2 + 1) * D]
                    mm(o, S.ones1[:], S.fc2b[:], start=True, stop=False)
                    for f in range(KF):
                        m = mm(o, ff[:, f, j * N:(j + 1) * N], S.fc2[:, f, :], start=False, stop=(f == KF - 1))
                m.then_inc(late.filled.sem, 1)

            def late_u(it):
                transposed(it, late, U1, hh, out_ok)

            def late_down(it):
                pe.wait_ge(*late.copied(it, U1))
                pe.wait_ge(*late.copied(it, U2))
                by_image(late.bank(DN), 0, u1[:], u2[:], w.dn, HI).then_inc(late.filled.sem, 1)
                by_image(late.bank(DN + 1), 1, u1[:], u2[:], w.dn, HI).then_inc(late.filled.sem, 1)

            def late_d(it):
                pe.wait_ge(*late.copied(it, DN + 1))
                transposed(it, late, D1, dn[:].rearrange("p g k r -> p g (k r)"), None)

            def late_up(it):
                pe.wait_ge(*late.copied(it, D1))
                pe.wait_ge(*late.copied(it, D2))
                by_image(late.bank(UP), 0, d1[:], d2[:], w.up, HI).then_inc(late.filled.sem, 1)
                by_image(late.bank(UP + 1), 1, d1[:], d2[:], w.up, HI).then_inc(late.filled.sem, 1)

            def lead():
                pre_z(0)
                pre_features(0)
                pre_router1(0)
                pre_router2(0)
                for t in range(2):
                    pre_qk(0, t)
                pre_v(0)
                pre_logits(0)
                for n in range(AHEAD):
                    scores(0, n)

            def body(it, first, last):
                for n in range(NU):
                    if n + AHEAD < NU or not last:
                        scores(*unit(it, n + AHEAD))
                    if n in (5, 9):
                        back(it, n // 4 - 1)
                    turn(it, n)
                    if n == 0 and not first:
                        late_o(it - 1)
                    if n == 1 and not first:
                        late_wo(it - 1)
                    if n == 4 and not first:
                        late_y(it - 1)
                    if n == 5 and not last:
                        pre_z(it + 1)
                    if n == 6:
                        for m in range(3):
                            if not first:
                                late_features(it - 1, 2 * m)
                                late_features(it - 1, 2 * m + 1)
                            if not last:
                                (pre_features, pre_router1, pre_router2)[m](it + 1)
                    if n == 7 and not last:
                        pre_qk(it + 1, 0)
                    if n == 7 and not first:
                        late_mlp(it - 1, 0)
                    if n == 8 and not first:
                        late_mlp(it - 1, 1)
                    if n == 9 and not first:
                        late_u(it - 1)
                    if n == 10 and not last:
                        pre_qk(it + 1, 1)
                    if n == 10 and not first:
                        late_down(it - 1)
                    if n == 11 and not first:
                        late_d(it - 1)
                    if n > 0:
                        values(it, n - 1)
                values(it, NU - 1)
                if not first:
                    late_up(it - 1)
                if not last:
                    pre_v(it + 1)
                back(it, NQ - 1)
                if not last:
                    pre_logits(it + 1)

            def tail(it):
                late_o(it)
                late_wo(it)
                late_y(it)
                for f in range(KF):
                    late_features(it, f)
                late_mlp(it, 0)
                late_mlp(it, 1)
                late_u(it)
                late_down(it)
                late_d(it)
                late_up(it)

            steps(pe, lead, body, tail)

        @block.scalar
        def _(act):
            credit(act, proj.outs["act"], late.outs["act"], exp_ok, pt_out, ot_ok, head_ok[0])
            cp = nc.scalar.activation

            def evac(it, tiles, n, out, rows_=128, func=ACT.Copy, **kw):
                act.wait_ge(*done(tiles.filled, it, n))
                cp(out, tiles.bank(n)[0:rows_, 0:GN], func, **kw).then_inc(tiles.out(n), 1)

            def col(i):
                return S.c4a[:, i:i + 1]

            def pre_z(it):
                act.wait_ge(*done(proj.filled, it, Z1))
                t = proj.bank(Z1)[0:LO, 0:GN]
                cp(r1[:], t, ACT.Identity, scale=col(c.rg), bias=col(c.rb))
                cp(xa1[:], images(t), ACT.Identity, scale=col(c.g1), bias=col(c.b1)).then_inc(proj.out(Z1), 1)

            def pre_features(it):
                act.wait_ge(*done(proj.filled, it, R))
                act.wait_ge(*done(gm_ok, it, -1))
                cp(e[:], images(proj.bank(R)[0:RHD, 0:GN]), ACT.Gelu, bias=col(c.r)).then_inc(proj.out(R), 1)

            def pre_router1(it):
                evac(it, proj, H1, h1[:], RHD, ACT.Gelu, bias=col(c.h1))

            def pre_router2(it):
                evac(it, proj, H2, h2[0:RHD // 2, :], RHD // 2, ACT.Gelu, bias=S.c4a[0:RHD // 2, c.h2:c.h2 + 1])

            def pre_q(it, t):
                evac(it, proj, Q0 + 2 * t, q[:, t, :], TF, ACT.Identity, bias=S.c4a[0:TF, c.q + t:c.q + t + 1])
                act.wait_ge(*proj.copied(it, Q0 + 2 * t))
                for h in range(0, TH, 2):
                    cp(qh[:, TH * t + h, :], q[:, t, :], ACT.Copy, scale=S.c4a[0:TF, c.mask + h:c.mask + h + 1]
                       ).then_inc(head_ok[0].sem, 1)

            def pre_v(it):
                act.wait_ge(*done(proj.filled, it, V0))
                cp(v[:, 0:2, :, 0:HD], proj.bank(V0)[0:N, 0:2 * D].rearrange("p (g h d) -> p g h d", g=2, h=HEADS), ACT.Copy
                   ).then_inc(proj.out(V0), 1)

            def outputs(it, g):
                act.wait_ge(*done(pv_ps, it, HQ * g + HQ - 1))
                act.wait_ge(*done(back_ps, it, before(g, 2, NQ)))
                cp(ot[:, g % 2, :], O[:, 0:GN], ACT.Copy).then_inc(ot_ok.sem, 1)

            def exp(it, n):
                act.wait_ge(*units.copied(it, n))
                pp = p[:, n % (AHEAD + 1), :, :]
                cp(pp, pp, ACT.Exp, scale=float(HD) ** -0.5).then_inc(exp_ok.sem, 1)

            def late_o(it):
                evac(it, late, O1, o1[:], LO)

            def late_y(it):
                evac(it, late, Y1, xf1[:], LO, ACT.Identity, scale=col(c.g2), bias=col(c.b2))

            def late_features(it, f):
                evac(it, late, F + f, ff[:, f, :], 128, ACT.Gelu, bias=col(c.f + f))

            def late_u(it):
                evac(it, late, U1, u1[:], LO)

            def late_d(it):
                evac(it, late, D1, d1[:], LO)

            def lead():
                pre_z(0)
                pre_features(0)
                pre_router1(0)
                pre_router2(0)
                for t in range(2):
                    pre_q(0, t)
                pre_v(0)
                for n in range(AHEAD):
                    exp(0, n)

            def body(it, first, last):
                for n in range(NU):
                    act.wait_ge(*done(pt_ps, it, n))
                    cp(pT[:, n % 2, :, :], PT[0:N, 0:GN], ACT.Copy).then_inc(pt_out.sem, 1)
                    if n == 0 and not first:
                        late_o(it - 1)
                    if n + AHEAD < NU or not last:
                        exp(*unit(it, n + AHEAD))
                    if n == 4 and not first:
                        late_y(it - 1)
                    if n == 4:
                        outputs(it, 0)
                    if n == 5 and not last:
                        pre_z(it + 1)
                    if n == 6:
                        for m in range(3):
                            if not first:
                                late_features(it - 1, 2 * m)
                                late_features(it - 1, 2 * m + 1)
                            if not last:
                                (pre_features, pre_router1, pre_router2)[m](it + 1)
                    if n == 7 and not last:
                        pre_q(it + 1, 0)
                    if n == 8:
                        outputs(it, 1)
                    if n == 9 and not first:
                        late_u(it - 1)
                    if n == 10 and not last:
                        pre_q(it + 1, 1)
                    if n == 11 and not first:
                        late_d(it - 1)
                outputs(it, NQ - 1)
                if not last:
                    pre_v(it + 1)

            def tail(it):
                late_o(it)
                late_y(it)
                for f in range(KF):
                    late_features(it, f)
                late_u(it)
                late_d(it)

            steps(act, lead, body, tail)

        @block.gpsimd
        def _(pool):
            credit(pool, *veps_ok, *rstd_ok, xmid_ok, xlast_ok, hx_ok, head_ok[1])

            def power(it, i):
                pool.wait_ge(*done(mean_ok[i], it, G - 1))
                settle(pool, S)
                nc.gpsimd.tensor_scalar(veps[:, i, :], mv[:, i, :, 1], 1.0, EPS, ALU.mult, ALU.add).then_inc(veps_ok[i].sem, 1)
                pool.wait_ge(*done(veps_ok[i], it, 0))
                nc.gpsimd.tensor_tensor(rstd[:, i, :], veps[:, i, :], S.mhalf[0:N, 0:G], ALU.pow).then_inc(rstd_ok[i].sem, 1)

            def keep_mid(it):
                pool.wait_ge(*done(xlast_ok, it, -1))
                pool.wait_ge(*done(x_ok, it, G - 1))
                settle(pool, S)
                nc.gpsimd.tensor_copy(xmid[:], xnext[:]).then_inc(xmid_ok.sem, 1)

            def keep_last(it):
                pool.wait_ge(*done(hh_ok, it, -1))
                pool.wait_ge(*done(xmid_ok, it, 0))
                settle(pool, S)
                nc.gpsimd.tensor_copy(x[:], xmid[:]).then_inc(xlast_ok.sem, 1)

            def heads(it, t):
                pool.wait_ge(*proj.copied(it, Q0 + 2 * t))
                settle(pool, S)
                for h in range(1, TH, 2):
                    nc.gpsimd.tensor_scalar(qh[:, TH * t + h, :], q[:, t, :], S.c4a[0:TF, c.mask + h:c.mask + h + 1], None, ALU.mult
                                            ).then_inc(head_ok[1].sem, 1)

            def out(it):
                pool.wait_ge(*done(out_ok, it, G - 1))
                hg = rows(it)
                nc.gpsimd.tensor_tensor(hg, hg, hh[:], ALU.add).then_inc(hx_ok.sem, 1)

            def lead():
                credit(pool, veps_ok[0], veps_ok[1], rstd_ok[0], rstd_ok[1])
                keep_mid(0)
                heads(0, 0)
                heads(0, 1)

            def body(it, first, last):
                if not last:
                    power(it + 1, 0)
                if not first:
                    power(it - 1, 2)
                if not last:
                    power(it + 1, 1)
                keep_last(it)
                if not last:
                    keep_mid(it + 1)
                    heads(it + 1, 0)
                if not first:
                    out(it - 1)
                if not last:
                    heads(it + 1, 1)

            def tail(it):
                power(it, 2)
                out(it)

            steps(pool, lead, body, tail)

        @block.vector
        def _(dve):
            credit(dve, *stat_ok, *mean_ok, x_ok, z_ok, y_ok, proj.outs["dve"], late.outs["dve"], units.outs["dve"],
                   gm_ok, gs_ok, bit_ok, nb_ok, sel_ok, mx_ok, den_ok, o_ok, hh_ok, out_ok)
            nv = nc.vector

            def stat(it, i, src):
                settle(dve, S)
                for j in range(G):
                    nv.bn_stats(stats[:, i, j, :], src[:, j, :]).then_inc(stat_ok[i].sem, 1)
                dve.wait_ge(*done(stat_ok[i], it, G - 1))
                settle(dve, S)
                for j in range(G):
                    nv.bn_aggr(mv[:, i, j, :], stats[:, i, j, :]).then_inc(mean_ok[i].sem, 1)

            def norm(it, i, src, out, ok):
                dve.wait_ge(*done(mean_ok[i], it, G - 1))
                dve.wait_ge(*done(rstd_ok[i], it, 0))
                for j in range(G):
                    nv.tensor_scalar(out[:, j, :], src[:, j, :], mv[:, i, j, 0:1], rstd[:, i, j:j + 1],
                                     ALU.subtract, ALU.mult).then_inc(ok.sem, 1)

            def colb(i):
                return S.c4b[:, i:i + 1]

            def pair(tiles, n):
                return tiles.bank(n)[0:N, 0:2 * D].rearrange("p (g n) -> p g n", g=2)

            def pre_x(it):
                dve.wait_ge(*done(xmid_ok, it, -1))
                norm(it, 0, rows(it), xnext, x_ok)

            def pre_stat(it):
                dve.wait_ge(*done(x_ok, it, G - 1))
                stat(it, 1, xnext)

            def pre_z(it):
                dve.wait_ge(*done(proj.filled, it, Z2 - proj.filled.per))
                norm(it, 1, xnext, z, z_ok)

            def pre_z_copy(it):
                dve.wait_ge(*done(proj.filled, it, Z2))
                t = proj.bank(Z2)[0:HI, 0:GN]
                nv.tensor_scalar(r2[:], t, colb(c.rg), colb(c.rb), ALU.mult, ALU.add)
                nv.tensor_scalar(xa2[0:HI, :], t, colb(c.g1), colb(c.b1), ALU.mult, ALU.add).then_inc(proj.out(Z2), 1)

            def pre_mean(it):
                dve.wait_ge(*proj.copied(it, R))
                nv.tensor_reduce(gm[:], e[:, :, 1:N], AX.X, ALU.add).then_inc(gm_ok.sem, 1)
                dve.wait_ge(*done(gm_ok, it, 0))
                nv.tensor_scalar(gs[:], gm[:], 1.0 / (N - 1), None, ALU.mult).then_inc(gs_ok.sem, 1)

            def pre_k(it, t):
                dve.wait_ge(*done(proj.filled, it, K0 + 2 * t))
                nv.tensor_scalar(k[:, t, :], proj.bank(K0 + 2 * t)[0:TF, 0:GN], S.c4a[0:TF, c.k + t:c.k + t + 1], None, ALU.add
                                 ).then_inc(proj.out(K0 + 2 * t), 1)

            def pre_v(it):
                dve.wait_ge(*done(proj.filled, it, V1))
                nv.tensor_copy(v[:, 2:4, :, 0:HD], proj.bank(V1)[0:N, 0:2 * D].rearrange("p (g h d) -> p g h d", g=2, h=HEADS)
                               ).then_inc(proj.out(V1), 1)

            def softmax_in(it, n):
                sc = images(units.bank(n)[0:N, 0:GN])
                dve.wait_ge(*done(units.filled, it, n))
                nv.tensor_reduce(mx[:, n % 2, :], sc, AX.X, ALU.max).then_inc(mx_ok.sem, 1)
                dve.wait_ge(*done(mx_ok, it, n))
                dve.wait_ge(*done(pt_ps, it, n - AHEAD - 1))
                nv.tensor_tensor(p[:, n % (AHEAD + 1), :, :], sc, bc(mx[:, n % 2, :].unsqueeze(2), [N, G, N]), ALU.subtract
                                 ).then_inc(units.out(n), 1)

            def pre_logits(it):
                dve.wait_ge(*done(proj.filled, it, LG))
                nv.tensor_copy(logit[:], images(proj.bank(LG)[0:N, 0:4 * G])).then_inc(proj.out(LG), 1)

            def router(it):
                dve.wait_ge(*proj.copied(it, LG))
                two = logit[:].rearrange("p g (b t) -> p g b t", t=2)
                nv.tensor_tensor(bits[:], two[:, :, :, 1], two[:, :, :, 0], ALU.is_gt).then_inc(bit_ok.sem, 1)
                dve.wait_ge(*done(bit_ok, it, 0))
                nv.memset(bits[0:1, :, :], 1.0).then_inc(bit_ok.sem, 1)
                dve.wait_ge(*done(bit_ok, it, 1))
                nv.tensor_scalar(nbits[:], bits[:], -1.0, 1.0, ALU.mult, ALU.add).then_inc(nb_ok.sem, 1)
                dve.wait_ge(*done(nb_ok, it, 0))
                for i, (a_, b_) in enumerate(((nbits, nbits), (nbits, bits), (bits, nbits))):
                    nv.tensor_tensor(sel[:, :, i], a_[:, :, 0], b_[:, :, 1], ALU.mult).then_inc(sel_ok.sem, 1)

            def divide(it, g):
                tile = O[0:N, :].rearrange("p (g h d) -> p g h d", g=G, h=HQ)
                dve.wait_ge(*done(back_ps, it, g))
                nv.reciprocal(den[:], tile[:, :, :, HD]).then_inc(den_ok.sem, 1)
                dve.wait_ge(*done(den_ok, it, g))
                if g == 0:
                    dve.wait_ge(*done(late.filled, it - 1, O2))
                nv.tensor_tensor(o[:, :, g * HQ * HD:(g + 1) * HQ * HD].rearrange("p g (h d) -> p g h d", h=HQ),
                                 tile[:, :, :, 0:HD], bc(den[:].unsqueeze(3), [N, G, HQ, HD]), ALU.mult).then_inc(o_ok.sem, 1)

            def late_o(it):
                dve.wait_ge(*done(late.filled, it, O2))
                nv.tensor_copy(o2[0:HI, :], late.bank(O2)[0:HI, 0:GN]).then_inc(late.out(O2), 1)

            def late_hh(it):
                dve.wait_ge(*done(xlast_ok, it, 0))
                dve.wait_ge(*done(hx_ok, it, -1))
                dve.wait_ge(*done(sel_ok, it, 2))
                for h in range(2):
                    dve.wait_ge(*done(late.filled, it, WO + h))
                    t = pair(late, WO + h)
                    for j in (2 * h, 2 * h + 1):
                        nv.scalar_tensor_tensor(out=hh[:, j, :], in0=t[:, j % 2, :], scalar=bits[:, j, 0:1], in1=x[:, j, :],
                                                op0=ALU.mult, op1=ALU.add).then_inc(hh_ok.sem, 1)
                    dve.wait_ge(*done(hh_ok, it, 2 * h + 1))
                    dve.sem_inc(late.out(WO + h), 1)

            def late_y(it):
                norm(it, 2, hh, y, y_ok)

            def late_y_copy(it):
                dve.wait_ge(*done(late.filled, it, Y2))
                nv.tensor_scalar(xf2[:], late.bank(Y2)[0:HI, 0:GN], colb(c.g2), colb(c.b2), ALU.mult, ALU.add
                                 ).then_inc(late.out(Y2), 1)

            def late_mlp(it, h):
                dve.wait_ge(*done(late.filled, it, FO + h))
                t = pair(late, FO + h)
                for j in (2 * h, 2 * h + 1):
                    nv.scalar_tensor_tensor(out=hh[:, j, :], in0=t[:, j % 2, :], scalar=bits[:, j, 1:2], in1=hh[:, j, :],
                                            op0=ALU.mult, op1=ALU.add).then_inc(out_ok.sem, 1)
                dve.wait_ge(*done(out_ok, it, 2 * h + 1))
                dve.sem_inc(late.out(FO + h), 1)

            def late_u(it):
                dve.wait_ge(*done(late.filled, it, U2))
                nv.tensor_copy(u2[:], late.bank(U2)[0:HI, 0:GN]).then_inc(late.out(U2), 1)

            def late_down(it):
                for h in range(2):
                    dve.wait_ge(*done(late.filled, it, DN + h))
                    t = pair(late, DN + h).rearrange("p g (k r) -> p g k r", k=3)
                    nv.tensor_tensor(dn[:, 2 * h:2 * h + 2, :, :], t, bc(sel[:, 2 * h:2 * h + 2, :].unsqueeze(3),
                                     [N, 2, 3, D // 3]), ALU.mult).then_inc(late.out(DN + h), 1)

            def late_d(it):
                dve.wait_ge(*done(late.filled, it, D2))
                nv.tensor_copy(d2[:], late.bank(D2)[0:HI, 0:GN]).then_inc(late.out(D2), 1)

            def late_up(it):
                dve.wait_ge(*done(hx_ok, it, 0))
                for h in range(2):
                    dve.wait_ge(*done(late.filled, it, UP + h))
                    hj = rows(it)[:, 2 * h:2 * h + 2, :]
                    nv.tensor_tensor(hj, pair(late, UP + h), hj, ALU.add).then_inc(late.out(UP + h), 1)

            def lead():
                credit(dve, stat_ok[0], mean_ok[0], x_ok, stat_ok[1], mean_ok[1], z_ok)
                pre_z_copy(0)
                pre_mean(0)
                for t in range(2):
                    pre_k(0, t)
                pre_v(0)
                pre_logits(0)
                for n in range(AHEAD):
                    softmax_in(0, n)

            def body(it, first, last):
                for n in range(NU):
                    if n + AHEAD < NU or not last:
                        softmax_in(*unit(it, n + AHEAD))
                    if n in (5, 9):
                        divide(it, n // 4 - 1)
                    if n == 0 and not first:
                        late_o(it - 1)
                    if n == 0 and not last:
                        stat(it + 1, 0, rows(it + 1))
                    if n == 1 and not first:
                        late_hh(it - 1)
                    if n == 2 and not first:
                        stat(it - 1, 2, hh)
                    if n == 2 and not last:
                        pre_x(it + 1)
                    if n == 3 and not last:
                        pre_stat(it + 1)
                    if n == 3 and not first:
                        late_y(it - 1)
                    if n == 4 and not first:
                        late_y_copy(it - 1)
                    if n == 4 and not last:
                        pre_z(it + 1)
                    if n == 5 and not last:
                        pre_z_copy(it + 1)
                    if n == 6 and not last:
                        pre_mean(it + 1)
                    if n == 7 and not last:
                        pre_k(it + 1, 0)
                    if n == 7 and not first:
                        late_mlp(it - 1, 0)
                    if n == 8 and not first:
                        late_mlp(it - 1, 1)
                    if n == 9 and not first:
                        late_u(it - 1)
                    if n == 10 and not last:
                        pre_k(it + 1, 1)
                    if n == 10 and not first:
                        late_down(it - 1)
                    if n == 11 and not first:
                        late_d(it - 1)
                router(it)
                if not first:
                    late_up(it - 1)
                if not last:
                    pre_v(it + 1)
                divide(it, NQ - 1)
                if not last:
                    pre_logits(it + 1)

            def tail(it):
                late_o(it)
                late_hh(it)
                stat(it, 2, hh)
                late_y(it)
                late_y_copy(it)
                late_mlp(it, 0)
                late_mlp(it, 1)
                late_u(it)
                late_down(it)
                late_d(it)
                late_up(it)

            steps(dve, lead, body, tail)


def program(nc, dram):
    with ExitStack() as ctx:
        def sb(name, shape, dt=F32):
            return ctx.enter_context(nc.sbuf_tensor(name, shape, dt))

        S = Names()
        S.H = sb("H", [128, B, D])
        S.ident, S.iota, S.mhalf = sb("ident", [128, 128]), sb("iota", [128, E]), sb("mhalf", [128, 8])
        S.consts_ok = ctx.enter_context(nc.semaphore("consts_ok"))
        S.settled = ctx.enter_context(nc.semaphore("settled"))
        S.weights_in = ctx.enter_context(nc.semaphore("weights_in"))
        o0 = dram.w0a.shape[1]
        S.w0a, S.w0b = sb("w0a", [LO, o0]), sb("w0b", [HI + 1, o0])
        S.c0a, S.c0b = sb("c0a", [LO, 3]), sb("c0b", [HI, 3])
        S.cat1, S.cat2 = sb("cat1", [LO, G, NK]), sb("cat2", [HI + 1, G, NK])
        S.a0_o2, S.a0_tS2 = sb("a0_o2", [HI + 1, G, N]), sb("a0_tS2", [HI + 33, G, N])
        S.t1, S.t2, S.fwT = sb("t1", [LO, B * N]), sb("t2", [HI + 33, B * N]), sb("fwT", [E, B * N])
        S.w1w, S.w1g = sb("w1w", [D // 2 + 1, 2, 512 + 2 * D]), sb("w1g", [D // 2, 2, 3 * D // 2])
        S.a1_v, S.a1_out1 = sb("a1_v", [N, G, 8, 32]), sb("a1_out1", [D // 2 + 1, GN])
        S.fills = [(S.a1_v[:], 0.0)]
        S.fills += [(t, 1.0) for t in (S.a1_v[:, :, :, D // 8:D // 8 + 1], S.a1_out1[D // 2:D // 2 + 1, :],
                                       S.cat2[HI:HI + 1, :, :], S.a0_o2[HI:HI + 1, :, :], S.a0_tS2[HI:HI + 33, :, :])]
        S.b2 = sb("b2", [E, D])
        S.n_consts = 3 + len(S.fills)
        S.loads = [(S.w0a[:], dram.w0a), (S.w0b[:], dram.w0b), (S.c0a[:], dram.c0a), (S.c0b[:], dram.c0b)]
        S.loads += [(S.cat1[:, j, N:NK], dram.mem[0:LO, :]) for j in range(G)]
        S.loads += [(S.cat2[0:HI, j, N:NK], dram.mem[LO:D, :]) for j in range(G)]
        S.loads += [(S.b2[:], dram.b2), (S.w1w[:], dram.w1w), (S.w1g[:], dram.w1g)]
        tok_phase(nc, dram, S)
        with ExitStack() as early:
            experts_memory(nc, early, S)
            attn0_phase(nc, dram, S)
            experts_phase(nc, dram, S)
        S.w4a, S.w4b = sb("w4a", [LO, W4.width]), sb("w4b", [HI + 1, W4.width])
        S.c4a, S.c4b = sb("c4a", [LO, 25]), sb("c4b", [HI, 6])
        S.ro1, S.ro2, S.ro3 = sb("ro1", [128, 2, 128]), sb("ro2", [128, 64]), sb("ro3", [65, 4])
        S.fc2, S.fc2b, S.ones1 = sb("fc2", [128, 6, D]), sb("fc2b", [1, D]), sb("ones1", [1, N])
        S.f_xa2, S.f_o2, S.f_h2 = sb("f_xa2", [HI + 1, GN]), sb("f_o2", [HI + 1, GN]), sb("f_h2", [65, GN])
        S.f_v = sb("f_v", [N, G, 12, 32])
        S.late_fill = [(S.f_v[:], 0.0), (S.f_xa2[HI:HI + 1, :], 1.0), (S.f_o2[HI:HI + 1, :], 1.0), (S.f_h2[64:65, :], 1.0),
                       (S.f_v[:, :, :, D // 12:D // 12 + 1], 1.0), (S.ones1[:], 1.0)]
        S.late_loads = [(t[:], d) for t, d in ((S.w4a, dram.w4a), (S.w4b, dram.w4b), (S.c4a, dram.c4a), (S.c4b, dram.c4b),
                                               (S.ro1, dram.ro1), (S.ro2, dram.ro2), (S.ro3, dram.ro3), (S.fc2, dram.fc2),
                                               (S.fc2b, dram.fc2b))]
        S.late_fill_ok = ctx.enter_context(nc.semaphore("late_fill_ok"))
        S.early_ok = ctx.enter_context(nc.semaphore("early_ok"))
        S.e_stats, S.e_mv, S.e_veps, S.e_rstd = sb("e_stats", [N, G, 6]), sb("e_mv", [N, G, 2]), sb("e_veps", [N, G]), sb("e_rstd", [N, G])
        S.e_x, S.e_z = sb("e_x", [N, G, D]), sb("e_z", [N, G, D])
        S.late_in = ctx.enter_context(nc.semaphore("late_in"))
        attn1_phase(nc, dram, S)
        ffn1_phase(nc, dram, S)


def kernel(**inputs):
    import concourse.bacc as bacc
    from concourse.bass_utils import run_bass_kernel_spmd

    a = {k: np.ascontiguousarray(v) for k, v in inputs.items()}
    nc = bacc.Bacc("TRN2", target_bir_lowering=False, num_devices=1)
    arrays, dram = {}, Names()

    def give(name, x):
        x = np.ascontiguousarray(x)
        arrays["in_" + name] = x
        return nc.dram_tensor("in_" + name, x.shape, mybir.dt.from_np(x.dtype), kind="ExternalInput").ap()

    patches = a["x"].reshape(B, CHANNELS, GRID, PATCH, GRID, PATCH).transpose(1, 3, 5, 0, 2, 4).reshape(-1, 128, B * NP)
    dram.patches = give("patches", patches.transpose(1, 0, 2))
    dram.conv = give("conv", a["L0_tok_conv_w"].reshape(D, -1).T.reshape(-1, 128, D).transpose(1, 0, 2))
    dram.conv_b = give("conv_b", a["L0_tok_conv_b"][None])
    side = 32
    edges = np.arange(1.0 / side, 1.0, 1.0 / side, dtype=np.float32)
    frac = np.arange(0.0, 1.0 - 1e-06, 1.0 / GRID, dtype=np.float32)
    at = np.searchsorted(edges, frac, side="right")
    ids = (at[:, None] * side + at).reshape(-1)
    dram.pos = give("pos", np.concatenate([a["L0_tok_pos_table"][ids]] * 3))
    dram.txt = give("txt", a["txt"])

    def halves(*cols):
        rows = np.concatenate([np.concatenate([m, b[None]]) for m, b in cols], axis=1)
        return rows[0:LO], rows[LO:D + 1]

    z = np.zeros(D, np.float32)
    w0 = halves((a["L0_attn_Wq"], z), (a["L0_attn_Wk"], z), (a["L0_attn_Wv"], a["L0_attn_bv"]),
                (a["L0_attn_Wo"], a["L0_attn_bo"]), (a["L0_ffn_gate_w"].T, a["L0_ffn_gate_b"]))
    dram.w0a, dram.w0b = give("w0a", w0[0]), give("w0b", w0[1])
    c0 = np.stack([a["L0_attn_bq"], a["L0_attn_bk"], a["L0_ffn_scale"]], axis=1)
    dram.c0a, dram.c0b = give("c0a", c0[0:LO]), give("c0b", c0[LO:D])
    dram.mem = give("mem", a["L0_attn_memory"].T)
    def pair_tiles(x):
        x = x.reshape(E // 2, 2, *x.shape[1:])
        return np.concatenate([x[:, 0, ..., 0:LO], x[:, 1, ..., 0:LO], x[:, 0, ..., LO:D], x[:, 1, ..., LO:D]], axis=-1)

    w1 = np.concatenate([a["L0_ffn_w1"], a["L0_ffn_b1"][:, None, :]], axis=1)
    w1 = np.concatenate([pair_tiles(w1[..., 0:I]), pair_tiles(w1[..., I:2 * I])], axis=-1)
    dram.w1a, dram.w1b, dram.b1 = give("w1a", w1[:, 0:LO]), give("w1b", w1[:, LO:D]), give("b1", w1[:, D])
    w2 = pair_tiles(a["L0_ffn_w2"].transpose(0, 2, 1)).transpose(0, 2, 1).reshape(E // 2, 3, 128, D)
    dram.w2 = give("w2", w2.transpose(0, 2, 1, 3).reshape(E // 2, 128, 3 * D))
    dram.b2 = give("b2", a["L0_ffn_b2"])
    def heads(m, n, wd):
        m = m.reshape(m.shape[0], n, -1)
        return np.concatenate([m, np.zeros((*m.shape[0:2], wd - m.shape[2]), np.float32)], axis=2).reshape(m.shape[0], n * wd)

    qkv = a["L1_attn_w_qkv"].T
    rows = np.concatenate([heads(qkv[:, 0:D], 8, 32), heads(qkv[:, D:2 * D], 8, 32), qkv[:, 2 * D:],
                           a["L1_attn_w_proj"].T], axis=1)
    bias = np.concatenate([np.zeros(512 + D, np.float32), a["L1_attn_b_proj"]])[None]
    GDIM = D // 2
    dram.w1w = give("w1w", np.stack([np.concatenate([rows[0:GDIM], np.zeros_like(bias)]), np.concatenate([rows[GDIM:], bias])], axis=1))
    dram.w1g = give("w1g", np.stack([a["L1_attn_w_g0"].T, a["L1_attn_w_g1"].T], axis=1))
    f = {n[len("L1_ffn_"):]: v for n, v in a.items() if n.startswith("L1_ffn_")}
    none = lambda n: np.zeros(n, np.float32)
    down = f["lra_down"].reshape(D, D).T
    up = f["lra_up"].transpose(0, 2, 1).reshape(D, D)
    w4 = halves((f["r_in_w"].T, none(128)), (f["wq"].T, none(D)), (f["wk"].T, none(D)),
                (f["wv"].T, f["bv"]), (f["wo"].T, f["bo"]), (f["fc1_w"].T, none(768)), (down, none(D)), (up, none(D)))
    dram.w4a, dram.w4b = give("w4a", w4[0]), give("w4b", w4[1])
    per_feature = np.stack([f["r_ln_g"], f["r_ln_b"], f["ln1_g"], f["ln1_b"], f["ln2_g"], f["ln2_b"]], axis=1)
    mask = (np.arange(LO)[:, None] // (D // 12) == np.arange(6)).astype(np.float32)
    other = [f["r_in_b"][:, None], f["r_o1_b"][:, None], np.concatenate([f["r_o2_b"], none(64)])[:, None],
             *(np.concatenate([f[n].reshape(2, D // 2).T, np.zeros((LO - D // 2, 2), np.float32)]) for n in ("bq", "bk")),
             mask, f["fc1_b"].reshape(6, 128).T]
    dram.c4a = give("c4a", np.concatenate([per_feature[0:LO], *other], axis=1))
    dram.c4b = give("c4b", per_feature[LO:D])
    dram.ro1 = give("ro1", f["r_o1_w"].T.reshape(2, 128, 128).transpose(1, 0, 2))
    dram.ro2 = give("ro2", f["r_o2_w"].T)
    dram.ro3 = give("ro3", np.concatenate([f["r_o3_w"].T, f["r_o3_b"][None]]))
    dram.fc2 = give("fc2", f["fc2_w"].T.reshape(6, 128, D).transpose(1, 0, 2))
    dram.fc2b = give("fc2b", f["fc2_b"][None])
    dram.eb = nc.dram_tensor("eb_scratch", [E // 2, 2, 768], F32, kind="Internal").ap()
    dram.fw = nc.dram_tensor("fw_scratch", [E, B * N], F32, kind="Internal").ap()
    dram.out = nc.dram_tensor("out_0", [B, N, D], F32, kind="ExternalOutput").ap()
    program(nc, dram)
    r = run_bass_kernel_spmd(nc, [arrays], core_ids=[0])
    return r.results[0]["out_0"]
```
